# Optimizing a Trainium2 kernel written in Bass

```python
import numpy as np
import jax
import jax.numpy as jnp

def _softmax(x, axis=-1):
    return jax.nn.softmax(x, axis=axis)

def _gelu(x):
    return jax.nn.gelu(x, approximate=True)

def _silu(x):
    return jax.nn.silu(x)

def _sigmoid(x):
    return jax.nn.sigmoid(x)

def _layernorm(x, axis=-1, eps=1e-05):
    m = jnp.mean(x, axis=axis, keepdims=True)
    v = jnp.var(x, axis=axis, keepdims=True)
    return (x - m) / jnp.sqrt(v + eps)

def _scatter_add(tgt, idx, src, axis=0):
    return tgt.at[idx].add(src)

def _segment_sum(src, seg, n):
    return jax.ops.segment_sum(src, seg, n)
kernel_name = 'mk_perceiver_d1_seqx_r2_b3fb58'

def setup_inputs(seed: int=0):
    np.random.seed(seed)
    _w = jnp.asarray

    def _rec_inputs():
        import jax
        import jax.numpy as jnp
        _rk = jax.random.key(seed)
        x = -0.0003929 + 0.9999 * jax.random.normal(jax.random.fold_in(_rk, 1), (16, 64, 512), jnp.float32)
        _lenS = 64 - jax.random.randint(jax.random.fold_in(_rk, 7), (16,), 0, max(1, 64 // 4) + 1, jnp.int32)
        _lenS2 = 512 - jax.random.randint(jax.random.fold_in(_rk, 8), (16,), 0, max(1, 512 // 4) + 1, jnp.int32)
        _ctx_1024P = jax.random.normal(jax.random.fold_in(_rk, 11), (16, 16, 512), jnp.float32)
        _ctx_1024c = jax.random.dirichlet(jax.random.fold_in(_rk, 511), 0.3 * jnp.ones((16,), jnp.float32), (16, 512))
        _ctx_1024t = jnp.einsum('bsk,bkd->bsd', _ctx_1024c, _ctx_1024P)
        _ctx_1024t = _ctx_1024t * jax.lax.rsqrt(jnp.mean(jnp.square(_ctx_1024t)) + 1e-12) * 0.953939
        ctx_1024 = 2.81802e-05 + 1.00001 * (_ctx_1024t + 0.3 * jax.random.normal(jax.random.fold_in(_rk, 611), (16, 512, 512), jnp.float32))
        return (x, ctx_1024)
    x, ctx_1024 = _rec_inputs()

    def _L0_xattn_setup():
        import jax, jax.numpy as jnp
        import numpy as np
        E = 512
        NUM_HEADS = 16
        DK = E // NUM_HEADS
        EPS = 1e-05
        NEG_INF = -jnp.inf

        def layer_norm(x, g, b):
            mu = jnp.mean(x, axis=-1, keepdims=True)
            var = jnp.var(x, axis=-1, keepdims=True)
            return (x - mu) * jax.lax.rsqrt(var + EPS) * g + b

        def self_attn(x, Wq, Wk, Wv):
            Q, K, V = (x @ Wq, x @ Wk, x @ Wv)
            energy = jnp.einsum('bqd,bkd->bqk', Q, K)
            S = energy.shape[-1]
            lengths = jnp.sum(energy[:, 0] != 0, axis=-1)
            kidx = jnp.arange(S)
            pad = kidx[None, None, :] >= lengths[:, None, None]
            causal = kidx[None, :] < kidx[:, None]
            causal = (kidx[None, :] > kidx[:, None])[None]
            energy = jnp.where(pad | causal, NEG_INF, energy)
            score = jax.nn.softmax(energy / np.sqrt(DK), axis=-1)
            return jnp.einsum('bqk,bkd->bqd', score, V)

        def cross_attn(x, context, Wq, Wk, Wv):
            Q = x @ Wq
            K, V = (context @ Wk, context @ Wv)
            energy = jnp.einsum('bqd,bkd->bqk', Q, K)
            Sk = energy.shape[-1]
            lengths = jnp.sum(energy[:, 0] != 0, axis=-1)
            kidx = jnp.arange(Sk)
            pad = kidx[None, None, :] >= lengths[:, None, None]
            energy = jnp.where(pad, NEG_INF, energy)
            score = jax.nn.softmax(energy / np.sqrt(DK), axis=-1)
            return jnp.einsum('bqk,bkd->bqd', score, V)
        key = jax.random.key(seed)
        ks = jax.random.split(key, 12)
        B, S = (8, 1024)
        s = 1.0 / np.sqrt(E)
        inp = {'x': jax.random.normal(ks[0], (B, S, E), jnp.float32), 'context': jax.random.normal(ks[1], (B, S, E), jnp.float32), 'Wq1': jax.random.normal(ks[2], (E, E), jnp.float32) * s, 'Wk1': jax.random.normal(ks[3], (E, E), jnp.float32) * s, 'Wv1': jax.random.normal(ks[4], (E, E), jnp.float32) * s, 'Wq2': jax.random.normal(ks[5], (E, E), jnp.float32) * s, 'Wk2': jax.random.normal(ks[6], (E, E), jnp.float32) * s, 'Wv2': jax.random.normal(ks[7], (E, E), jnp.float32) * s, 'fc1_w': jax.random.normal(ks[8], (E, E), jnp.float32) * s, 'fc1_b': jnp.zeros((E,), jnp.float32), 'fc2_w': jax.random.normal(ks[9], (E, E), jnp.float32) * s, 'fc2_b': jnp.zeros((E,), jnp.float32), 'ln1_g': jnp.ones((E,), jnp.float32), 'ln1_b': jnp.zeros((E,), jnp.float32), 'ln2_g': jnp.ones((E,), jnp.float32), 'ln2_b': jnp.zeros((E,), jnp.float32), 'ln3_g': jnp.ones((E,), jnp.float32), 'ln3_b': jnp.zeros((E,), jnp.float32)}
        return inp
    _L0_xattn_all = _L0_xattn_setup()
    _L0_xattn_in = {k: v for k, v in _L0_xattn_all.items() if k in ('Wq1', 'Wk1', 'Wv1', 'Wq2', 'Wk2', 'Wv2', 'fc1_w', 'fc1_b', 'fc2_w', 'fc2_b', 'ln1_g', 'ln1_b', 'ln2_g', 'ln2_b', 'ln3_g', 'ln3_b')}
    del _L0_xattn_all

    def _L0_attn_setup():
        import jax, jax.numpy as jnp
        import numpy as np
        BATCH, SEQ, D_MODEL = (2, 2048, 512)
        EXPAND, N_HEADS, D_STATE, D_CONV, CHUNK = (2, 16, 16, 4, 64)
        D_INNER = EXPAND * D_MODEL
        HEAD_DIM = D_INNER // N_HEADS
        LN_EPS = 1e-05

        def silu(v):
            return v * jax.nn.sigmoid(v)

        def _forward(x, W_in, conv_w, conv_b, W_xproj, W_dt, b_dt, A_log, D_skip, W_out, ln_g, ln_b):
            b, L, _ = x.shape
            xz = x @ W_in
            xe, z = jnp.split(xz, 2, axis=-1)
            xp = jnp.pad(xe, ((0, 0), (D_CONV - 1, 0), (0, 0)))
            xc = conv_b
            for j in range(D_CONV):
                xc = xc + conv_w[:, j] * xp[:, j:j + L, :]
            xc = silu(xc)
            proj = xc @ W_xproj
            dt_raw = proj[..., :N_HEADS]
            Bm = proj[..., N_HEADS:N_HEADS + D_STATE]
            Cm = proj[..., N_HEADS + D_STATE:]
            dt = jax.nn.softplus(dt_raw @ W_dt + b_dt)
            A = -jnp.exp(A_log)
            xh = xc.reshape(b, L, N_HEADS, HEAD_DIM)
            dth = dt.reshape(b, L, N_HEADS, HEAD_DIM)
            nc = L // CHUNK
            dt_cum = dth.reshape(b, nc, CHUNK, N_HEADS, HEAD_DIM).cumsum(axis=2)
            decay = jnp.exp(A[None, None, None, :, None] * dt_cum).reshape(b, L, N_HEADS, HEAD_DIM)
            xs = (jnp.moveaxis(xh, 1, 0), jnp.moveaxis(dth, 1, 0), jnp.moveaxis(decay, 1, 0), jnp.moveaxis(Bm, 1, 0), jnp.moveaxis(Cm, 1, 0))
            state0 = jnp.zeros((b, N_HEADS, HEAD_DIM, D_STATE), x.dtype)

            def step(state, inp):
                x_t, dt_t, dec_t, B_t, C_t = inp
                state = state * dec_t[..., None] + (dt_t * x_t)[..., None] * B_t[:, None, None, :]
                y_t = jnp.einsum('bhdn,bn->bhd', state, C_t)
                return (state, y_t)
            _, ys = jax.lax.scan(step, state0, xs)
            y = jnp.moveaxis(ys, 0, 1)
            y = y + xh * D_skip[None, None, :, None]
            y = y.reshape(b, L, D_INNER) * silu(z)
            mu = y.mean(-1, keepdims=True)
            var = ((y - mu) ** 2).mean(-1, keepdims=True)
            y = (y - mu) * jax.lax.rsqrt(var + LN_EPS) * ln_g + ln_b
            return y @ W_out
        key = jax.random.key(seed)
        ks = jax.random.split(key, 10)

        def w(k, shape, fan):
            return jax.random.normal(k, shape, jnp.float32) / np.float32(np.sqrt(fan))
        x = jax.random.normal(ks[0], (BATCH, SEQ, D_MODEL), jnp.float32)
        W_in = w(ks[1], (D_MODEL, 2 * D_INNER), D_MODEL)
        conv_w = w(ks[2], (D_INNER, D_CONV), D_CONV)
        conv_b = 0.01 * jax.random.normal(ks[3], (D_INNER,), jnp.float32)
        W_xproj = w(ks[4], (D_INNER, N_HEADS + 2 * D_STATE), D_INNER)
        W_dt = w(ks[5], (N_HEADS, D_INNER), N_HEADS)
        u = jax.random.uniform(ks[6], (N_HEADS,), jnp.float32)
        dt_init = jnp.exp(u * (np.log(0.1) - np.log(0.001)) + np.log(0.001))
        b_dt = jnp.repeat(jnp.log(jnp.expm1(dt_init)), HEAD_DIM)
        A_log = jnp.log(jnp.linspace(1.0, 16.0, N_HEADS)).astype(jnp.float32)
        D_skip = jnp.ones((N_HEADS,), jnp.float32)
        W_out = w(ks[7], (D_INNER, D_MODEL), D_INNER)
        ln_g = jnp.ones((D_INNER,), jnp.float32)
        ln_b = jnp.zeros((D_INNER,), jnp.float32)
        return {'x': x, 'W_in': W_in, 'conv_w': conv_w, 'conv_b': conv_b, 'W_xproj': W_xproj, 'W_dt': W_dt, 'b_dt': b_dt, 'A_log': A_log, 'D_skip': D_skip, 'W_out': W_out, 'ln_g': ln_g, 'ln_b': ln_b}
    _L0_attn_all = _L0_attn_setup()
    _L0_attn_in = {k: v for k, v in _L0_attn_all.items() if k in ('W_in', 'conv_w', 'conv_b', 'W_xproj', 'W_dt', 'b_dt', 'A_log', 'D_skip', 'W_out', 'ln_g', 'ln_b')}
    del _L0_attn_all

    def _L0_ffn_setup():
        import math
        import jax, jax.numpy as jnp
        import numpy as np
        B, T, D, H, E, K, S = (4, 2048, 512, 1024, 16, 2, 2)
        ROUTE_SCALE = 1.0

        def _swiglu(x, w1, w3, w2):
            return jax.nn.silu(x @ w1) * (x @ w3) @ w2
        key = jax.random.key(seed)
        ks = jax.random.split(key, 9)
        s = 0.02
        return {'x': jax.random.normal(ks[0], (B, T, D), jnp.float32), 'gate_w': jax.random.normal(ks[1], (D, E), jnp.float32) * s, 'gate_b': jnp.zeros((E,), jnp.float32), 'ew1': jax.random.normal(ks[2], (E, D, H), jnp.float32) * s, 'ew3': jax.random.normal(ks[3], (E, D, H), jnp.float32) * s, 'ew2': jax.random.normal(ks[4], (E, H, D), jnp.float32) * s, 'sw1': jax.random.normal(ks[5], (S, D, H), jnp.float32) * s, 'sw3': jax.random.normal(ks[6], (S, D, H), jnp.float32) * s, 'sw2': jax.random.normal(ks[7], (S, H, D), jnp.float32) * s}
    _L0_ffn_all = _L0_ffn_setup()
    _L0_ffn_in = {k: v for k, v in _L0_ffn_all.items() if k in ('gate_w', 'gate_b', 'ew1', 'ew3', 'ew2', 'sw1', 'sw3', 'sw2')}
    del _L0_ffn_all
    return {'x': x, 'ctx_1024': ctx_1024, 'L0_xattn_Wq1': _L0_xattn_in['Wq1'], 'L0_xattn_Wk1': _L0_xattn_in['Wk1'], 'L0_xattn_Wv1': _L0_xattn_in['Wv1'], 'L0_xattn_Wq2': _L0_xattn_in['Wq2'], 'L0_xattn_Wk2': _L0_xattn_in['Wk2'], 'L0_xattn_Wv2': _L0_xattn_in['Wv2'], 'L0_xattn_fc1_w': _L0_xattn_in['fc1_w'], 'L0_xattn_fc1_b': _L0_xattn_in['fc1_b'], 'L0_xattn_fc2_w': _L0_xattn_in['fc2_w'], 'L0_xattn_fc2_b': _L0_xattn_in['fc2_b'], 'L0_xattn_ln1_g': _L0_xattn_in['ln1_g'], 'L0_xattn_ln1_b': _L0_xattn_in['ln1_b'], 'L0_xattn_ln2_g': _L0_xattn_in['ln2_g'], 'L0_xattn_ln2_b': _L0_xattn_in['ln2_b'], 'L0_xattn_ln3_g': _L0_xattn_in['ln3_g'], 'L0_xattn_ln3_b': _L0_xattn_in['ln3_b'], 'L0_attn_W_in': _L0_attn_in['W_in'], 'L0_attn_conv_w': _L0_attn_in['conv_w'], 'L0_attn_conv_b': _L0_attn_in['conv_b'], 'L0_attn_W_xproj': _L0_attn_in['W_xproj'], 'L0_attn_W_dt': _L0_attn_in['W_dt'], 'L0_attn_b_dt': _L0_attn_in['b_dt'], 'L0_attn_A_log': _L0_attn_in['A_log'], 'L0_attn_D_skip': _L0_attn_in['D_skip'], 'L0_attn_W_out': _L0_attn_in['W_out'], 'L0_attn_ln_g': _L0_attn_in['ln_g'], 'L0_attn_ln_b': _L0_attn_in['ln_b'], 'L0_ffn_gate_w': _L0_ffn_in['gate_w'], 'L0_ffn_gate_b': _L0_ffn_in['gate_b'], 'L0_ffn_ew1': _L0_ffn_in['ew1'], 'L0_ffn_ew3': _L0_ffn_in['ew3'], 'L0_ffn_ew2': _L0_ffn_in['ew2'], 'L0_ffn_sw1': _L0_ffn_in['sw1'], 'L0_ffn_sw3': _L0_ffn_in['sw3'], 'L0_ffn_sw2': _L0_ffn_in['sw2']}

def reference(x, ctx_1024, L0_xattn_Wq1, L0_xattn_Wk1, L0_xattn_Wv1, L0_xattn_Wq2, L0_xattn_Wk2, L0_xattn_Wv2, L0_xattn_fc1_w, L0_xattn_fc1_b, L0_xattn_fc2_w, L0_xattn_fc2_b, L0_xattn_ln1_g, L0_xattn_ln1_b, L0_xattn_ln2_g, L0_xattn_ln2_b, L0_xattn_ln3_g, L0_xattn_ln3_b, L0_attn_W_in, L0_attn_conv_w, L0_attn_conv_b, L0_attn_W_xproj, L0_attn_W_dt, L0_attn_b_dt, L0_attn_A_log, L0_attn_D_skip, L0_attn_W_out, L0_attn_ln_g, L0_attn_ln_b, L0_ffn_gate_w, L0_ffn_gate_b, L0_ffn_ew1, L0_ffn_ew3, L0_ffn_ew2, L0_ffn_sw1, L0_ffn_sw3, L0_ffn_sw2):
    import jax
    import jax.numpy as jnp

    def _L0_xattn_ref(x, context, Wq1, Wk1, Wv1, Wq2, Wk2, Wv2, fc1_w, fc1_b, fc2_w, fc2_b, ln1_g, ln1_b, ln2_g, ln2_b, ln3_g, ln3_b):
        import jax, jax.numpy as jnp
        import numpy as np
        E = 512
        NUM_HEADS = 16
        DK = E // NUM_HEADS
        EPS = 1e-05
        NEG_INF = -jnp.inf

        def layer_norm(x, g, b):
            mu = jnp.mean(x, axis=-1, keepdims=True)
            var = jnp.var(x, axis=-1, keepdims=True)
            return (x - mu) * jax.lax.rsqrt(var + EPS) * g + b

        def self_attn(x, Wq, Wk, Wv):
            Q, K, V = (x @ Wq, x @ Wk, x @ Wv)
            energy = jnp.einsum('bqd,bkd->bqk', Q, K)
            S = energy.shape[-1]
            lengths = jnp.sum(energy[:, 0] != 0, axis=-1)
            kidx = jnp.arange(S)
            pad = kidx[None, None, :] >= lengths[:, None, None]
            causal = kidx[None, :] < kidx[:, None]
            causal = (kidx[None, :] > kidx[:, None])[None]
            energy = jnp.where(pad | causal, NEG_INF, energy)
            score = jax.nn.softmax(energy / np.sqrt(DK), axis=-1)
            return jnp.einsum('bqk,bkd->bqd', score, V)

        def cross_attn(x, context, Wq, Wk, Wv):
            Q = x @ Wq
            K, V = (context @ Wk, context @ Wv)
            energy = jnp.einsum('bqd,bkd->bqk', Q, K)
            Sk = energy.shape[-1]
            lengths = jnp.sum(energy[:, 0] != 0, axis=-1)
            kidx = jnp.arange(Sk)
            pad = kidx[None, None, :] >= lengths[:, None, None]
            energy = jnp.where(pad, NEG_INF, energy)
            score = jax.nn.softmax(energy / np.sqrt(DK), axis=-1)
            return jnp.einsum('bqk,bkd->bqd', score, V)
        z = self_attn(x, Wq1, Wk1, Wv1)
        x = layer_norm(x + z, ln1_g, ln1_b)
        z = cross_attn(x, context, Wq2, Wk2, Wv2)
        x = layer_norm(x + z, ln2_g, ln2_b)
        z = jax.nn.relu(x @ fc1_w + fc1_b)
        z = z @ fc2_w + fc2_b
        return layer_norm(x + z, ln3_g, ln3_b)

    def _L0_attn_ref(x, W_in, conv_w, conv_b, W_xproj, W_dt, b_dt, A_log, D_skip, W_out, ln_g, ln_b):
        import jax, jax.numpy as jnp
        import numpy as np
        BATCH, SEQ, D_MODEL = (2, 2048, 512)
        EXPAND, N_HEADS, D_STATE, D_CONV, CHUNK = (2, 16, 16, 4, 64)
        D_INNER = EXPAND * D_MODEL
        HEAD_DIM = D_INNER // N_HEADS
        LN_EPS = 1e-05

        def silu(v):
            return v * jax.nn.sigmoid(v)

        def _forward(x, W_in, conv_w, conv_b, W_xproj, W_dt, b_dt, A_log, D_skip, W_out, ln_g, ln_b):
            b, L, _ = x.shape
            xz = x @ W_in
            xe, z = jnp.split(xz, 2, axis=-1)
            xp = jnp.pad(xe, ((0, 0), (D_CONV - 1, 0), (0, 0)))
            xc = conv_b
            for j in range(D_CONV):
                xc = xc + conv_w[:, j] * xp[:, j:j + L, :]
            xc = silu(xc)
            proj = xc @ W_xproj
            dt_raw = proj[..., :N_HEADS]
            Bm = proj[..., N_HEADS:N_HEADS + D_STATE]
            Cm = proj[..., N_HEADS + D_STATE:]
            dt = jax.nn.softplus(dt_raw @ W_dt + b_dt)
            A = -jnp.exp(A_log)
            xh = xc.reshape(b, L, N_HEADS, HEAD_DIM)
            dth = dt.reshape(b, L, N_HEADS, HEAD_DIM)
            nc = L // CHUNK
            dt_cum = dth.reshape(b, nc, CHUNK, N_HEADS, HEAD_DIM).cumsum(axis=2)
            decay = jnp.exp(A[None, None, None, :, None] * dt_cum).reshape(b, L, N_HEADS, HEAD_DIM)
            xs = (jnp.moveaxis(xh, 1, 0), jnp.moveaxis(dth, 1, 0), jnp.moveaxis(decay, 1, 0), jnp.moveaxis(Bm, 1, 0), jnp.moveaxis(Cm, 1, 0))
            state0 = jnp.zeros((b, N_HEADS, HEAD_DIM, D_STATE), x.dtype)

            def step(state, inp):
                x_t, dt_t, dec_t, B_t, C_t = inp
                state = state * dec_t[..., None] + (dt_t * x_t)[..., None] * B_t[:, None, None, :]
                y_t = jnp.einsum('bhdn,bn->bhd', state, C_t)
                return (state, y_t)
            _, ys = jax.lax.scan(step, state0, xs)
            y = jnp.moveaxis(ys, 0, 1)
            y = y + xh * D_skip[None, None, :, None]
            y = y.reshape(b, L, D_INNER) * silu(z)
            mu = y.mean(-1, keepdims=True)
            var = ((y - mu) ** 2).mean(-1, keepdims=True)
            y = (y - mu) * jax.lax.rsqrt(var + LN_EPS) * ln_g + ln_b
            return y @ W_out
        return _forward(x, W_in, conv_w, conv_b, W_xproj, W_dt, b_dt, A_log, D_skip, W_out, ln_g, ln_b)

    def _L0_ffn_ref(x, gate_w, gate_b, ew1, ew3, ew2, sw1, sw3, sw2):
        import math
        import jax, jax.numpy as jnp
        import numpy as np
        B, T, D, H, E, K, S = (4, 2048, 512, 1024, 16, 2, 2)
        ROUTE_SCALE = 1.0

        def _swiglu(x, w1, w3, w2):
            return jax.nn.silu(x @ w1) * (x @ w3) @ w2
        Bx, Tx, Dx = x.shape
        flat = x.reshape(-1, Dx)
        N = flat.shape[0]
        n_experts = gate_w.shape[1]
        logits = flat @ gate_w
        scores = jax.nn.softmax(logits.astype(jnp.float32), -1) + gate_b
        _, topi = jax.lax.top_k(scores, K)
        weights = jnp.take_along_axis(logits, topi, axis=-1) * ROUTE_SCALE
        weights = weights.astype(flat.dtype)
        capacity = math.ceil(N * K / n_experts * 1.25)

        def per_expert(gid, w1, w3, w2):
            match = topi == gid
            assigned = match.any(-1)
            w_tok = jnp.sum(jnp.where(match, weights, 0.0), -1)
            wm = jnp.where(assigned, w_tok, -jnp.inf)
            vals, idx = jax.lax.top_k(wm, capacity)
            valid = assigned[idx]
            xs = flat[idx]
            y = _swiglu(xs, w1, w3, w2) * jnp.where(valid, vals, 0.0)[:, None]
            return (idx, y)
        idxs, ys = jax.vmap(per_expert)(jnp.arange(n_experts), ew1, ew3, ew2)
        out = jnp.zeros_like(flat).at[idxs.reshape(-1)].add(ys.reshape(-1, Dx))
        shared = jax.vmap(lambda w1, w3, w2: _swiglu(flat, w1, w3, w2))(sw1, sw3, sw2)
        out = out + shared.mean(0)
        return out.reshape(Bx, Tx, Dx)
    x = x + _L0_xattn_ref(_layernorm(x, axis=-1), ctx_1024, L0_xattn_Wq1, L0_xattn_Wk1, L0_xattn_Wv1, L0_xattn_Wq2, L0_xattn_Wk2, L0_xattn_Wv2, L0_xattn_fc1_w, L0_xattn_fc1_b, L0_xattn_fc2_w, L0_xattn_fc2_b, L0_xattn_ln1_g, L0_xattn_ln1_b, L0_xattn_ln2_g, L0_xattn_ln2_b, L0_xattn_ln3_g, L0_xattn_ln3_b)
    x = x + _L0_attn_ref(_layernorm(x, axis=-1), L0_attn_W_in, L0_attn_conv_w, L0_attn_conv_b, L0_attn_W_xproj, L0_attn_W_dt, L0_attn_b_dt, L0_attn_A_log, L0_attn_D_skip, L0_attn_W_out, L0_attn_ln_g, L0_attn_ln_b)
    x = x + _L0_ffn_ref(_layernorm(x, axis=-1), L0_ffn_gate_w, L0_ffn_gate_b, L0_ffn_ew1, L0_ffn_ew3, L0_ffn_ew2, L0_ffn_sw1, L0_ffn_sw3, L0_ffn_sw2)
    return x

_drawn_inputs = setup_inputs


def setup_inputs(seed=0):
    import zlib

    import numpy as np

    out = dict(_drawn_inputs(seed))
    spreads = {'L0_xattn_fc1_b': (0.0, 0.1),
     'L0_xattn_fc2_b': (0.0, 0.1),
     'L0_xattn_ln1_g': (1.0, 0.2),
     'L0_xattn_ln1_b': (0.0, 0.1),
     'L0_xattn_ln2_g': (1.0, 0.2),
     'L0_xattn_ln2_b': (0.0, 0.1),
     'L0_xattn_ln3_g': (1.0, 0.2),
     'L0_xattn_ln3_b': (0.0, 0.1),
     'L0_attn_D_skip': (1.0, 0.2),
     'L0_attn_ln_g': (1.0, 0.2),
     'L0_attn_ln_b': (0.0, 0.1),
     'L0_ffn_gate_b': (0.0, 0.1)}
    factors = {'L0_attn_conv_b': 8.0,
     'L0_attn_A_log': 8.0,
     'L0_ffn_gate_w': 3.13,
     'L0_ffn_ew1': 3.122,
     'L0_ffn_ew3': 3.059,
     'L0_ffn_ew2': 3.056,
     'L0_ffn_sw1': 8.0,
     'L0_ffn_sw3': 7.878,
     'L0_ffn_sw2': 7.889}
    for name, (base, spread) in spreads.items():
        noise = np.random.default_rng([zlib.crc32(name.encode()), seed]).standard_normal(out[name].shape)
        drawn = base * np.exp(spread * noise) if base else spread * noise
        out[name] = jnp.asarray(drawn.astype(out[name].dtype))
    for name, factor in factors.items():
        out[name] = (out[name] * factor).astype(out[name].dtype)
    return out
```

```python
from contextlib import ExitStack

import concourse.bass as bass
from concourse import mybir

F32 = mybir.dt.float32
U32 = mybir.dt.uint32
ALU = mybir.AluOpType
ACT = mybir.ActivationFunctionType
AX = mybir.AxisListType

P = 128
D = 512
KD = D // P
NB = 16
L = 64
N = NB * L
NT = N // P
TG = 256
G = N // TG
SK = 512
KS = SK // P
C = 1024
MC = C // P
NS = 16
Q = 8
E = 16
H = 1024
MH = H // P
CAP = 160
SCALE = float(1.0 / (32.0 ** 0.5))
EPS = 1e-5
BIG = -1.0e30
NOT_MINE = -3.0e38


def constants(nc, sb, sem, d):
    c = {}
    c["ident"] = sb("ident", [P, P])
    c["ones"] = sb("ones", [P, P])
    c["ones_over_c"] = sb("ones_over_c", [P, P])
    c["causal"] = sb("causal", [P, P])
    c["same_batch"] = sb("same_batch", [P, P])
    c["first_row"] = sb("first_row", [P, P])
    c["key_in_batch"] = sb("key_in_batch", [P, P])
    c["key_index"] = sb("key_index", [P, SK])
    c["expert_index"] = sb("expert_index", [P, E])
    c["own_chunk"] = sb("own_chunk", [P, 16, NS])
    c["next_chunk"] = sb("next_chunk", [P, Q, Q])
    c["in_sequence"] = sb("in_sequence", [P, TG])
    c["rep_state"] = sb("rep_state", [NS, Q, NS])
    c["lower"] = sb("lower", [P, P])
    c["upper"] = sb("upper", [P, P])
    c["minus_half"] = sb("minus_half", [P, 2])
    c["eps"] = sb("eps", [P, 2])
    return c


def build_constants(nc, c, s_const):
    pool = nc.gpsimd
    n = [0]

    def put(ins, wait=False):
        ins.then_inc(s_const, 1)
        n[0] += 1
        if wait:
            pool.wait_ge(s_const, n[0])

    def select(t, out, pattern, base, mult, op, fill):
        put(pool.affine_select(out=out, in_=out, compare_op=op, fill=fill, base=base,
                               pattern=pattern, channel_multiplier=mult), wait=True)

    for name in ("ones", "same_batch", "causal", "first_row", "own_chunk", "next_chunk", "rep_state",
                 "in_sequence", "lower", "upper"):
        put(pool.memset(c[name][:], 1.0))
    put(pool.memset(c["ident"][:], 0.0))
    put(pool.memset(c["ones_over_c"][:], 1.0 / C))
    put(pool.memset(c["minus_half"][:], -0.5))
    put(pool.memset(c["eps"][:], EPS))
    for name, pat in (("key_in_batch", [[0, 2], [1, L]]), ("key_index", [[1, SK]]), ("expert_index", [[1, E]])):
        put(pool.iota(c[name][:], pattern=pat, base=0, channel_multiplier=0,
                      allow_small_or_imprecise_dtypes=True))
    pool.wait_ge(s_const, n[0])
    select(c, c["ident"][:], [[-1, P]], 0, 1, ALU.not_equal, 1.0)
    sbm = c["same_batch"][:].rearrange("p (b j) -> p b j", b=2)
    select(c, sbm, [[-L, 2], [0, L]], 0, 1, ALU.is_ge, 0.0)
    select(c, sbm, [[L, 2], [0, L]], L - 1, -1, ALU.is_ge, 0.0)
    cm = c["causal"][:]
    select(c, cm, [[1, P]], 0, -1, ALU.is_gt, 0.0)
    put(pool.memset(c["causal"][L:P, 0:L], 1.0), wait=True)
    fr = c["first_row"][:].rearrange("p (b j) -> p b j", b=2)
    select(c, fr, [[-L, 2], [0, L]], 0, 1, ALU.is_equal, 0.0)
    oc = c["own_chunk"][:]
    select(c, oc, [[-Q, 16], [0, NS]], 0, 1, ALU.is_ge, 0.0)
    select(c, oc, [[Q, 16], [0, NS]], Q - 1, -1, ALU.is_ge, 0.0)
    nx = c["next_chunk"][:]
    select(c, nx, [[-NS, Q], [0, Q]], NS, 1, ALU.is_ge, 0.0)
    select(c, nx, [[NS, Q], [0, Q]], -1, -1, ALU.is_ge, 0.0)
    select(c, c["rep_state"][:], [[0, Q], [-1, NS]], 0, 1, ALU.is_equal, 0.0)
    isq = c["in_sequence"][:].rearrange("p (a t) -> p a t", t=L)
    put(pool.memset(isq[:, :, 0:1], 0.0))
    select(c, c["lower"][:], [[-1, P]], 0, 1, ALU.is_gt, 0.0)
    select(c, c["upper"][:], [[1, P]], 0, -1, ALU.is_gt, 0.0)
    pool.wait_ge(s_const, n[0])
    put(pool.memset(c["lower"][0:1, 0:1], 0.0))
    return n[0]


def attention_block(nc, d, c, s_const, n_const, xres, sem, s_x):
    with ExitStack() as ctx:
        def sb(name, shape, dt=F32):
            return ctx.enter_context(nc.sbuf_tensor("A_" + name, shape, dt))

        ps = ctx.enter_context(nc.psum_tensor("psA", [P, 8, 512], F32))
        wqT = sb("wqT", [P, KD, D])
        wkT = sb("wkT", [P, KD, D])
        wqk = [sb(f"wqk{a}", [P, KD, D]) for a in range(2)]
        wv1 = sb("wv1", [P, KD, D])
        wv2 = sb("wv2", [P, KD, D])
        fc1 = sb("fc1", [P, KD, D])
        fc2 = sb("fc2", [P, KD, D])
        fc1_b = sb("fc1_b", [P, KD])
        fc2_b = sb("fc2_b", [1, D])
        ln = sb("ln_gb", [P, 6, D])
        ctx_kd = sb("ctx_kd", [P, 2, KS, D])
        ctx_dk = sb("ctx_dk", [P, 2, KD, SK])
        xn = sb("xn", [P, 2, D])
        tT = sb("tT", [P, KD, TG])
        qT = sb("qT", [P, KD, TG])
        v1 = sb("v1", [P, 2, D])
        pr1 = sb("pr1", [P, 2, P])
        pr1T = sb("pr1T", [P, 2, P])
        msk1 = sb("msk1", [P, 2, P])
        x1 = sb("x1", [P, 2, D])
        pr2 = sb("pr2", [P, 2, SK])
        pr2T = sb("pr2T", [P, 2, KS, P])
        msk2 = sb("msk2", [P, 2, SK])
        cT = sb("cT", [P, 2, KD, P])
        x2 = sb("x2", [P, 2, D])
        hT = sb("hT", [P, KD, TG])
        bst = sb("bst", [P, 2, 6])
        mv = sb("mvA", [P, 2, 2])
        ve = sb("veA", [P, 2])
        rstd = sb("rstdA", [P, 2])
        cnt = sb("cnt", [P, 4])
        nmx = sb("nmx", [P, 4])
        rsum = sb("rsum", [P, 4])
        rinv = sb("rinv", [P, 4])

        s_w = {k: sem("A_" + k) for k in ("w0", "w1", "rest", "ln", "ctx0")}
        s_ctx = sem("A_ctx_in")
        s_wqk_mm = sem("A_wqk_mm")
        s_wqk = sem("A_wqk")
        s_xn = sem("A_xn")
        s_tr = sem("A_transposed")
        s_tT = sem("A_tT")
        s_q_mm = sem("A_q_mm")
        s_q = sem("A_q")
        s_v_mm = sem("A_v_mm")
        s_v = sem("A_v")
        s_e1 = sem("A_e1")
        s_cnt = sem("A_cnt")
        s_len = sem("A_len")
        s_bias = sem("A_bias")
        s_exp = sem("A_exp")
        s_pT = sem("A_pT")
        s_pTs = sem("A_pTs")
        s_z = sem("A_z")
        s_var = sem("A_var")
        s_ve = sem("A_ve")
        s_rstd = sem("A_rstd")
        s_x1 = sem("A_x1")
        s_e2 = sem("A_e2")
        s_c_mm = sem("A_c_mm")
        s_c = sem("A_c")
        s_x2 = sem("A_x2")
        s_f1_mm = sem("A_f1_mm")
        s_h = sem("A_h")
        s_dve = sem("A_dve")
        s_done = sem("A_done")

        def stand_alone(eng):
            eng.sem_inc(s_passed, 1)

        s_passed = sem("A_waits_passed")

        block = ctx.enter_context(nc.Block())

        def w_view(w):
            return w.rearrange("(k p) n -> p k n", p=P)

        @block.sync
        def _(sp):
            sp.dma_start(xres[:], d["x"].rearrange("(t p) n -> p t n", p=P)).then_inc(s_x, 16)
            sp.dma_start(wqT[:], w_view(d["wq1T"])).then_inc(s_w["w0"], 16)
            sp.dma_start(wkT[:], w_view(d["wk1T"])).then_inc(s_w["w0"], 16)
            sp.dma_start(wv1[:], w_view(d["wv1"])).then_inc(s_w["rest"], 16)
            for n in range(6):
                sp.dma_start(ln[:, n, :], d["ln"][n].partition_broadcast(P)).then_inc(s_w["ln"], 16)
            sp.dma_start(wv2[:], w_view(d["wv2"])).then_inc(s_w["rest"], 16)
            sp.dma_start(fc1[:], w_view(d["fc1_w"])).then_inc(s_w["rest"], 16)
            sp.dma_start(fc2[:], w_view(d["fc2_w"])).then_inc(s_w["rest"], 16)
            sp.dma_start(fc1_b[:], d["fc1_b"]).then_inc(s_w["rest"], 16)
            sp.dma_start(fc2_b[:], d["fc2_b"]).then_inc(s_w["rest"], 16)
            sp.wait_ge(s_wqk_mm, 4)
            sp.dma_start(wqT[:], w_view(d["wq2T"])).then_inc(s_w["w1"], 16)
            sp.dma_start(wkT[:], w_view(d["wk2T"])).then_inc(s_w["w1"], 16)

            def load_ctx(pair):
                for h in range(2):
                    sp.dma_start(ctx_dk[:, h], d["ctxT"][pair, h]).then_inc(s_ctx, 16)
                for h in range(2):
                    sp.dma_start(ctx_kd[:, h], d["ctx"][pair, h]).then_inc(s_ctx, 16)

            load_ctx(0)
            with nc.sync.Fori(0, 2 * G - 1) as pair:
                sp.wait_ge(s_c_mm, pair + 1)
                load_ctx(pair + 1)

        @block.gpsimd
        def _(pool):
            with nc.gpsimd.Fori(0, G) as g:
                for n in range(4):
                    pool.wait_ge(s_var, 8 * g + 2 * n + 2)
                    nc.gpsimd.tensor_tensor(ve[:], mv[:, :, 1], c["eps"][:], ALU.add).then_inc(s_ve, 1)
                    pool.wait_ge(s_ve, 4 * g + n + 1)
                    nc.gpsimd.tensor_tensor(rstd[:], ve[:], c["minus_half"][:, 0:2], ALU.pow).then_inc(s_rstd, 1)

        @block.tensor
        def _(pe):
            pe.wait_ge(s_const, n_const)
            for a in range(2):
                pe.wait_ge(s_w[f"w{a}"], 32)
                for m in range(KD):
                    if a:
                        pe.wait_ge(s_wqk, m + 1)
                    for k in range(KD):
                        mm = nc.tensor.matmul(ps[:, m, :], wqT[:, k, m * P:(m + 1) * P], wkT[:, k, :],
                                              start=(k == 0), stop=(k == KD - 1))
                    mm.then_inc(s_wqk_mm, 1)
            pe.wait_ge(s_w["rest"], 16 * 6)
            pe.wait_ge(s_wqk, 8)
            bT = ps[:, 0:2, :].rearrange("p b (k t) -> p (b k) t", k=2)

            def transposes(src):
                for i in range(2):
                    for k in range(KD):
                        mm = nc.tensor.transpose(bT[:, k, i * P:(i + 1) * P], src[:, i, k * P:(k + 1) * P],
                                                 c["ident"][:])
                mm.then_inc(s_tr, 1)

            def widths_out(w, src, s):
                for m in range(KD):
                    for k in range(KD):
                        mm = nc.tensor.matmul(bT[:, m, :], w[:, k, m * P:(m + 1) * P], src[:, k, :],
                                              start=(k == 0), stop=(k == KD - 1))
                mm.then_inc(s, 1)

            with nc.tensor.Fori(0, G) as g:
                pe.wait_ge(s_xn, 2 * g + 2)
                transposes(xn)
                pe.wait_ge(s_tT, 6 * g + 2)
                widths_out(wqk[0], tT, s_q_mm)
                for i in range(2):
                    for k in range(KD):
                        mm = nc.tensor.matmul(ps[:, 2 + i, :], tT[:, k, i * P:(i + 1) * P], wv1[:, k, :],
                                              start=(k == 0), stop=(k == KD - 1))
                    mm.then_inc(s_v_mm, 1)
                pe.wait_ge(s_q, 4 * g + 2)
                for i in range(2):
                    for k in range(KD):
                        mm = nc.tensor.matmul(ps[:, 4 + i, 0:P], qT[:, k, i * P:(i + 1) * P],
                                              tT[:, k, i * P:(i + 1) * P], start=(k == 0), stop=(k == KD - 1))
                    mm.then_inc(s_e1, 1)
                pe.wait_ge(s_cnt, 4 * g + 2)
                nc.tensor.matmul(ps[:, 6, 0:2], c["first_row"][:], cnt[:, 0:2], start=True,
                                 stop=True).then_inc(s_len, 1)
                for i in range(2):
                    pe.wait_ge(s_exp, 4 * g + i + 1)
                    nc.tensor.transpose(ps[:, 7, i * P:(i + 1) * P], pr1[:, i, :], c["ident"][:]).then_inc(s_pT, 1)
                for i in range(2):
                    pe.wait_ge(s_pTs, 4 * g + i + 1)
                    pe.wait_ge(s_v, 2 * g + i + 1)
                    nc.tensor.matmul(ps[:, 2 + i, :], pr1T[:, i, :], v1[:, i, :], start=True,
                                     stop=True).then_inc(s_z, 1)
                pe.wait_ge(s_x1, 2 * g + 2)
                transposes(x1)
                pe.wait_ge(s_tT, 6 * g + 4)
                widths_out(wqk[1], tT, s_q_mm)
                pe.wait_ge(s_q, 4 * g + 4)

                for i in range(2):
                    pe.wait_ge(s_ctx, 64 * (2 * g + i + 1))
                    for h in range(2):
                        for k in range(KD):
                            mm = nc.tensor.matmul(ps[h * L:(h + 1) * L, 4 + i, :],
                                                  qT[:, k, i * P + h * L:i * P + (h + 1) * L],
                                                  ctx_dk[:, h, k, :], start=(k == 0), stop=(k == KD - 1))
                    mm.then_inc(s_e2, 1)
                    pe.wait_ge(s_cnt, 4 * g + 3 + i)
                    nc.tensor.matmul(ps[:, 6, 2 + i:3 + i], c["first_row"][:], cnt[:, 2 + i:3 + i], start=True,
                                     stop=True).then_inc(s_len, 1)
                    pe.wait_ge(s_exp, 4 * g + 3 + i)
                    for b in range(KS):
                        mm = nc.tensor.transpose(ps[:, 4 + i, b * P:(b + 1) * P], pr2[:, i, b * P:(b + 1) * P],
                                                 c["ident"][:])
                    mm.then_inc(s_pT, 1)
                    pe.wait_ge(s_pTs, 4 * g + 3 + i)
                    for h in range(2):
                        for m in range(KD):
                            for b in range(KS):
                                o = m * P + h * L
                                mm = nc.tensor.matmul(ps[:, i, o:o + L], ctx_kd[:, h, b, m * P:(m + 1) * P],
                                                      pr2T[:, i, b, h * L:(h + 1) * L],
                                                      start=(b == 0), stop=(b == KS - 1))
                    mm.then_inc(s_c_mm, 1)
                for i in range(2):
                    pe.wait_ge(s_c, 2 * g + i + 1)
                    for k in range(KD):
                        mm = nc.tensor.matmul(ps[:, 2 + i, :], cT[:, i, k, :], wv2[:, k, :],
                                              start=(k == 0), stop=(k == KD - 1))
                    mm.then_inc(s_z, 1)
                pe.wait_ge(s_x2, 2 * g + 2)
                transposes(x2)
                pe.wait_ge(s_tT, 6 * g + 6)
                widths_out(fc1, tT, s_f1_mm)
                pe.wait_ge(s_h, 4 * g + 4)
                for i in range(2):
                    for k in range(KD):
                        nc.tensor.matmul(ps[:, 2 + i, :], hT[:, k, i * P:(i + 1) * P], fc2[:, k, :],
                                         start=(k == 0), stop=False)
                    nc.tensor.matmul(ps[:, 2 + i, :], c["ones"][0:1, :], fc2_b[0:1, :], start=False,
                                     stop=True).then_inc(s_z, 1)

        @block.scalar
        def _(act):
            for a in range(2):
                for m in range(KD):
                    act.wait_ge(s_wqk_mm, 4 * a + m + 1)
                    nc.scalar.copy(wqk[a][:, m, :], ps[:, m, :]).then_inc(s_wqk, 1)
            act.wait_ge(s_w["rest"], 16 * 6)

            with nc.scalar.Fori(0, G) as g:
                def spread(n_tr):
                    act.wait_ge(s_tr, 3 * g + n_tr)
                    for b in range(2):
                        nc.scalar.copy(tT[:, 2 * b:2 * b + 2, :].rearrange("p k t -> p (k t)"),
                                       ps[:, b, :]).then_inc(s_tT, 1)

                def queries(n):
                    act.wait_ge(s_q_mm, 2 * g + n)
                    for b in range(2):
                        nc.scalar.copy(qT[:, 2 * b:2 * b + 2, :].rearrange("p k t -> p (k t)"),
                                       ps[:, b, :]).then_inc(s_q, 1)

                spread(1)
                queries(1)
                for i in range(2):
                    act.wait_ge(s_bias, 4 * g + i + 1)
                    nc.scalar.activation(pr1[:, i, :], msk1[:, i, :], ACT.Exp, bias=nmx[:, i:i + 1], scale=SCALE,
                                         accum_out=rsum[:, i:i + 1]).then_inc(s_exp, 1)
                act.wait_ge(s_pT, 4 * g + 2)
                for i in range(2):
                    nc.scalar.copy(pr1T[:, i, :], ps[:, 7, i * P:(i + 1) * P]).then_inc(s_pTs, 1)
                spread(2)
                queries(2)
                for i in range(2):
                    act.wait_ge(s_bias, 4 * g + 3 + i)
                    nc.scalar.activation(pr2[:, i, :], msk2[:, i, :], ACT.Exp, bias=nmx[:, 2 + i:3 + i],
                                         scale=SCALE, accum_out=rsum[:, 2 + i:3 + i]).then_inc(s_exp, 1)
                    act.wait_ge(s_pT, 4 * g + 3 + i)
                    nc.scalar.copy(pr2T[:, i].rearrange("p b t -> p (b t)"), ps[:, 4 + i, :]).then_inc(s_pTs, 1)
                    act.wait_ge(s_c_mm, 2 * g + i + 1)
                    nc.scalar.copy(cT[:, i].rearrange("p k t -> p (k t)"), ps[:, i, :]).then_inc(s_c, 1)
                spread(3)
                act.wait_ge(s_f1_mm, g + 1)
                for m in range(KD):
                    nc.scalar.activation(hT[:, m, :], ps[:, m // 2, (m % 2) * TG:(m % 2 + 1) * TG], ACT.Relu,
                                         bias=fc1_b[:, m:m + 1]).then_inc(s_h, 1)

        DVE_STEPS = 44

        @block.vector
        def _(dve):
            dve.wait_ge(s_const, n_const)
            dve.wait_ge(s_x, 16)
            dve.wait_ge(s_w["ln"], 16 * 6)
            with nc.vector.Fori(0, G) as g:
                steps = [0]

                def own(*instructions):
                    for ins in instructions:
                        ins.then_inc(s_dve, 1)
                    steps[0] += len(instructions)
                    dve.wait_ge(s_dve, DVE_STEPS * g + steps[0])

                def norm(which, src, dst, gains, s_out):
                    stand_alone(dve)
                    own(*[nc.vector.bn_stats(bst[:, i, :], src(i)) for i in range(2)])
                    stand_alone(dve)
                    for i in range(2):
                        nc.vector.bn_aggr(mv[:, i, :], bst[:, i, :]).then_inc(s_var, 1)
                    dve.wait_ge(s_rstd, 4 * g + which + 1)
                    dve.wait_ge(s_var, 8 * g + 2 * which + 2)
                    ins = [nc.vector.tensor_scalar(dst(i), src(i), mv[:, i, 0:1], rstd[:, i:i + 1],
                                                   ALU.subtract, ALU.mult) for i in range(2)]
                    if gains is not None:
                        own(*ins)
                        own(*[nc.vector.tensor_tensor(dst(i), dst(i), ln[:, 2 * gains, :], ALU.mult)
                              for i in range(2)])
                        ins = [nc.vector.tensor_tensor(dst(i), dst(i), ln[:, 2 * gains + 1, :], ALU.add)
                               for i in range(2)]
                    if s_out is None:
                        own(*ins)
                    else:
                        for x in ins:
                            x.then_inc(s_out, 1)

                norm(0, lambda i: xres[:, 2 * g + i, :], lambda i: xn[:, i, :], None, s_xn)
                for i in range(2):
                    dve.wait_ge(s_v_mm, 2 * g + i + 1)
                    nc.vector.tensor_copy(v1[:, i, :], ps[:, 2 + i, :]).then_inc(s_v, 1)
                for i in range(2):
                    dve.wait_ge(s_e1, 2 * g + i + 1)
                    nc.vector.scalar_tensor_tensor(msk1[:, i, :], ps[:, 4 + i, 0:P], 0.0, c["same_batch"][:],
                                                   ALU.not_equal, ALU.mult,
                                                   accum_out=cnt[:, i:i + 1]).then_inc(s_cnt, 1)
                dve.wait_ge(s_len, 3 * g + 1)
                dve.wait_ge(s_cnt, 4 * g + 2)
                own(*[nc.vector.scalar_tensor_tensor(msk1[:, i, :], c["key_in_batch"][:], ps[:, 6, i:i + 1],
                                                     c["causal"][:], ALU.is_ge, ALU.max) for i in range(2)])
                own(*[nc.vector.scalar_tensor_tensor(msk1[:, i, :], msk1[:, i, :], BIG, ps[:, 4 + i, 0:P],
                                                     ALU.mult, ALU.add) for i in range(2)])
                own(*[nc.vector.tensor_reduce(cnt[:, i:i + 1], msk1[:, i, :], AX.X, ALU.max) for i in range(2)])
                for i in range(2):
                    nc.vector.tensor_scalar(nmx[:, i:i + 1], cnt[:, i:i + 1], -SCALE, None,
                                            ALU.mult).then_inc(s_bias, 1)
                for i in range(2):
                    dve.wait_ge(s_exp, 4 * g + i + 1)
                    own(nc.vector.reciprocal(rinv[:, i:i + 1], rsum[:, i:i + 1]))
                    dve.wait_ge(s_z, 6 * g + i + 1)
                    own(nc.vector.scalar_tensor_tensor(x1[:, i, :], ps[:, 2 + i, :], rinv[:, i:i + 1], xn[:, i, :],
                                                       ALU.mult, ALU.add))
                norm(1, lambda i: x1[:, i, :], lambda i: x1[:, i, :], 0, s_x1)
                for i in range(2):
                    dve.wait_ge(s_e2, 2 * g + i + 1)
                    nc.vector.tensor_scalar(msk2[:, i, :], ps[:, 4 + i, :], 0.0, None, ALU.not_equal, ALU.add,
                                            accum_out=cnt[:, 2 + i:3 + i]).then_inc(s_cnt, 1)
                    dve.wait_ge(s_len, 3 * g + 2 + i)
                    dve.wait_ge(s_cnt, 4 * g + 3 + i)
                    own(nc.vector.tensor_scalar(msk2[:, i, :], c["key_index"][:], ps[:, 6, 2 + i:3 + i], BIG,
                                                ALU.is_ge, ALU.mult))
                    own(nc.vector.tensor_tensor(msk2[:, i, :], msk2[:, i, :], ps[:, 4 + i, :], ALU.add))
                    own(nc.vector.tensor_reduce(cnt[:, 2 + i:3 + i], msk2[:, i, :], AX.X, ALU.max))
                    nc.vector.tensor_scalar(nmx[:, 2 + i:3 + i], cnt[:, 2 + i:3 + i], -SCALE, None,
                                            ALU.mult).then_inc(s_bias, 1)
                for i in range(2):
                    dve.wait_ge(s_exp, 4 * g + 3 + i)
                    own(nc.vector.reciprocal(rinv[:, 2 + i:3 + i], rsum[:, 2 + i:3 + i]))
                    dve.wait_ge(s_z, 6 * g + 3 + i)
                    own(nc.vector.scalar_tensor_tensor(x2[:, i, :], ps[:, 2 + i, :], rinv[:, 2 + i:3 + i],
                                                       x1[:, i, :], ALU.mult, ALU.add))
                norm(2, lambda i: x2[:, i, :], lambda i: x2[:, i, :], 1, s_x2)
                for i in range(2):
                    dve.wait_ge(s_z, 6 * g + 5 + i)
                    own(nc.vector.tensor_tensor(x1[:, i, :], ps[:, 2 + i, :], x2[:, i, :], ALU.add))
                norm(3, lambda i: x1[:, i, :], lambda i: x1[:, i, :], 2, None)
                for i in range(2):
                    nc.vector.tensor_tensor(xres[:, 2 * g + i, :], xres[:, 2 * g + i, :], x1[:, i, :],
                                            ALU.add).then_inc(s_done, 1)
                assert steps[0] == DVE_STEPS, steps[0]
            dve.wait_ge(s_done, 2 * G)


def mamba_block(nc, d, c, s_const, n_const, xres, xf_d, xfT_d, logits, sem, s_xf_d, zero_rows):
    with ExitStack() as ctx:
        def sb(name, shape, dt=F32):
            return ctx.enter_context(nc.sbuf_tensor("B_" + name, shape, dt))

        ps = ctx.enter_context(nc.psum_tensor("psB", [P, 8, 512], F32))
        w_in = sb("w_in", [P, KD, 2 * C])
        w_x = sb("w_x", [P, MC, 96])
        w_dt = sb("w_dt", [NS + 1, C])
        w_out = sb("w_out", [P, MC, D])
        gate_w = sb("gate_w", [P, KD, E])
        chan = sb("chan", [P, MC, 9])
        a_neg = sb("a_neg", [P, MC])
        b_out = sb("b_out", [P, D])
        xm = sb("xm", [P, 2, D])
        xmT = sb("xmT", [P, KD, TG])
        b_rep = xmT[:].rearrange("p k t -> p (k t)").rearrange("p (m j) -> p m j", m=MC)
        xe = sb("xe", [P, MC, 4, L + 3])
        zs = sb("zs", [P, MC, TG])
        xc = sb("xc", [P, MC, TG])
        dtr = sb("dtr", [NS + 1, TG])
        bT = sb("bT", [NS, TG])
        cTt = sb("cTt", [NS, TG])
        btok = sb("btok", [P, 2, NS])
        bd = sb("bd", [P, 2, 16, NS])
        cd = sb("cd", [P, 4, L])
        t0 = sb("t0", [P, MC, TG])
        t1 = sb("t1", [P, MC, TG])
        dec = sb("dec", [P, MC, TG])
        v = [sb(f"v{a}", [P, MC, TG]) for a in range(2)]
        y = sb("y", [P, MC, TG])
        prod = sb("prod", [P, MC, TG])
        cb = prod[0:NS].rearrange("n m t -> n (m t)").rearrange("n (j t) -> n j t", j=Q)
        vend = sb("vend", [P, MC, TG])
        st = sb("st", [P, MC, TG * NS // Q])
        stmp = sb("stmp", [P, 4 * MC, NS])
        bst = sb("bstB", [P, 2, 6])
        mv = sb("mvB", [P, 2, 2])
        ve = sb("veB", [P, 2])
        rstd = sb("rstdB", [P, 2])
        vT = dec[:].rearrange("p m t -> p (m t)").rearrange("p (i n) -> p i n", i=2)
        stT = [t1, v[0]]

        def stT_of(b):
            return stT[b // 2][:].rearrange("p m t -> p (m t)")[:, (b % 2) * C:(b % 2 + 1) * C]

        s_w = sem("B_weights")
        s_g = sem("B_gate_w")
        s_brep = sem("B_brep")
        s_gain = sem("B_gain")
        s_bo = sem("B_bo")
        s_aexp = sem("B_aexp")
        s_aneg = sem("B_aneg")
        s_bo_mm = sem("B_bo_mm")
        s_zero = sem("B_zero")
        s_xm = sem("B_xm")
        s_var = sem("B_var")
        s_ve = sem("B_ve")
        s_rstd = sem("B_rstd")
        s_tr = sem("B_tr")
        s_xmT = sem("B_xmT")
        s_xz_mm = sem("B_xz_mm")
        s_xz = sem("B_xz")
        s_conv = sem("B_conv")
        s_xc = sem("B_xc")
        s_pr_mm = sem("B_pr_mm")
        s_pr = sem("B_pr")
        s_dt_mm = sem("B_dt_mm")
        s_act = sem("B_act")
        s_ln = sem("B_ln")
        s_cb = sem("B_cb")
        s_cb_mm = sem("B_cb_mm")
        s_cr_mm = sem("B_cr_mm")
        s_cd = sem("B_cd")
        s_bd = sem("B_bd")
        s_S = sem("B_S")
        s_dec = sem("B_dec")
        s_v = sem("B_v")
        s_vend = sem("B_vend")
        s_prod = sem("B_prod")
        s_vT_mm = sem("B_vT_mm")
        s_vT = sem("B_vT")
        s_u_mm = sem("B_u_mm")
        s_u = sem("B_u")
        s_st = sem("B_st")
        s_sT_mm = sem("B_sT_mm")
        s_sT = sem("B_sT")
        s_y2 = sem("B_y2")
        s_y = sem("B_y")
        s_mean = sem("B_mean")
        s_yc = sem("B_yc")
        s_sq = sem("B_sq")
        s_vcol = sem("B_vcol")
        s_vc = sem("B_vc")
        s_out = sem("B_out")
        s_lg_mm = sem("B_lg_mm")
        s_lg = sem("B_lg")
        s_dve = sem("B_dve")

        def stand_alone(eng):
            eng.sem_inc(s_passed, 1)

        s_passed = sem("B_waits_passed")

        block = ctx.enter_context(nc.Block())

        @block.sync
        def _(sp):
            for k in range(KD):
                sp.dma_start(w_in[:, k, :], d["w_in"][k * P:(k + 1) * P, :]).then_inc(s_w, 16)
            sp.dma_start(w_x[:], d["w_x"].rearrange("(m p) n -> p m n", p=P)).then_inc(s_w, 16)
            sp.dma_start(w_dt[:], d["w_dt"]).then_inc(s_w, 16)
            sp.dma_start(chan[:], d["chan"]).then_inc(s_w, 16)
            sp.dma_start(w_out[:], d["w_out"].rearrange("(m p) n -> p m n", p=P)).then_inc(s_w, 16)
            sp.dma_start(gate_w[:], d["gate_w"].rearrange("(k p) n -> p k n", p=P)).then_inc(s_g, 16)
            zero_rows(sp)
            sp.sem_inc(s_xf_d, 1)
            with nc.sync.Fori(0, G) as g:
                sp.wait_ge(s_xm, 4 * g + 4)
                sp.dma_start(xf_d.rearrange("(g i p) n -> g p i n", i=2, p=P)[g], xm[:]).then_inc(s_xf_d, 16)
                sp.wait_ge(s_xmT, 4 * g + 4)
                sp.dma_start(xfT_d.rearrange("(k p) (g t) -> g p k t", p=P, g=G)[g], xmT[:]).then_inc(s_xf_d, 16)

        N_W = 16 * 8

        @block.gpsimd
        def _(pool):
            pool.memset(xe[:].rearrange("p m b t -> p (m b) t")[:, :, 0:3], 0.0).then_inc(s_zero, 1)
            pool.memset(cb, 0.0).then_inc(s_zero, 1)
            pool.memset(dtr[:], 1.0).then_inc(s_zero, 1)
            pool.wait_ge(s_zero, 3)
            with nc.gpsimd.Fori(0, G) as g:
                def rsqrt(n):
                    pool.wait_ge(s_var, 4 * g + n)
                    nc.gpsimd.tensor_tensor(ve[:], mv[:, :, 1], c["eps"][:], ALU.add).then_inc(s_ve, 1)

                def power(n):
                    pool.wait_ge(s_ve, 3 * g + n)
                    nc.gpsimd.tensor_tensor(rstd[:], ve[:], c["minus_half"][:, 0:2], ALU.pow).then_inc(s_rstd, 1)

                rsqrt(2)
                power(1)
                pool.wait_ge(s_pr, 4 * g + 4)
                for j in range(Q):
                    nc.gpsimd.tensor_tensor(cb[:, j, j:TG], cTt[:, j:TG], bT[:, 0:TG - j], ALU.mult).then_inc(s_cb, 1)
                for i in range(2):
                    nc.gpsimd.tensor_tensor(bd[:, i], c["own_chunk"][:],
                                            btok[:, i, :].unsqueeze(1).to_broadcast([P, 16, NS]),
                                            ALU.mult).then_inc(s_bd, 1)
                dch = dec[:].rearrange("p m (k t) -> p (m k) t", t=Q)
                pch = prod[:].rearrange("p m (k t) -> p (m k) t", t=Q)
                pool.wait_ge(s_cb_mm, g + 1)
                pool.wait_ge(s_dec, 8 * g + 8)
                nc.gpsimd.tensor_tensor(pch[:, :, 0:1], dch[:, :, 0:1],
                                        c["ones"][:, 0:1].unsqueeze(1).to_broadcast([P, MC * TG // Q, 1]),
                                        ALU.mult).then_inc(s_prod, 1)
                for t in range(1, Q):
                    pool.wait_ge(s_prod, 8 * g + t)
                    nc.gpsimd.tensor_tensor(pch[:, :, t:t + 1], pch[:, :, t - 1:t], dch[:, :, t:t + 1],
                                            ALU.mult).then_inc(s_prod, 1)
                pool.wait_ge(s_vc, g + 1)
                nc.gpsimd.tensor_tensor(ve[:], mv[:, :, 1], c["eps"][:], ALU.add).then_inc(s_ve, 1)
                power(2)
                rsqrt(4)
                power(3)

        @block.tensor
        def _(pe):
            pe.wait_ge(s_brep, MC)
            for m in range(MC):
                mm = nc.tensor.matmul(ps[:, 0, :], b_rep[:, m, :], w_out[:, m, :], start=(m == 0), stop=(m == MC - 1))
            mm.then_inc(s_bo_mm, 1)
            pe.wait_ge(s_gain, MC)
            pe.wait_ge(s_bo, 1)
            pe.wait_ge(s_zero, 3)
            pe.wait_ge(s_g, 16)

            with nc.tensor.Fori(0, G) as g:
                dmaj = ps[:, 0:2, :].rearrange("p b (k t) -> p (b k) t", k=2)

                def transposes():
                    for i in range(2):
                        for k in range(KD):
                            mm = nc.tensor.transpose(dmaj[:, k, i * P:(i + 1) * P], xm[:, i, k * P:(k + 1) * P],
                                                     c["ident"][:])
                    mm.then_inc(s_tr, 1)

                pe.wait_ge(s_xm, 4 * g + 2)
                transposes()
                pe.wait_ge(s_xmT, 4 * g + 2)
                for j in range(MC):
                    if j >= 6:
                        pe.wait_ge(s_xz, 8 * g + j - 5)
                    for a in range(2):
                        m = 2 * j + a
                        for k in range(KD):
                            mm = nc.tensor.matmul(ps[:, 2 + j % 6, a * TG:(a + 1) * TG], w_in[:, k, m * P:(m + 1) * P],
                                                  xmT[:, k, :], start=(k == 0), stop=(k == KD - 1))
                    mm.then_inc(s_xz_mm, 1)
                pe.wait_ge(s_xc, g + 1)
                for m in range(MC):
                    nc.tensor.matmul(ps[0:96, 0, 0:TG], w_x[:, m, :], xc[:, m, :], start=(m == 0), stop=(m == MC - 1))
                for i in range(2):
                    for m in range(MC):
                        mm = nc.tensor.matmul(ps[:, 1, i * NS:(i + 1) * NS], xc[:, m, i * P:(i + 1) * P],
                                              w_x[:, m, 32:32 + NS], start=(m == 0), stop=(m == MC - 1))
                mm.then_inc(s_pr_mm, 1)
                pe.wait_ge(s_pr, 4 * g + 4)
                pe.wait_ge(s_xz, 8 * g + 8)
                for m in range(MC):
                    mm = nc.tensor.matmul(ps[:, m // 2, (m % 2) * TG:(m % 2 + 1) * TG], w_dt[:, m * P:(m + 1) * P],
                                          dtr[:], start=True, stop=True)
                mm.then_inc(s_dt_mm, 1)
                nc.tensor.matmul(ps[:, 4, 0:TG], c["rep_state"][:].rearrange("n k m -> n (k m)"), cTt[:],
                                 start=True, stop=True).then_inc(s_cr_mm, 1)
                pe.wait_ge(s_cd, g + 1)
                for j in range(Q):
                    pe.wait_ge(s_cb, 8 * g + j + 1)
                    mm = nc.tensor.matmul(ps[:, 4 + j // 2, (j % 2) * TG:(j % 2 + 1) * TG], c["ones"][0:NS, :],
                                          cb[:, j, :], start=True, stop=True)
                mm.then_inc(s_cb_mm, 1)
                pe.wait_ge(s_vend, 8 * g + 8)
                for i in range(2):
                    for a in range(2):
                        for m in range(4):
                            mm = nc.tensor.transpose(ps[:, 2 * i + a, m * P:(m + 1) * P],
                                                     vend[:, 4 * a + m, i * P:(i + 1) * P], c["ident"][:])
                        mm.then_inc(s_vT_mm, 1)
                for i in range(2):
                    pe.wait_ge(s_bd, 2 * g + i + 1)
                    pe.wait_ge(s_vT, 4 * g + 4)
                    for a in range(4):
                        if i:
                            pe.wait_ge(s_u, 8 * g + a + 1)
                        for m in range(2 * a, 2 * a + 2):
                            mm = nc.tensor.matmul(ps[:, a, (m % 2) * TG:(m % 2 + 1) * TG], vT[:, i, m * P:(m + 1) * P],
                                                  bd[:, i].rearrange("p k n -> p (k n)"), start=True, stop=True)
                        mm.then_inc(s_u_mm, 1)
                pe.wait_ge(s_st, g + 1)
                for b in range(4):
                    for a in range(2):
                        j = 2 * b + a
                        if j >= 4:
                            pe.wait_ge(s_sT, 8 * g + j - 3)
                        for m in range(4):
                            mm = nc.tensor.transpose(ps[:, j % 4, m * P:(m + 1) * P],
                                                     st[:, 4 * a + m, b * P:(b + 1) * P], c["ident"][:])
                        mm.then_inc(s_sT_mm, 1)
                pe.wait_ge(s_sT, 8 * g + 8)
                for m in range(MC):
                    for b in range(4):
                        mm = nc.tensor.matmul(ps[:, 4 + m // 2, (m % 2) * TG + b * L:(m % 2) * TG + (b + 1) * L],
                                              stT_of(b)[:, m * P:(m + 1) * P], cd[:, b, :], start=True, stop=True)
                mm.then_inc(s_y2, 1)
                pe.wait_ge(s_y, g + 1)
                for m in range(MC):
                    mm = nc.tensor.matmul(ps[:, 0, 0:TG], c["ones_over_c"][:], y[:, m, :], start=(m == 0),
                                          stop=(m == MC - 1))
                mm.then_inc(s_mean, 1)
                pe.wait_ge(s_yc, g + 1)
                for i in range(2):
                    for m in range(MC):
                        mm = nc.tensor.matmul(ps[:, 2 + i, :], y[:, m, i * P:(i + 1) * P], w_out[:, m, :],
                                              start=(m == 0), stop=(m == MC - 1))
                    mm.then_inc(s_out, 1)
                pe.wait_ge(s_sq, g + 1)
                for i in range(2):
                    for m in range(MC):
                        mm = nc.tensor.matmul(ps[:, 1, i:i + 1], t1[:, m, i * P:(i + 1) * P],
                                              c["ones_over_c"][:, 0:1], start=(m == 0), stop=(m == MC - 1))
                mm.then_inc(s_vcol, 1)
                pe.wait_ge(s_xm, 4 * g + 4)
                transposes()
                pe.wait_ge(s_xmT, 4 * g + 4)
                for i in range(2):
                    for k in range(KD):
                        mm = nc.tensor.matmul(ps[:, 2, i * E:(i + 1) * E], xmT[:, k, i * P:(i + 1) * P], gate_w[:, k, :],
                                              start=(k == 0), stop=(k == KD - 1))
                mm.then_inc(s_lg_mm, 1)

        ACT_STEPS = 2

        @block.scalar
        def _(act):
            act.wait_ge(s_w, N_W)
            for m in range(MC):
                nc.scalar.activation(b_rep[:, m, :], c["ones"][:], ACT.Identity,
                                     scale=chan[:, m, 8:9]).then_inc(s_brep, 1)
            nc.scalar.activation(a_neg[:], chan[:, :, 5], ACT.Exp).then_inc(s_aexp, 1)
            act.wait_ge(s_bo_mm, 1)
            for m in range(MC):
                nc.scalar.activation(w_out[:, m, :], w_out[:, m, :], ACT.Identity,
                                     scale=chan[:, m, 7:8]).then_inc(s_gain, 1)
            act.wait_ge(s_aneg, 1)
            with nc.scalar.Fori(0, G) as g:
                steps = [0]

                def own(ins):
                    ins.then_inc(s_act, 1)
                    steps[0] += 1
                    act.wait_ge(s_act, ACT_STEPS * g + steps[0])

                def spread(n):
                    act.wait_ge(s_tr, 2 * g + n)
                    for b in range(2):
                        nc.scalar.copy(xmT[:, 2 * b:2 * b + 2, :].rearrange("p k t -> p (k t)"),
                                       ps[:, b, :]).then_inc(s_xmT, 1)

                act.wait_ge(s_xf_d, 32 * g + 1)
                spread(1)
                for j in range(MC):
                    act.wait_ge(s_xz_mm, 8 * g + j + 1)
                    src = ps[:, 2 + j % 6, :]
                    if j < 4:
                        nc.scalar.copy(xe[:, 2 * j:2 * j + 2].rearrange("p m b t -> p (m b) t")[:, :, 3:],
                                       src.rearrange("p (mb t) -> p mb t", t=L)).then_inc(s_xz, 1)
                    else:
                        nc.scalar.activation(zs[:, 2 * j - 8:2 * j - 6, :].rearrange("p m t -> p (m t)"), src,
                                             ACT.Silu).then_inc(s_xz, 1)
                act.wait_ge(s_conv, MC * g + MC)
                nc.scalar.activation(xc[:], xc[:], ACT.Silu).then_inc(s_xc, 1)
                act.wait_ge(s_pr_mm, g + 1)
                nc.scalar.copy(dtr[0:NS, :], ps[0:NS, 0, 0:TG]).then_inc(s_pr, 1)
                nc.scalar.copy(bT[:], ps[32:32 + NS, 0, 0:TG]).then_inc(s_pr, 1)
                nc.scalar.copy(cTt[:], ps[64:64 + NS, 0, 0:TG]).then_inc(s_pr, 1)
                nc.scalar.copy(btok[:].rearrange("p i n -> p (i n)"), ps[:, 1, 0:2 * NS]).then_inc(s_pr, 1)
                act.wait_ge(s_dt_mm, g + 1)
                own(nc.scalar.activation(t0[:].rearrange("p m t -> p (m t)"),
                                         ps[:, 0:4, :].rearrange("p b n -> p (b n)"), ACT.Abs))
                own(nc.scalar.activation(t0[:], t0[:], ACT.Exp, scale=-1.0))
                nc.scalar.activation(t1[:], t0[:], ACT.Ln, bias=1.0).then_inc(s_ln, 1)
                for m in range(MC):
                    act.wait_ge(s_S, MC * g + m + 1)
                    nc.scalar.activation(dec[:, m, :], t1[:, m, :], ACT.Exp, scale=a_neg[:, m:m + 1]).then_inc(s_dec, 1)
                for j in range(Q):
                    act.wait_ge(s_v, 8 * g + j + 1)
                    src = v[j % 2][:].rearrange("p m (k t) -> p (m k) t", t=Q)[:, :, Q - 1:Q]
                    dst = vend[:].rearrange("p m (k t) -> p (m k) t", t=Q)[:, :, Q - 1 - j:Q - j]
                    nc.scalar.copy(dst, src).then_inc(s_vend, 1)
                act.wait_ge(s_prod, 8 * g + 8)
                for b in range(4):
                    act.wait_ge(s_vT_mm, 4 * g + b + 1)
                    nc.scalar.copy(vT[:, b // 2, (b % 2) * 512:(b % 2 + 1) * 512], ps[:, b, :]).then_inc(s_vT, 1)
                for i in range(2):
                    for a in range(4):
                        act.wait_ge(s_u_mm, 8 * g + 4 * i + a + 1)
                        nc.scalar.copy(st[:, 2 * a:2 * a + 2, i * TG:(i + 1) * TG],
                                       ps[:, a, :].rearrange("p (m n) -> p m n", m=2)).then_inc(s_u, 1)
                for j in range(8):
                    act.wait_ge(s_sT_mm, 8 * g + j + 1)
                    nc.scalar.copy(stT_of(j // 2)[:, (j % 2) * 512:(j % 2 + 1) * 512], ps[:, j % 4, :]).then_inc(s_sT, 1)
                act.wait_ge(s_yc, g + 1)
                nc.scalar.activation(t1[:], y[:], ACT.Square).then_inc(s_sq, 1)
                spread(2)
                act.wait_ge(s_lg_mm, g + 1)
                nc.scalar.copy(logits[:, bass.ds(2 * g, 2), :],
                               ps[:, 2, 0:2 * E].rearrange("p (i e) -> p i e", i=2)).then_inc(s_lg, 1)
                assert steps[0] == ACT_STEPS, steps[0]

        DVE_STEPS = 72

        @block.vector
        def _(dve):
            dve.wait_ge(s_w, N_W)
            dve.wait_ge(s_aexp, 1)
            nc.vector.tensor_scalar(a_neg[:], a_neg[:], -1.0, None, ALU.mult).then_inc(s_aneg, 1)
            dve.wait_ge(s_bo_mm, 1)
            nc.vector.tensor_copy(b_out[:], ps[:, 0, :]).then_inc(s_bo, 1)
            dve.wait_ge(s_bo, 1)

            with nc.vector.Fori(0, G) as g:
                steps = [0]

                def own(*instructions):
                    for ins in instructions:
                        ins.then_inc(s_dve, 1)
                    steps[0] += len(instructions)
                    dve.wait_ge(s_dve, DVE_STEPS * g + steps[0])

                def chunks(t):
                    return t[:].rearrange("p m (k t) -> p (m k) t", t=Q)

                def norm(src, dst, n, s_out):
                    stand_alone(dve)
                    own(*[nc.vector.bn_stats(bst[:, i, :], src(i)) for i in range(2)])
                    stand_alone(dve)
                    for i in range(2):
                        nc.vector.bn_aggr(mv[:, i, :], bst[:, i, :]).then_inc(s_var, 1)
                    dve.wait_ge(s_rstd, 3 * g + (1 if n == 1 else 3))
                    dve.wait_ge(s_var, 4 * g + 2 * n)
                    for i in range(2):
                        nc.vector.tensor_scalar(dst(i), src(i), mv[:, i, 0:1], rstd[:, i:i + 1],
                                                ALU.subtract, ALU.mult).then_inc(s_out, 1)

                dve.wait_ge(s_xf_d, 32 * g + 1)
                norm(lambda i: xres[:, 2 * g + i, :], lambda i: xm[:, i, :], 1, s_xm)
                dve.wait_ge(s_xz, 8 * g + 4)
                own(*[nc.vector.tensor_scalar(xc[:, m, :].rearrange("p (b t) -> p b t", b=4), xe[:, m, :, 3:3 + L],
                                              chan[:, m, 3:4], chan[:, m, 4:5], ALU.mult, ALU.add)
                      for m in range(MC)])
                for j in range(3):
                    ins = [nc.vector.scalar_tensor_tensor(
                        xc[:, m, :].rearrange("p (b t) -> p b t", b=4), xe[:, m, :, j:j + L], chan[:, m, j:j + 1],
                        xc[:, m, :].rearrange("p (b t) -> p b t", b=4), ALU.mult, ALU.add) for m in range(MC)]
                    if j < 2:
                        own(*ins)
                for x in ins:
                    x.then_inc(s_conv, 1)
                dve.wait_ge(s_cr_mm, g + 1)
                nc.vector.tensor_tensor(cd[:].rearrange("p b t -> p (b t)").rearrange("p (b t) -> p b t", b=4),
                                        ps[:, 4, 0:TG].rearrange("p (b t) -> p b t", b=4),
                                        c["next_chunk"][:].rearrange("p k t -> p (k t)").unsqueeze(1).to_broadcast(
                                            [P, 4, L]), ALU.mult).then_inc(s_cd, 1)
                dve.wait_ge(s_ln, g + 1)
                own(nc.vector.tensor_scalar(y[:], t0[:], 1.0, 1.0, ALU.add, ALU.subtract))
                own(nc.vector.tensor_tensor(y[:], t1[:], y[:], ALU.subtract))
                own(nc.vector.tensor_tensor(y[:], y[:], t0[:], ALU.add))
                own(nc.vector.scalar_tensor_tensor(y[:].rearrange("p m t -> p (m t)"),
                                                   ps[:, 0:4, :].rearrange("p b n -> p (b n)"), 0.0,
                                                   y[:].rearrange("p m t -> p (m t)"), ALU.max, ALU.add))
                for m in range(MC):
                    nc.vector.tensor_tensor_scan(t1[:, m, :], c["in_sequence"][:], y[:, m, :], 0.0, ALU.mult,
                                                 ALU.add).then_inc(s_S, 1)
                nc.vector.tensor_tensor(v[0][:], y[:], xc[:], ALU.mult).then_inc(s_v, 1)
                dve.wait_ge(s_v, 8 * g + 1)
                dve.wait_ge(s_cb_mm, g + 1)

                def weight(j):
                    return ps[:, 4 + j // 2, (j % 2) * TG:(j % 2 + 1) * TG].rearrange(
                        "p (k t) -> p k t", t=Q).unsqueeze(1)[:, :, :, j:Q].to_broadcast([P, MC, TG // Q, Q - j])

                def four(t, j):
                    return t[:].rearrange("p m (k t) -> p m k t", t=Q)[:, :, :, j:Q]

                own(nc.vector.tensor_tensor(four(y, 0), four(v[0], 0), weight(0), ALU.mult))
                dve.wait_ge(s_dec, 8 * g + 8)
                for j in range(1, Q):
                    new, old = v[j % 2], v[(j - 1) % 2]
                    if j >= 2:
                        dve.wait_ge(s_vend, 8 * g + j - 1)
                    nc.vector.tensor_tensor(chunks(new)[:, :, j:Q], chunks(dec)[:, :, j:Q],
                                            chunks(old)[:, :, j - 1:Q - 1], ALU.mult).then_inc(s_v, 1)
                    dve.wait_ge(s_v, 8 * g + j + 1)
                    own(nc.vector.tensor_tensor(four(t0, j), four(new, j), weight(j), ALU.mult))
                    own(nc.vector.tensor_tensor(chunks(y)[:, :, j:Q], chunks(y)[:, :, j:Q], chunks(t0)[:, :, j:Q],
                                                ALU.add))
                own(*[nc.vector.scalar_tensor_tensor(y[:, m, :], xc[:, m, :], chan[:, m, 6:7], y[:, m, :],
                                                     ALU.mult, ALU.add) for m in range(MC)])
                dve.wait_ge(s_u, 8 * g + 8)
                dve.wait_ge(s_prod, 8 * g + 8)
                stk = st[:].rearrange("p m (b k n) -> p (m b) k n", b=4, k=Q)
                pck = prod[:].rearrange("p m (b k t) -> p (m b) k t", b=4, k=Q)
                for k in range(1, Q - 1):
                    own(nc.vector.tensor_tensor(stmp[:], stk[:, :, k - 1, :],
                                                pck[:, :, k, Q - 1:Q].to_broadcast([P, 4 * MC, NS]), ALU.mult))
                    add = nc.vector.tensor_tensor(stk[:, :, k, :], stk[:, :, k, :], stmp[:], ALU.add)
                    if k < Q - 2:
                        own(add)
                add.then_inc(s_st, 1)
                dve.wait_ge(s_y2, g + 1)
                own(nc.vector.tensor_tensor(v[1][:].rearrange("p m t -> p (m t)"),
                                            prod[:].rearrange("p m t -> p (m t)"),
                                            ps[:, 4:8, :].rearrange("p b n -> p (b n)"), ALU.mult))
                own(nc.vector.tensor_tensor(y[:], y[:], v[1][:], ALU.add))
                nc.vector.tensor_tensor(y[:], y[:], zs[:], ALU.mult).then_inc(s_y, 1)
                dve.wait_ge(s_mean, g + 1)
                dve.wait_ge(s_y, g + 1)
                nc.vector.tensor_tensor(y[:], y[:], ps[:, 0, 0:TG].unsqueeze(1).to_broadcast([P, MC, TG]),
                                        ALU.subtract).then_inc(s_yc, 1)
                own(*[nc.vector.tensor_tensor(xres[:, 2 * g + i, :], xres[:, 2 * g + i, :], b_out[:], ALU.add)
                      for i in range(2)])
                dve.wait_ge(s_vcol, g + 1)
                nc.vector.tensor_copy(mv[:, :, 1], ps[:, 1, 0:2]).then_inc(s_vc, 1)
                dve.wait_ge(s_rstd, 3 * g + 2)
                dve.wait_ge(s_out, 2 * g + 2)
                own(*[nc.vector.scalar_tensor_tensor(xres[:, 2 * g + i, :], ps[:, 2 + i, :], rstd[:, i:i + 1],
                                                     xres[:, 2 * g + i, :], ALU.mult, ALU.add) for i in range(2)])
                norm(lambda i: xres[:, 2 * g + i, :], lambda i: xm[:, i, :], 2, s_xm)
                assert steps[0] == DVE_STEPS, steps[0]


def ffn_block(nc, d, c, xres, xf_d, xfT_d, xs_d, ys_d, logits, sem, s_xf_d, s_zero_d):
    with ExitStack() as ctx:
        def sb(name, shape, dt=F32):
            return ctx.enter_context(nc.sbuf_tensor("C_" + name, shape, dt))

        ps = ctx.enter_context(nc.psum_tensor("psC", [P, 8, 512], F32))
        TH = 512
        REST = CAP - P
        w1 = [sb(f"w1_{q}", [P, KD, H]) for q in range(2)]
        w3 = [sb(f"w3_{q}", [P, KD, H]) for q in range(2)]
        w2 = [sb(f"w2_{q}", [P, MH, D]) for q in range(2)]
        xfT = sb("xfT", [P, KD, N])
        xf = sb("xf", [P, NT, D])
        gate_b = sb("gate_b", [P, E])
        hT = sb("hTs", [P, MH, TH])
        sl = [sb(f"sl{a}", [P, TH]) for a in range(2)]
        sc = sb("sc", [P, NT, E])
        red = sb("red", [P, NT])
        best = sb("best", [P, NT, 8])
        best_i = sb("best_i", [P, NT, 8], U32)
        pick = sb("pick", [P, NT, 2])
        onehot = sb("onehot", [P, 2, NT, E])
        prod = sb("prodR", [P, NT, E])
        gate = sb("gate", [P, 2, NT])
        queue = sb("queue", [P, NT, E])
        queueT = sb("queueT", [E, N])
        onehotT = sb("onehotT", [E, 2, N])
        junk = sb("junk", [P, N])
        own_w = sb("own_w", [P, 2, NT])
        part = sb("part", [P, 2, NT, 4])
        rank = sb("rank", [P, 2, NT])
        slot = sb("slot", [P, 2, NT])
        keep = sb("keep", [P, 2, NT])
        slot_i = sb("slot_i", [P, 2, NT], U32)
        xs = [sb(f"xs{q}", [P, D]) for q in range(2)]
        xsr = [sb(f"xsr{q}", [REST, D]) for q in range(2)]
        flat = hT[:].rearrange("p m t -> p (m t)")
        xsT = [flat[:, q * KD * CAP:(q + 1) * KD * CAP].rearrange("p (k s) -> p k s", k=KD) for q in range(2)]
        eT = [flat[:, (2 * KD + q * MH) * CAP:(2 * KD + (q + 1) * MH) * CAP].rearrange("p (m s) -> p m s", m=MH)
              for q in range(2)]
        yT = sb("yT", [P, KD, CAP])
        gathered = xfT[:].rearrange("p k t -> p (k t)").rearrange("p (a k n) -> p a k n", a=4, k=2)
        yo = [gathered[:, 2, q, :] for q in range(2)]
        yor = [gathered[0:REST, 3, q, :] for q in range(2)]

        s_in = sem("C_in")
        s_wA = [sem(f"C_w13_{q}") for q in range(2)]
        s_wB = [sem(f"C_w2_{q}") for q in range(2)]
        s_r = sem("C_router")
        s_ex = sem("C_exp")
        s_qT_mm = sem("C_queueT_mm")
        s_qT = sem("C_queueT")
        s_row_mm = sem("C_row_mm")
        s_row = sem("C_row")
        s_slot = sem("C_slot")
        s_xs_d = sem("C_xs_d")
        s_h_mm = sem("C_h_mm")
        s_sl = sem("C_sl")
        s_h = sem("C_h")
        s_y_mm = sem("C_y_mm")
        s_y = sem("C_y")
        s_xs = [sem(f"C_xs{q}") for q in range(2)]
        s_xT_mm = sem("E_xT_mm")
        s_xT = sem("E_xT")
        s_e_mm = sem("E_h_mm")
        s_esl = sem("E_sl")
        s_e = sem("E_h")
        s_yT_mm = sem("E_yT_mm")
        s_yT = sem("E_yT")
        s_yo_mm = sem("E_yo_mm")
        s_yo = sem("E_yo")
        s_ys = [sem(f"E_ys{q}") for q in range(2)]
        s_g = [sem(f"F_g{a}") for a in range(2)]
        s_f = sem("F_sum")
        s_res = sem("F_out")

        units = [(hf, s) for s in range(2) for hf in range(2)]
        FIRST_ROW = 10

        block = ctx.enter_context(nc.Block())

        def load_w13(eng, q, a, b):
            eng.dma_start(w1[q][:], a.rearrange("(k p) n -> p k n", p=P)).then_inc(s_wA[q], 16)
            eng.dma_start(w3[q][:], b.rearrange("(k p) n -> p k n", p=P)).then_inc(s_wA[q], 16)

        def load_w2(eng, q, a):
            eng.dma_start(w2[q][:], a.rearrange("(m p) n -> p m n", p=P)).then_inc(s_wB[q], 16)

        def load_xs(eng, q, e):
            rows = xs_d.rearrange("(e s) n -> e s n", e=E)[e]
            eng.dma_start(xs[q][:], rows[0:P, :]).then_inc(s_xs[q], 16)
            eng.dma_start(xsr[q][:], rows[P:CAP, :]).then_inc(s_xs[q], 16)

        @block.sync
        def _(sp):
            sp.wait_ge(s_xf_d, 32 * G + 1)
            sp.dma_start(xfT[:], xfT_d.rearrange("(k p) t -> p k t", p=P)).then_inc(s_in, 16)
            load_w13(sp, 0, d["sw1"][0], d["sw3"][0])
            load_w2(sp, 0, d["sw2"][0])
            sp.dma_start(gate_b[:], d["gate_b"].partition_broadcast(P)).then_inc(s_in, 16)
            sp.dma_start(xf[:], xf_d.rearrange("(t p) n -> p t n", p=P)).then_inc(s_in, 16)
            load_w13(sp, 1, d["sw1"][1], d["sw3"][1])
            load_w2(sp, 1, d["sw2"][1])
            for q in range(2):
                sp.wait_ge(s_h_mm, 16 * q + 16)
                load_w13(sp, q, d["ew1"][q], d["ew3"][q])
                sp.wait_ge(s_y_mm, 8 * q + 8)
                load_w2(sp, q, d["ew2"][q])
            sp.wait_ge(s_xs_d, 16 * 2 * NT)
            for q in range(2):
                load_xs(sp, q, q)
            with nc.sync.Fori(0, E // 2 - 1) as ep:
                for q in range(2):
                    sp.wait_ge(s_e_mm, MH * (2 * ep + q + 1))
                    load_w13(sp, q, d["ew1"][2 * ep + q + 2], d["ew3"][2 * ep + q + 2])
                    load_xs(sp, q, 2 * ep + q + 2)
                    sp.wait_ge(s_yT_mm, 2 * (2 * ep + q + 1))
                    load_w2(sp, q, d["ew2"][2 * ep + q + 2])
            for t in range(NT):
                sp.wait_ge(s_f, 2 * t + 2)
                sp.dma_start(d["out"][t * P:(t + 1) * P, :], xres[:, t, :]).then_inc(s_res, 16)
            sp.wait_ge(s_res, 16 * NT)

        @block.gpsimd
        def _(pool):
            pool.wait_ge(s_slot, 1)
            pool.wait_ge(s_in, 48)
            pool.wait_ge(s_zero_d, 32)
            for t in range(NT):
                for k in range(2):
                    nc.gpsimd.indirect_dma_start(
                        xs_d, bass.IndirectOffsetOnAxis(ap=slot_i[:, k, t:t + 1], axis=0), xf[:, t, :], None,
                        bounds_check=E * CAP - 1, oob_is_err=False).then_inc(s_xs_d, 16)
            for q in range(2):
                pool.wait_ge(s_ys[q], 32 * E // 2 + 1)
            for t in range(NT):
                if t >= 2:
                    pool.wait_ge(s_f, 2 * t - 2)
                for k in range(2):
                    nc.gpsimd.indirect_dma_start(
                        gathered[:, t % 2, k, :], None, ys_d, bass.IndirectOffsetOnAxis(ap=slot_i[:, k, t:t + 1], axis=0),
                        bounds_check=E * CAP, oob_is_err=False).then_inc(s_g[t % 2], 16)

        @block.tensor
        def _(pe):
            pe.wait_ge(s_in, 48)

            def queues(n):
                if n == 0:
                    pe.wait_ge(s_r, R_QUEUE)
                else:
                    pe.wait_ge(s_qT, 2 * n)
                for t in range(NT):
                    src = queue[:, t, :] if n == 0 else onehot[:, n - 1, t, :]
                    mm = nc.tensor.transpose(ps[0:E, t // 4, (t % 4) * P:(t % 4 + 1) * P], src, c["ident"][:])
                mm.then_inc(s_qT_mm, 1)

            def row(r):
                t, k = r // 2, r % 2
                if r == 0:
                    pe.wait_ge(s_qT, 6)
                else:
                    pe.wait_ge(s_row, r)
                for b in range(2):
                    mm = nc.tensor.matmul(ps[:, b, :], onehotT[:, k, t * P:(t + 1) * P], queueT[:, b * 512:(b + 1) * 512],
                                          start=True, stop=True)
                mm.then_inc(s_row_mm, 1)

            step = 0
            for hf, s in units:
                if hf == 0:
                    pe.wait_ge(s_wA[s], 32)
                for m in range(MH):
                    if FIRST_ROW - 4 <= step < FIRST_ROW - 1:
                        queues(step - FIRST_ROW + 4)
                    if FIRST_ROW <= step < FIRST_ROW + 2 * NT:
                        row(step - FIRST_ROW)
                    if step >= 2:
                        pe.wait_ge(s_h, step - 1)
                    for a, w in enumerate((w1, w3)):
                        for k in range(KD):
                            mm = nc.tensor.matmul(ps[:, 2 + 2 * (step % 2) + a, :], w[s][:, k, m * P:(m + 1) * P],
                                                  xfT[:, k, hf * TH:(hf + 1) * TH], start=(k == 0), stop=(k == KD - 1))
                    mm.then_inc(s_h_mm, 1)
                    step += 1
                if hf == 0:
                    pe.wait_ge(s_wB[s], 16)
                pe.wait_ge(s_h, step)
                for t in range(4):
                    n = 4 * (2 * s + hf) + t
                    if n >= 2:
                        pe.wait_ge(s_y, n - 1)
                    for m in range(MH):
                        mm = nc.tensor.matmul(ps[:, 6 + n % 2, :], hT[:, m, t * P:(t + 1) * P], w2[s][:, m, :],
                                              start=(m == 0), stop=(m == MH - 1))
                    mm.then_inc(s_y_mm, 1)

            def rows_in(q, e):
                pe.wait_ge(s_xs[q], 16 * (e - q) + 32)
                for k in range(KD):
                    o = (k % 2) * CAP
                    nc.tensor.transpose(ps[:, k // 2, o:o + P], xs[q][:, k * P:(k + 1) * P], c["ident"][:])
                    mm = nc.tensor.transpose(ps[:, k // 2, o + P:o + CAP], xsr[q][:, k * P:(k + 1) * P],
                                             c["ident"][0:REST, 0:REST])
                mm.then_inc(s_xT_mm, 1)

            def expert(q, e, last):
                pe.wait_ge(s_wA[q], 16 * (e - q) + 64)
                pe.wait_ge(s_xT, 2 * e + 2)
                for m in range(MH):
                    if m >= 3:
                        pe.wait_ge(s_e, MH * e + m - 2)
                    if m == 2:
                        pe.wait_ge(s_yo, 2 * e + 1)
                    for a, w in enumerate((w1, w3)):
                        for k in range(KD):
                            mm = nc.tensor.matmul(ps[:, 2 + m % 3, a * CAP:(a + 1) * CAP], w[q][:, k, m * P:(m + 1) * P],
                                                  xsT[q][:, k, :], start=(k == 0), stop=(k == KD - 1))
                    mm.then_inc(s_e_mm, 1)
                if not last:
                    rows_in(1 - q, e + 1)
                pe.wait_ge(s_wB[q], 8 * (e - q) + 32)
                pe.wait_ge(s_e, MH * e + MH)
                for dm in range(KD):
                    for m in range(MH):
                        mm = nc.tensor.matmul(ps[:, 5 + dm // 2, (dm % 2) * CAP:(dm % 2 + 1) * CAP],
                                              w2[q][:, m, dm * P:(dm + 1) * P], eT[q][:, m, :],
                                              start=(m == 0), stop=(m == MH - 1))
                    if dm % 2:
                        mm.then_inc(s_yT_mm, 1)
                for half in range(2):
                    pe.wait_ge(s_yT, 2 * e + half + 1)
                    for dm in range(2 * half, 2 * half + 2):
                        mm = nc.tensor.transpose(ps[:, 7, dm * P:(dm + 1) * P], yT[:, dm, 0:P], c["ident"][:])
                mm.then_inc(s_yo_mm, 1)
                for dm in range(KD):
                    mm = nc.tensor.transpose(ps[0:REST, 4, dm * P:(dm + 1) * P], yT[:, dm, P:CAP], c["ident"][:])
                mm.then_inc(s_yo_mm, 1)

            pe.wait_ge(s_row, 2 * NT)
            rows_in(0, 0)
            with nc.tensor.Fori(0, E // 2 - 1) as ep:
                expert(0, 2 * ep, False)
                expert(1, 2 * ep + 1, False)
            expert(0, E - 2, False)
            expert(1, E - 1, True)

        @block.scalar
        def _(act):
            act.wait_ge(s_r, R_SHIFT)
            nc.scalar.activation(sc[:], sc[:], ACT.Exp).then_inc(s_ex, 1)
            step = 0
            for hf, s in units:
                for m in range(MH):
                    if FIRST_ROW - 4 <= step < FIRST_ROW - 1:
                        n = step - FIRST_ROW + 4
                        act.wait_ge(s_qT_mm, n + 1)
                        for b in range(2):
                            dst = queueT[:, b * 512:(b + 1) * 512] if n == 0 else onehotT[:, n - 1, b * 512:(b + 1) * 512]
                            nc.scalar.copy(dst, ps[0:E, b, :]).then_inc(s_qT, 1)
                    act.wait_ge(s_h_mm, step + 1)
                    if step >= 2:
                        act.wait_ge(s_h, step - 1)
                    nc.scalar.activation(sl[step % 2][:], ps[:, 2 + 2 * (step % 2), :], ACT.Silu).then_inc(s_sl, 1)
                    step += 1

            def rows_in(q, e):
                act.wait_ge(s_xT_mm, e + 1)
                for b in range(2):
                    nc.scalar.copy(xsT[q][:, 2 * b:2 * b + 2, :].rearrange("p k s -> p (k s)"),
                                   ps[:, b, 0:2 * CAP]).then_inc(s_xT, 1)

            def expert(q, e, last):
                for m in range(MH):
                    act.wait_ge(s_e_mm, MH * e + m + 1)
                    if m >= 2:
                        act.wait_ge(s_e, MH * e + m - 1)
                    nc.scalar.activation(sl[m % 2][:, 0:CAP], ps[:, 2 + m % 3, 0:CAP], ACT.Silu).then_inc(s_esl, 1)
                if not last:
                    rows_in(1 - q, e + 1)
                act.wait_ge(s_ys[q], 16 * (e - q) + 1)
                act.wait_ge(s_yo_mm, 2 * e + 1)
                nc.scalar.copy(yo[q], ps[:, 7, :]).then_inc(s_yo, 1)
                act.wait_ge(s_yo_mm, 2 * e + 2)
                nc.scalar.copy(yor[q], ps[0:REST, 4, :]).then_inc(s_yo, 1)
                rows = ys_d[0:E * CAP, :].rearrange("(e s) n -> e s n", e=E)[e]
                act.wait_ge(s_yo, 2 * e + 3)
                act.dma_start(rows[0:P, :], yo[q]).then_inc(s_ys[q], 16)
                act.dma_start(rows[P:CAP, :], yor[q]).then_inc(s_ys[q], 16)

            act.sem_inc(s_yo, 1)
            for q in range(2):
                act.sem_inc(s_ys[q], 1)
            rows_in(0, 0)
            with nc.scalar.Fori(0, E // 2 - 1) as ep:
                expert(0, 2 * ep, False)
                expert(1, 2 * ep + 1, False)
            expert(0, E - 2, False)
            expert(1, E - 1, True)

        @block.vector
        def _(dve):
            done = [0]

            def own(*instructions):
                for ins in instructions:
                    ins.then_inc(s_r, 1)
                done[0] += len(instructions)
                dve.wait_ge(s_r, done[0])

            wide = [P, NT, E]
            own(nc.vector.tensor_reduce(red[:], logits[:], AX.X, ALU.max))
            own(nc.vector.tensor_tensor(sc[:], logits[:], red[:].unsqueeze(2).to_broadcast(wide), ALU.subtract))
            assert done[0] == R_SHIFT
            dve.wait_ge(s_ex, 1)
            own(nc.vector.tensor_reduce(red[:], sc[:], AX.X, ALU.add))
            own(nc.vector.reciprocal(red[:], red[:]))
            own(nc.vector.tensor_tensor(sc[:], sc[:], red[:].unsqueeze(2).to_broadcast(wide), ALU.mult))
            dve.wait_ge(s_in, 48)
            own(nc.vector.tensor_tensor(sc[:], sc[:], gate_b[:].unsqueeze(1).to_broadcast(wide), ALU.add))
            own(*[nc.vector.max(best[:, t, :], sc[:, t, :]) for t in range(NT)])
            own(*[nc.vector.max_index(best_i[:, t, :], best[:, t, :], sc[:, t, :]) for t in range(NT)])
            own(nc.vector.tensor_copy(pick[:], best_i[:, :, 0:2]))
            for k in range(2):
                own(nc.vector.tensor_tensor(onehot[:, k], pick[:, :, k:k + 1].to_broadcast(wide),
                                            c["expert_index"][:].unsqueeze(1).to_broadcast(wide), ALU.is_equal))
                own(nc.vector.tensor_tensor(prod[:], onehot[:, k], logits[:], ALU.mult))
                own(nc.vector.tensor_reduce(gate[:, k, :], prod[:], AX.X, ALU.add))
            own(nc.vector.tensor_tensor(queue[:], onehot[:, 0], onehot[:, 1], ALU.add))
            own(nc.vector.tensor_tensor(prod[:], queue[:], logits[:], ALU.mult))
            own(nc.vector.tensor_scalar(queue[:], queue[:], -NOT_MINE, NOT_MINE, ALU.mult, ALU.add))
            own(nc.vector.tensor_tensor(queue[:], queue[:], prod[:], ALU.add))
            assert done[0] == R_QUEUE, done[0]
            own(nc.vector.memset(part[:], 0.0))

            def rank_row(r):
                t, k = r // 2, r % 2
                w = own_w[:, k, t:t + 1]
                a, b = t * P, (t + 1) * P
                row = ps[:, 0:2, :].rearrange("p b n -> p (b n)")
                dve.wait_ge(s_row_mm, r + 1)
                own(nc.vector.scalar_tensor_tensor(junk[:, a:b], row[:, a:b], 1.0, c["ident"][:], ALU.mult, ALU.mult,
                                                   accum_out=w))
                ins = []
                if t > 0:
                    ins.append(nc.vector.tensor_scalar(junk[:, 0:a], row[:, 0:a], w, None, ALU.is_ge, ALU.add,
                                                       accum_out=part[:, k, t, 0:1]))
                if t < NT - 1:
                    ins.append(nc.vector.tensor_scalar(junk[:, b:N], row[:, b:N], w, None, ALU.is_gt, ALU.add,
                                                       accum_out=part[:, k, t, 1:2]))
                ins.append(nc.vector.scalar_tensor_tensor(junk[:, a:b], row[:, a:b], w, c["lower"][:], ALU.is_ge,
                                                          ALU.mult, accum_out=part[:, k, t, 2:3]))
                own(*ins)
                own(nc.vector.scalar_tensor_tensor(junk[:, a:b], row[:, a:b], w, c["upper"][:], ALU.is_gt,
                                                   ALU.mult, accum_out=part[:, k, t, 3:4]))
                nc.vector.tensor_copy(own_w[:, k, t:t + 1], own_w[:, k, t:t + 1]).then_inc(s_row, 1)

            def slots():
                dve.wait_ge(s_row, 2 * NT)
                own(nc.vector.tensor_reduce(rank[:], part[:], AX.X, ALU.add))
                own(nc.vector.tensor_scalar(keep[:], rank[:], float(CAP), None, ALU.is_lt))
                own(nc.vector.scalar_tensor_tensor(slot[:], pick[:].rearrange("p t k -> p k t"), float(CAP), rank[:],
                                                   ALU.mult, ALU.add))
                own(nc.vector.scalar_tensor_tensor(slot[:], slot[:], float(-E * CAP), keep[:], ALU.add, ALU.mult))
                own(nc.vector.tensor_scalar(slot[:], slot[:], float(E * CAP), None, ALU.add))
                nc.vector.tensor_copy(slot_i[:], slot[:]).then_inc(s_slot, 1)

            step = 0
            for hf, s in units:
                for m in range(MH):
                    if FIRST_ROW <= step < FIRST_ROW + 2 * NT:
                        rank_row(step - FIRST_ROW)
                    if step == FIRST_ROW + 2 * NT:
                        slots()
                    dve.wait_ge(s_sl, step + 1)
                    nc.vector.tensor_tensor(hT[:, m, :], sl[step % 2][:], ps[:, 3 + 2 * (step % 2), :],
                                            ALU.mult).then_inc(s_h, 1)
                    step += 1
                for t in range(4):
                    n = 4 * (2 * s + hf) + t
                    dve.wait_ge(s_y_mm, n + 1)
                    if n >= 8:
                        dve.wait_ge(s_y, n - 7)
                    nc.vector.scalar_tensor_tensor(xres[:, 4 * hf + t, :], ps[:, 6 + n % 2, :], 0.5,
                                                   xres[:, 4 * hf + t, :], ALU.mult, ALU.add).then_inc(s_y, 1)

            def expert(q, e):
                for m in range(MH):
                    dve.wait_ge(s_esl, MH * e + m + 1)
                    nc.vector.tensor_tensor(eT[q][:, m, :], sl[m % 2][:, 0:CAP], ps[:, 2 + m % 3, CAP:2 * CAP],
                                            ALU.mult).then_inc(s_e, 1)
                for half in range(2):
                    dve.wait_ge(s_yT_mm, 2 * e + half + 1)
                    nc.vector.tensor_copy(yT[:, 2 * half:2 * half + 2, :].rearrange("p k s -> p (k s)"),
                                          ps[:, 5 + half, 0:2 * CAP]).then_inc(s_yT, 1)

            with nc.vector.Fori(0, E // 2) as ep:
                for q in range(2):
                    expert(q, 2 * ep + q)
            dve.wait_ge(s_y, 16)
            for t in range(NT):
                dve.wait_ge(s_g[t % 2], 32 * (t // 2 + 1))
                for k in range(2):
                    if k:
                        dve.wait_ge(s_f, 2 * t + 1)
                    nc.vector.scalar_tensor_tensor(xres[:, t, :], gathered[:, t % 2, k, :], gate[:, k, t:t + 1], xres[:, t, :],
                                                   ALU.mult, ALU.add).then_inc(s_f, 1)


R_SHIFT = 2
R_QUEUE = 33


def perceiver_kernel(nc, d):
    with ExitStack() as ctx:
        def sb(name, shape, dt=F32):
            return ctx.enter_context(nc.sbuf_tensor(name, shape, dt))

        def sem(name):
            return ctx.enter_context(nc.semaphore(name))

        xf_d = nc.dram_tensor("xf_scratch", (N, D), F32, kind="Internal").ap()
        xfT_d = nc.dram_tensor("xfT_scratch", (D, N), F32, kind="Internal").ap()
        xs_d = nc.dram_tensor("queue_rows", (E * CAP, D), F32, kind="Internal").ap()
        ys_d = nc.dram_tensor("expert_rows", (E * CAP + 1, D), F32, kind="Internal").ap()
        xres = sb("xres", [P, NT, D])
        logits = sb("logits", [P, NT, E])
        zeros = sb("zeros", [P, D])
        c = constants(nc, sb, sem, d)
        s_const = sem("constants")
        s_x = sem("x_in")
        s_z = sem("zeros")
        s_xf_d = sem("xf_to_dram")
        s_zero_d = sem("zero_rows")

        with nc.Block() as block:
            n_const = [0]

            @block.gpsimd
            def _(pool):
                n_const[0] = build_constants(nc, c, s_const)
                pool.memset(zeros[:], 0.0).then_inc(s_z, 1)

        def zero_rows(sp):
            sp.wait_ge(s_z, 1)
            sp.dma_start(xs_d.rearrange("(a p) n -> p a n", p=P),
                         zeros[:].unsqueeze(1).to_broadcast([P, E * CAP // P, D])).then_inc(s_zero_d, 16)
            sp.dma_start(ys_d[E * CAP:E * CAP + 1, :], zeros[0:1, :]).then_inc(s_zero_d, 16)

        attention_block(nc, d, c, s_const, n_const[0], xres, sem, s_x)
        mamba_block(nc, d, c, s_const, n_const[0], xres, xf_d, xfT_d, logits, sem, s_xf_d, zero_rows)
        ffn_block(nc, d, c, xres, xf_d, xfT_d, xs_d, ys_d, logits, sem, s_xf_d, s_zero_d)


def kernel(**inputs):
    import numpy as np
    import concourse.bacc as bacc
    from concourse.bass_utils import run_bass_kernel_spmd

    a = {k: np.asarray(v) for k, v in inputs.items()}

    def by_channel(v):
        return v.reshape(MC, P).T

    pair = a["ctx_1024"].reshape(NB // 2, 2, KS, P, KD, P)
    w_x = np.zeros((C, 96), np.float32)
    for n in range(3):
        w_x[:, 32 * n:32 * n + NS] = a["L0_attn_W_xproj"][:, NS * n:NS * (n + 1)]
    chan = np.stack([by_channel(a["L0_attn_conv_w"][:, j]) for j in range(4)] + [
        by_channel(a["L0_attn_conv_b"]), by_channel(np.repeat(a["L0_attn_A_log"], C // 16)),
        by_channel(np.repeat(a["L0_attn_D_skip"], C // 16)), by_channel(a["L0_attn_ln_g"]),
        by_channel(a["L0_attn_ln_b"])], axis=2)
    host = {
        "x": a["x"].reshape(N, D),
        "ctx": pair.transpose(0, 1, 3, 2, 4, 5).reshape(NB // 2, 2, P, KS, D),
        "ctxT": pair.transpose(0, 1, 5, 4, 2, 3).reshape(NB // 2, 2, P, KD, SK),
        "wq1T": a["L0_xattn_Wq1"].T, "wk1T": a["L0_xattn_Wk1"].T, "wv1": a["L0_xattn_Wv1"],
        "wq2T": a["L0_xattn_Wq2"].T, "wk2T": a["L0_xattn_Wk2"].T, "wv2": a["L0_xattn_Wv2"],
        "fc1_w": a["L0_xattn_fc1_w"], "fc1_b": a["L0_xattn_fc1_b"].reshape(KD, P).T,
        "fc2_w": a["L0_xattn_fc2_w"], "fc2_b": a["L0_xattn_fc2_b"].reshape(1, D),
        "ln": np.stack([a[f"L0_xattn_ln{n}_{k}"] for n in (1, 2, 3) for k in "gb"]),
        "w_in": a["L0_attn_W_in"], "w_x": w_x,
        "w_dt": np.concatenate([a["L0_attn_W_dt"], a["L0_attn_b_dt"].reshape(1, C)], axis=0),
        "chan": chan, "w_out": a["L0_attn_W_out"],
        "gate_w": a["L0_ffn_gate_w"], "gate_b": a["L0_ffn_gate_b"],
        "ew1": a["L0_ffn_ew1"], "ew3": a["L0_ffn_ew3"], "ew2": a["L0_ffn_ew2"],
        "sw1": a["L0_ffn_sw1"], "sw3": a["L0_ffn_sw3"], "sw2": a["L0_ffn_sw2"],
    }
    nc = bacc.Bacc("TRN2", target_bir_lowering=False, num_devices=1)
    arrays, d = {}, {}
    for name, v in host.items():
        arrays["in_" + name] = np.ascontiguousarray(v)
        d[name] = nc.dram_tensor("in_" + name, v.shape, mybir.dt.from_np(v.dtype), kind="ExternalInput").ap()
    out = nc.dram_tensor("out_0", (N, D), F32, kind="ExternalOutput").ap()
    d["out"] = out
    perceiver_kernel(nc, d)
    r = run_bass_kernel_spmd(nc, [arrays], core_ids=[0])
    return r.results[0]["out_0"].reshape(NB, L, D)
```

```python
from contextlib import ExitStack

import concourse.bass as bass
from concourse import mybir

F32 = mybir.dt.float32
U32 = mybir.dt.uint32
ALU = mybir.AluOpType
ACT = mybir.ActivationFunctionType
AX = mybir.AxisListType

P = 128
D = 512
KD = D // P
NB = 16
L = 64
N = NB * L
NT = N // P
TG = 256
G = N // TG
SK = 512
KS = SK // P
C = 1024
MC = C // P
NS = 16
Q = 8
E = 16
H = 1024
MH = H // P
CAP = 160
SCALE = float(1.0 / (32.0 ** 0.5))
EPS = 1e-5
BIG = -1.0e30
NOT_MINE = -3.0e38


def constants(nc, sb, sem, d):
    c = {}
    c["ident"] = sb("ident", [P, P])
    c["ones"] = sb("ones", [P, P])
    c["ones_over_c"] = sb("ones_over_c", [P, P])
    c["causal"] = sb("causal", [P, P])
    c["same_batch"] = sb("same_batch", [P, P])
    c["first_row"] = sb("first_row", [P, P])
    c["key_in_batch"] = sb("key_in_batch", [P, P])
    c["key_index"] = sb("key_index", [P, SK])
    c["expert_index"] = sb("expert_index", [P, E])
    c["own_chunk"] = sb("own_chunk", [P, 16, NS])
    c["next_chunk"] = sb("next_chunk", [P, Q, Q])
    c["in_sequence"] = sb("in_sequence", [P, TG])
    c["rep_state"] = sb("rep_state", [NS, Q, NS])
    c["lower"] = sb("lower", [P, P])
    c["upper"] = sb("upper", [P, P])
    c["minus_half"] = sb("minus_half", [P, 2])
    c["eps"] = sb("eps", [P, 2])
    return c


def build_constants(nc, c, s_const):
    pool = nc.gpsimd
    n = [0]

    def put(ins, wait=False):
        ins.then_inc(s_const, 1)
        n[0] += 1
        if wait:
            pool.wait_ge(s_const, n[0])

    def select(t, out, pattern, base, mult, op, fill):
        put(pool.affine_select(out=out, in_=out, compare_op=op, fill=fill, base=base,
                               pattern=pattern, channel_multiplier=mult), wait=True)

    for name in ("ones", "same_batch", "causal", "first_row", "own_chunk", "next_chunk", "rep_state",
                 "in_sequence", "lower", "upper"):
        put(pool.memset(c[name][:], 1.0))
    put(pool.memset(c["ident"][:], 0.0))
    put(pool.memset(c["ones_over_c"][:], 1.0 / C))
    put(pool.memset(c["minus_half"][:], -0.5))
    put(pool.memset(c["eps"][:], EPS))
    for name, pat in (("key_in_batch", [[0, 2], [1, L]]), ("key_index", [[1, SK]]), ("expert_index", [[1, E]])):
        put(pool.iota(c[name][:], pattern=pat, base=0, channel_multiplier=0,
                      allow_small_or_imprecise_dtypes=True))
    pool.wait_ge(s_const, n[0])
    select(c, c["ident"][:], [[-1, P]], 0, 1, ALU.not_equal, 1.0)
    sbm = c["same_batch"][:].rearrange("p (b j) -> p b j", b=2)
    select(c, sbm, [[-L, 2], [0, L]], 0, 1, ALU.is_ge, 0.0)
    select(c, sbm, [[L, 2], [0, L]], L - 1, -1, ALU.is_ge, 0.0)
    cm = c["causal"][:]
    select(c, cm, [[1, P]], 0, -1, ALU.is_gt, 0.0)
    put(pool.memset(c["causal"][L:P, 0:L], 1.0), wait=True)
    fr = c["first_row"][:].rearrange("p (b j) -> p b j", b=2)
    select(c, fr, [[-L, 2], [0, L]], 0, 1, ALU.is_equal, 0.0)
    oc = c["own_chunk"][:]
    select(c, oc, [[-Q, 16], [0, NS]], 0, 1, ALU.is_ge, 0.0)
    select(c, oc, [[Q, 16], [0, NS]], Q - 1, -1, ALU.is_ge, 0.0)
    nx = c["next_chunk"][:]
    select(c, nx, [[-NS, Q], [0, Q]], NS, 1, ALU.is_ge, 0.0)
    select(c, nx, [[NS, Q], [0, Q]], -1, -1, ALU.is_ge, 0.0)
    select(c, c["rep_state"][:], [[0, Q], [-1, NS]], 0, 1, ALU.is_equal, 0.0)
    isq = c["in_sequence"][:].rearrange("p (a t) -> p a t", t=L)
    put(pool.memset(isq[:, :, 0:1], 0.0))
    select(c, c["lower"][:], [[-1, P]], 0, 1, ALU.is_gt, 0.0)
    select(c, c["upper"][:], [[1, P]], 0, -1, ALU.is_gt, 0.0)
    pool.wait_ge(s_const, n[0])
    put(pool.memset(c["lower"][0:1, 0:1], 0.0))
    return n[0]


def attention_block(nc, d, c, s_const, n_const, xres, s_x):
    sems = []
    with ExitStack() as ctx:
        def sb(name, shape, dt=F32):
            return ctx.enter_context(nc.sbuf_tensor("A_" + name, shape, dt))

        def sem(name):
            sems.append(nc.alloc_semaphore(name))
            return sems[-1]

        ps = ctx.enter_context(nc.psum_tensor("psA", [P, 8, 512], F32))
        B_TR, B_V, B_E, B_LEN = 0, 1, 2, 3
        B_E2, B_C, B_Z, B_LEN2 = 4, 5, 6, 7
        wqk = [sb(f"wqk{a}", [P, KD, D]) for a in range(2)]
        wv1 = sb("wv1", [P, KD, D])
        wv2 = sb("wv2", [P, KD, D])
        fc1 = sb("fc1", [P, KD, D])
        fc2 = sb("fc2", [P, KD, D])
        fc1_b = sb("fc1_b", [P, KD])
        fc2_b = sb("fc2_b", [1, D])
        ln = sb("ln_gb", [P, 6, D])
        ctx_kd = [sb(f"ctx_kd{q}", [P, 2, KS, D]) for q in range(2)]
        ctx_dk = [sb(f"ctx_dk{q}", [P, 2, KD, SK]) for q in range(2)]
        wqT, wkT = ctx_dk[1][:, 0], ctx_dk[1][:, 1]
        xn = sb("xn", [P, D])
        tT = sb("tT", [P, KD, P])
        q1T = sb("q1T", [P, KD, P])
        v1 = sb("v1", [P, D])
        msk1 = sb("msk1", [P, P])
        pr1 = sb("pr1", [P, P])
        pr1T = sb("pr1T", [P, P])
        x1 = [sb(f"x1_{q}", [P, D]) for q in range(2)]
        q2T = [sb(f"q2T_{q}", [P, KD, P]) for q in range(2)]
        msk2 = sb("msk2", [P, SK])
        pr2 = sb("pr2", [P, SK])
        pr2T = sb("pr2T", [P, KS, P])
        cT = sb("cT", [P, KD, P])
        x2 = sb("x2", [P, D])
        uT = sb("uT", [P, KD, P])
        hT = sb("hT", [P, KD, P])
        x3 = sb("x3", [P, D])
        bst = [sb(f"bst{n}", [P, 6]) for n in range(4)]
        mv = [sb(f"mv{n}", [P, 2]) for n in range(4)]
        ve = [sb(f"ve{n}", [P, 1]) for n in range(4)]
        rstd = [sb(f"rstd{n}", [P, 1]) for n in range(4)]
        cnt = [sb(f"cnt{n}", [P, 1]) for n in range(2)]
        top = [sb(f"top{n}", [P, 1]) for n in range(2)]
        nmx = [sb(f"nmx{n}", [P, 1]) for n in range(2)]
        rsum = [sb(f"rsum{n}", [P, 1]) for n in range(2)]
        rinv = [sb(f"rinv{n}", [P, 1]) for n in range(2)]

        s_w = {k: sem("A_" + k) for k in ("w0", "w1", "rest", "ln")}
        s_dk = [sem(f"A_ctx_dk{q}") for q in range(2)]
        s_kd = [sem(f"A_ctx_kd{q}") for q in range(2)]
        s_wqk_mm = sem("A_wqk_mm")
        s_wqk = sem("A_wqk")
        s_var = [sem(f"A_var{n}") for n in range(4)]
        s_ve = [sem(f"A_ve{n}") for n in range(4)]
        s_rstd = [sem(f"A_rstd{n}") for n in range(4)]
        s_xn = sem("A_xn")
        s_tr = sem("A_tr")
        s_tT = sem("A_tT")
        s_q_mm = sem("A_q_mm")
        s_q = sem("A_q")
        s_v_mm = sem("A_v_mm")
        s_v = sem("A_v")
        s_e = [sem(f"A_e{n}") for n in range(2)]
        s_cnt = [sem(f"A_cnt{n}") for n in range(2)]
        s_len = [sem(f"A_len{n}") for n in range(2)]
        s_bias = [sem(f"A_bias{n}") for n in range(2)]
        s_exp = [sem(f"A_exp{n}") for n in range(2)]
        s_pT_mm = [sem(f"A_pT_mm{n}") for n in range(2)]
        s_pT = [sem(f"A_pT{n}") for n in range(2)]
        s_z1 = sem("A_z1")
        s_x1 = sem("A_x1")
        s_c_mm = sem("A_c_mm")
        s_c = sem("A_c")
        s_z2 = sem("A_z2")
        s_x2 = sem("A_x2")
        s_tr2 = sem("A_tr2")
        s_uT = sem("A_uT")
        s_f1_mm = sem("A_f1_mm")
        s_h = sem("A_h")
        s_z3 = sem("A_z3")
        s_done = sem("A_done")
        s_own0, s_own1, s_own2, s_own3 = (sem(f"A_own{n}") for n in range(4))
        s_gain1 = sem("A_gain1")
        s_gain2 = sem("A_gain2")
        s_y3 = sem("A_y3")
        s_ownf = sem("A_ownf")
        s_ownb = sem("A_ownb")
        s_passed = sem("A_waits_passed")
        block = ctx.enter_context(nc.Block())

        def stand_alone(eng):
            eng.sem_inc(s_passed, 1)

        def steps(engine, prologue, step):
            prologue()
            with engine.Fori(0, NT // 2 - 1) as g:
                step(2 * g, 0, True)
                step(2 * g + 1, 1, True)
            step(NT - 2, 0, True)
            step(NT - 1, 1, False)

        def w_view(w):
            return w.rearrange("(k p) n -> p k n", p=P)

        @block.sync
        def _(sp):
            sp.dma_start(wqT, w_view(d["wq1T"])).then_inc(s_w["w0"], 16)
            sp.dma_start(wkT, w_view(d["wk1T"])).then_inc(s_w["w0"], 16)
            sp.dma_start(xres[:], d["x"].rearrange("(t p) n -> p t n", p=P)).then_inc(s_x, 16)
            sp.dma_start(wv1[:], w_view(d["wv1"])).then_inc(s_w["rest"], 16)
            sp.wait_ge(s_wqk_mm, KD)
            sp.dma_start(wqT, w_view(d["wq2T"])).then_inc(s_w["w1"], 16)
            sp.dma_start(wkT, w_view(d["wk2T"])).then_inc(s_w["w1"], 16)
            for n in range(6):
                sp.dma_start(ln[:, n, :], d["ln"][n].partition_broadcast(P)).then_inc(s_w["ln"], 16)

            def load_dk(t, q):
                for h in range(2):
                    sp.dma_start(ctx_dk[q][:, h], d["ctxT"][t, h]).then_inc(s_dk[q], 16)

            def load_kd(t, q):
                for h in range(2):
                    sp.dma_start(ctx_kd[q][:, h], d["ctx"][t, h]).then_inc(s_kd[q], 16)

            load_dk(0, 0)
            load_kd(0, 0)
            sp.dma_start(wv2[:], w_view(d["wv2"])).then_inc(s_w["rest"], 16)
            sp.dma_start(fc1[:], w_view(d["fc1_w"])).then_inc(s_w["rest"], 16)
            sp.dma_start(fc2[:], w_view(d["fc2_w"])).then_inc(s_w["rest"], 16)
            sp.dma_start(fc1_b[:], d["fc1_b"]).then_inc(s_w["rest"], 16)
            sp.dma_start(fc2_b[:], d["fc2_b"]).then_inc(s_w["rest"], 16)
            sp.wait_ge(s_wqk_mm, 2 * KD)
            load_dk(1, 1)
            load_kd(1, 1)
            with nc.sync.Fori(0, NT // 2 - 1) as g:
                for q in range(2):
                    sp.wait_ge(s_e[1], 2 * g + q + 1)
                    load_dk(2 * g + q + 2, q)
                    sp.wait_ge(s_c_mm, 2 * g + q + 1)
                    load_kd(2 * g + q + 2, q)

        @block.gpsimd
        def _(pool):
            def rsqrt(n, t):
                pool.wait_ge(s_var[n], t + 1)
                nc.gpsimd.tensor_tensor(ve[n][:], mv[n][:, 1:2], c["eps"][:, 0:1], ALU.add).then_inc(s_ve[n], 1)
                pool.wait_ge(s_ve[n], t + 1)
                nc.gpsimd.tensor_tensor(rstd[n][:], ve[n][:], c["minus_half"][:, 0:1], ALU.pow).then_inc(s_rstd[n], 1)

            def prologue():
                rsqrt(0, 0)
                rsqrt(1, 0)
                rsqrt(0, 1)

            def step(t, q, more):
                rsqrt(2, t)
                if more:
                    rsqrt(1, t + 1)
                    rsqrt(0, t + 2)
                rsqrt(3, t)

            def last(t, q, more):
                rsqrt(2, t)
                if more:
                    rsqrt(1, t + 1)
                rsqrt(3, t)

            prologue()
            with nc.gpsimd.Fori(0, NT // 2 - 1) as g:
                step(2 * g, 0, True)
                step(2 * g + 1, 1, True)
            last(NT - 2, 0, True)
            last(NT - 1, 1, False)

        @block.tensor
        def _(pe):
            pe.wait_ge(s_const, n_const)
            for a in range(2):
                pe.wait_ge(s_w[f"w{a}"], 32)
                for m in range(KD):
                    if a:
                        pe.wait_ge(s_wqk, m + 1)
                    for k in range(KD):
                        mm = nc.tensor.matmul(ps[:, m, :], wqT[:, k, m * P:(m + 1) * P], wkT[:, k, :],
                                              start=(k == 0), stop=(k == KD - 1))
                    mm.then_inc(s_wqk_mm, 1)
            pe.wait_ge(s_w["rest"], 16 * 6)
            pe.wait_ge(s_wqk, 2 * KD)

            def transposes(bank, src, s):
                for k in range(KD):
                    mm = nc.tensor.transpose(ps[:, bank, k * P:(k + 1) * P], src[:, k * P:(k + 1) * P], c["ident"][:])
                mm.then_inc(s, 1)

            def widths_out(bank, w, src, s):
                for m in range(KD):
                    for k in range(KD):
                        mm = nc.tensor.matmul(ps[:, bank, m * P:(m + 1) * P], w[:, k, m * P:(m + 1) * P], src[:, k, :],
                                              start=(k == 0), stop=(k == KD - 1))
                mm.then_inc(s, 1)

            def xn_transposed(t):
                pe.wait_ge(s_xn, t + 1)
                transposes(B_TR, xn, s_tr)

            def queries_values(t):
                pe.wait_ge(s_tT, 2 * t + 1)
                widths_out(B_TR, wqk[0], tT, s_q_mm)
                for k in range(KD):
                    mm = nc.tensor.matmul(ps[:, B_V, :], tT[:, k, :], wv1[:, k, :], start=(k == 0), stop=(k == KD - 1))
                mm.then_inc(s_v_mm, 1)

            def energies(t):
                pe.wait_ge(s_q, 2 * t + 1)
                for k in range(KD):
                    mm = nc.tensor.matmul(ps[:, B_E, 0:P], q1T[:, k, :], tT[:, k, :], start=(k == 0), stop=(k == KD - 1))
                mm.then_inc(s_e[0], 1)

            def keys_that_count(n, bank, t):
                pe.wait_ge(s_cnt[n], t + 1)
                nc.tensor.matmul(ps[:, bank, 0:1], c["first_row"][:], cnt[n][:], start=True, stop=True).then_inc(s_len[n], 1)

            def probabilities_transposed(t):
                pe.wait_ge(s_exp[0], t + 1)
                nc.tensor.transpose(ps[:, B_E, 0:P], pr1[:], c["ident"][:]).then_inc(s_pT_mm[0], 1)

            def attend(t):
                pe.wait_ge(s_pT[0], t + 1)
                pe.wait_ge(s_v, t + 1)
                nc.tensor.matmul(ps[:, B_V, :], pr1T[:], v1[:], start=True, stop=True).then_inc(s_z1, 1)

            def x1_transposed(t, q):
                pe.wait_ge(s_x1, t + 1)
                transposes(B_TR, x1[q], s_tr)

            def cross_queries(t):
                pe.wait_ge(s_tT, 2 * t + 2)
                widths_out(B_TR, wqk[1], tT, s_q_mm)

            def cross_energies(t, q):
                pe.wait_ge(s_q, 2 * t + 2)
                pe.wait_ge(s_dk[q], 16 * (t - q) + 32)
                for k in range(KD):
                    for h in range(2):
                        mm = nc.tensor.matmul(ps[h * L:(h + 1) * L, B_E2, :], q2T[q][:, k, h * L:(h + 1) * L],
                                              ctx_dk[q][:, h, k, :], start=(k == 0), stop=(k == KD - 1))
                mm.then_inc(s_e[1], 1)

            def cross_probabilities_transposed(t):
                pe.wait_ge(s_exp[1], t + 1)
                for b in range(KS):
                    mm = nc.tensor.transpose(ps[:, B_E2, b * P:(b + 1) * P], pr2[:, b * P:(b + 1) * P], c["ident"][:])
                mm.then_inc(s_pT_mm[1], 1)

            def contexts(t, q, h):
                if h == 0:
                    pe.wait_ge(s_pT[1], t + 1)
                    pe.wait_ge(s_kd[q], 16 * (t - q) + 32)
                for m in range(KD):
                    for b in range(KS):
                        o = m * P + h * L
                        mm = nc.tensor.matmul(ps[:, B_C, o:o + L], ctx_kd[q][:, h, b, m * P:(m + 1) * P],
                                              pr2T[:, b, h * L:(h + 1) * L], start=(b == 0), stop=(b == KS - 1))
                if h == 1:
                    mm.then_inc(s_c_mm, 1)

            def cross_values(t):
                pe.wait_ge(s_c, t + 1)
                for k in range(KD):
                    mm = nc.tensor.matmul(ps[:, B_Z, :], cT[:, k, :], wv2[:, k, :], start=(k == 0), stop=(k == KD - 1))
                mm.then_inc(s_z2, 1)

            def x2_transposed(t):
                pe.wait_ge(s_x2, t + 1)
                transposes(B_C, x2, s_tr2)

            def hidden(t):
                pe.wait_ge(s_uT, t + 1)
                widths_out(B_C, fc1, uT, s_f1_mm)

            def feed_forward(t):
                pe.wait_ge(s_h, 4 * t + 4)
                for k in range(KD):
                    nc.tensor.matmul(ps[:, B_Z, :], hT[:, k, :], fc2[:, k, :], start=(k == 0), stop=False)
                nc.tensor.matmul(ps[:, B_Z, :], c["ones"][0:1, :], fc2_b[0:1, :], start=False,
                                 stop=True).then_inc(s_z3, 1)

            def prologue():
                xn_transposed(0)
                queries_values(0)
                energies(0)
                keys_that_count(0, B_LEN, 0)
                probabilities_transposed(0)
                attend(0)
                x1_transposed(0, 0)
                cross_queries(0)

            def step(t, q, more):
                cross_energies(t, q)
                if more:
                    xn_transposed(t + 1)
                keys_that_count(1, B_LEN2, t)
                if more:
                    queries_values(t + 1)
                cross_probabilities_transposed(t)
                if more:
                    energies(t + 1)
                contexts(t, q, 0)
                if more:
                    keys_that_count(0, B_LEN, t + 1)
                contexts(t, q, 1)
                if more:
                    probabilities_transposed(t + 1)
                cross_values(t)
                if more:
                    attend(t + 1)
                x2_transposed(t)
                if more:
                    x1_transposed(t + 1, 1 - q)
                hidden(t)
                if more:
                    cross_queries(t + 1)
                feed_forward(t)

            steps(nc.tensor, prologue, step)

        @block.scalar
        def _(act):
            for a in range(2):
                for m in range(KD):
                    act.wait_ge(s_wqk_mm, KD * a + m + 1)
                    nc.scalar.copy(wqk[a][:, m, :], ps[:, m, :]).then_inc(s_wqk, 1)
            act.wait_ge(s_w["rest"], 16 * 6)

            def flat(t):
                return t[:].rearrange("p k t -> p (k t)")

            def copy_of(s_ready, n, dst, bank, s_out):
                act.wait_ge(s_ready, n)
                nc.scalar.copy(flat(dst), ps[:, bank, :]).then_inc(s_out, 1)

            def softmax(n, t):
                act.wait_ge(s_bias[n], t + 1)
                nc.scalar.activation((pr1, pr2)[n][:], (msk1, msk2)[n][:], ACT.Exp, bias=nmx[n][:], scale=SCALE,
                                     accum_out=rsum[n][:]).then_inc(s_exp[n], 1)

            def probabilities(t):
                act.wait_ge(s_pT_mm[0], t + 1)
                nc.scalar.copy(pr1T[:], ps[:, B_E, 0:P]).then_inc(s_pT[0], 1)

            def relu(t):
                act.wait_ge(s_f1_mm, t + 1)
                for m in range(KD):
                    nc.scalar.activation(hT[:, m, :], ps[:, B_C, m * P:(m + 1) * P], ACT.Relu,
                                         bias=fc1_b[:, m:m + 1]).then_inc(s_h, 1)

            def prologue():
                copy_of(s_tr, 1, tT, B_TR, s_tT)
                copy_of(s_q_mm, 1, q1T, B_TR, s_q)
                softmax(0, 0)
                probabilities(0)
                copy_of(s_tr, 2, tT, B_TR, s_tT)
                copy_of(s_q_mm, 2, q2T[0], B_TR, s_q)

            def step(t, q, more):
                if more:
                    copy_of(s_tr, 2 * t + 3, tT, B_TR, s_tT)
                softmax(1, t)
                if more:
                    copy_of(s_q_mm, 2 * t + 3, q1T, B_TR, s_q)
                copy_of(s_pT_mm[1], t + 1, pr2T, B_E2, s_pT[1])
                if more:
                    softmax(0, t + 1)
                copy_of(s_c_mm, t + 1, cT, B_C, s_c)
                if more:
                    probabilities(t + 1)
                copy_of(s_tr2, t + 1, uT, B_C, s_uT)
                if more:
                    copy_of(s_tr, 2 * t + 4, tT, B_TR, s_tT)
                relu(t)
                if more:
                    copy_of(s_q_mm, 2 * t + 4, q2T[1 - q], B_TR, s_q)

            steps(nc.scalar, prologue, step)

        OWN_F, OWN_B = 5, 7

        @block.vector
        def _(dve):
            dve.wait_ge(s_const, n_const)
            dve.wait_ge(s_x, 16)
            dve.wait_ge(s_w["ln"], 16 * 6)

            def statistics(n, src, s_own, count):
                stand_alone(dve)
                nc.vector.bn_stats(bst[n][:], src).then_inc(s_own, 1)
                dve.wait_ge(s_own, count)
                stand_alone(dve)

            def aggregate(n):
                nc.vector.bn_aggr(mv[n][:], bst[n][:]).then_inc(s_var[n], 1)

            def affine(n, src, dst, t, s_own, count, s_out):
                dve.wait_ge(s_var[n], t + 1)
                nc.vector.scalar_tensor_tensor(dst, src, mv[n][:, 0:1], ln[:, 2 * n - 2, :], ALU.subtract,
                                               ALU.mult).then_inc(s_own, 1)
                dve.wait_ge(s_rstd[n], t + 1)
                dve.wait_ge(s_own, count)
                nc.vector.scalar_tensor_tensor(dst, dst, rstd[n][:], ln[:, 2 * n - 1, :], ALU.mult,
                                               ALU.add).then_inc(s_out, 1)

            def input_statistics(t):
                statistics(0, xres[:, t, :], s_own0, t + 1)
                aggregate(0)

            def input_norm(t):
                dve.wait_ge(s_rstd[0], t + 1)
                dve.wait_ge(s_var[0], t + 1)
                nc.vector.tensor_scalar(xn[:], xres[:, t, :], mv[0][:, 0:1], rstd[0][:], ALU.subtract,
                                        ALU.mult).then_inc(s_xn, 1)

            def values(t):
                dve.wait_ge(s_v_mm, t + 1)
                nc.vector.tensor_copy(v1[:], ps[:, B_V, :]).then_inc(s_v, 1)

            def count_keys(t):
                dve.wait_ge(s_e[0], t + 1)
                nc.vector.scalar_tensor_tensor(msk1[:], ps[:, B_E, 0:P], 0.0, c["same_batch"][:], ALU.not_equal,
                                               ALU.mult, accum_out=cnt[0][:]).then_inc(s_cnt[0], 1)

            def mask(t):
                dve.wait_ge(s_cnt[0], t + 1)
                dve.wait_ge(s_len[0], t + 1)
                nc.vector.scalar_tensor_tensor(msk1[:], c["key_in_batch"][:], ps[:, B_LEN, 0:1], c["causal"][:],
                                               ALU.is_ge, ALU.max).then_inc(s_ownf, 1)
                dve.wait_ge(s_ownf, OWN_F * t + 1)
                nc.vector.scalar_tensor_tensor(msk1[:], msk1[:], BIG, ps[:, B_E, 0:P], ALU.mult,
                                               ALU.add).then_inc(s_ownf, 1)
                dve.wait_ge(s_ownf, OWN_F * t + 2)
                nc.vector.tensor_reduce(top[0][:], msk1[:], AX.X, ALU.max).then_inc(s_ownf, 1)
                dve.wait_ge(s_ownf, OWN_F * t + 3)
                nc.vector.tensor_scalar(nmx[0][:], top[0][:], -SCALE, None, ALU.mult).then_inc(s_bias[0], 1)

            def x1_sum(t, q):
                dve.wait_ge(s_exp[0], t + 1)
                nc.vector.reciprocal(rinv[0][:], rsum[0][:]).then_inc(s_ownf, 1)
                dve.wait_ge(s_ownf, OWN_F * t + 4)
                dve.wait_ge(s_z1, t + 1)
                nc.vector.scalar_tensor_tensor(x1[q][:], ps[:, B_V, :], rinv[0][:], xn[:], ALU.mult,
                                               ALU.add).then_inc(s_ownf, 1)
                dve.wait_ge(s_ownf, OWN_F * t + 5)
                statistics(1, x1[q][:], s_own1, t + 1)
                aggregate(1)

            def count_cross_keys(t):
                dve.wait_ge(s_e[1], t + 1)
                nc.vector.tensor_scalar(msk2[:], ps[:, B_E2, :], 0.0, None, ALU.not_equal, ALU.add,
                                        accum_out=cnt[1][:]).then_inc(s_cnt[1], 1)

            def cross_mask(t):
                dve.wait_ge(s_cnt[1], t + 1)
                dve.wait_ge(s_len[1], t + 1)
                nc.vector.tensor_scalar(msk2[:], c["key_index"][:], ps[:, B_LEN2, 0:1], BIG, ALU.is_ge,
                                        ALU.mult).then_inc(s_ownb, 1)
                dve.wait_ge(s_ownb, OWN_B * t + 1)
                nc.vector.tensor_tensor(msk2[:], msk2[:], ps[:, B_E2, :], ALU.add).then_inc(s_ownb, 1)
                dve.wait_ge(s_ownb, OWN_B * t + 2)
                nc.vector.tensor_reduce(top[1][:], msk2[:], AX.X, ALU.max).then_inc(s_ownb, 1)
                dve.wait_ge(s_ownb, OWN_B * t + 3)
                nc.vector.tensor_scalar(nmx[1][:], top[1][:], -SCALE, None, ALU.mult).then_inc(s_bias[1], 1)

            def x2_sum(t, q):
                dve.wait_ge(s_exp[1], t + 1)
                nc.vector.reciprocal(rinv[1][:], rsum[1][:]).then_inc(s_ownb, 1)
                dve.wait_ge(s_ownb, OWN_B * t + 4)
                dve.wait_ge(s_z2, t + 1)
                nc.vector.scalar_tensor_tensor(x2[:], ps[:, B_Z, :], rinv[1][:], x1[q][:], ALU.mult,
                                               ALU.add).then_inc(s_ownb, 1)
                dve.wait_ge(s_ownb, OWN_B * t + 5)
                statistics(2, x2[:], s_own2, t + 1)
                aggregate(2)

            def x3_sum(t):
                dve.wait_ge(s_x2, t + 1)
                dve.wait_ge(s_z3, t + 1)
                nc.vector.tensor_tensor(x3[:], ps[:, B_Z, :], x2[:], ALU.add).then_inc(s_ownb, 1)
                dve.wait_ge(s_ownb, OWN_B * t + 6)
                statistics(3, x3[:], s_own3, t + 1)
                aggregate(3)

            def result(t):
                affine(3, x3[:], x3[:], t, s_ownb, OWN_B * t + 7, s_y3)
                dve.wait_ge(s_y3, t + 1)
                nc.vector.tensor_tensor(xres[:, t, :], xres[:, t, :], x3[:], ALU.add).then_inc(s_done, 1)

            def prologue():
                input_statistics(0)
                input_norm(0)
                values(0)
                count_keys(0)
                mask(0)
                x1_sum(0, 0)
                affine(1, x1[0][:], x1[0][:], 0, s_gain1, 1, s_x1)
                input_statistics(1)
                input_norm(1)

            def step(t, q, more, after=True):
                count_cross_keys(t)
                cross_mask(t)
                if more:
                    values(t + 1)
                    count_keys(t + 1)
                    mask(t + 1)
                x2_sum(t, q)
                if more:
                    x1_sum(t + 1, 1 - q)
                affine(2, x2[:], x2[:], t, s_gain2, t + 1, s_x2)
                if more:
                    affine(1, x1[1 - q][:], x1[1 - q][:], t + 1, s_gain1, t + 2, s_x1)
                if after:
                    input_statistics(t + 2)
                    input_norm(t + 2)
                x3_sum(t)
                result(t)

            prologue()
            with nc.vector.Fori(0, NT // 2 - 1) as g:
                step(2 * g, 0, True)
                step(2 * g + 1, 1, True)
            step(NT - 2, 0, True, False)
            step(NT - 1, 1, False, False)
            dve.wait_ge(s_done, NT)

    nc.clear_and_free_semaphores(sems)
    nc.all_engine_barrier()


def mamba_block(nc, d, c, s_const, n_const, xres, xf_d, xfT_d, logits, s_xf_d, zero_rows):
    with ExitStack() as ctx:
        def sb(name, shape, dt=F32):
            return ctx.enter_context(nc.sbuf_tensor("B_" + name, shape, dt))

        def sem(name):
            return ctx.enter_context(nc.semaphore(name))

        ps = ctx.enter_context(nc.psum_tensor("psB", [P, 8, 512], F32))
        w_in = sb("w_in", [P, KD, 2 * C])
        w_x = sb("w_x", [P, MC, 96])
        w_dt = sb("w_dt", [NS + 1, C])
        w_out = sb("w_out", [P, MC, D])
        gate_w = sb("gate_w", [P, KD, E])
        chan = sb("chan", [P, MC, 9])
        a_neg = sb("a_neg", [P, MC])
        b_out = sb("b_out", [P, D])
        xm = sb("xm", [P, 2, D])
        xmT = sb("xmT", [P, KD, TG])
        b_rep = xmT[:].rearrange("p k t -> p (k t)").rearrange("p (m j) -> p m j", m=MC)
        xe = sb("xe", [P, MC, 4, L + 3])
        zs = sb("zs", [P, MC, TG])
        xc = sb("xc", [P, MC, TG])
        dtr = sb("dtr", [NS + 1, TG])
        bT = sb("bT", [NS, TG])
        cTt = sb("cTt", [NS, TG])
        btok = sb("btok", [P, 2, NS])
        bd = sb("bd", [P, 2, 16, NS])
        cd = sb("cd", [P, 4, L])
        t0 = sb("t0", [P, MC, TG])
        t1 = sb("t1", [P, MC, TG])
        dec = sb("dec", [P, MC, TG])
        v = [sb(f"v{a}", [P, MC, TG]) for a in range(2)]
        y = sb("y", [P, MC, TG])
        prod = sb("prod", [P, MC, TG])
        cb = prod[0:NS].rearrange("n m t -> n (m t)").rearrange("n (j t) -> n j t", j=Q)
        vend = sb("vend", [P, MC, TG])
        st = sb("st", [P, MC, TG * NS // Q])
        stmp = sb("stmp", [P, 4 * MC, NS])
        bst = sb("bstB", [P, 2, 6])
        mv = sb("mvB", [P, 2, 2])
        ve = sb("veB", [P, 2])
        rstd = sb("rstdB", [P, 2])
        vT = dec[:].rearrange("p m t -> p (m t)").rearrange("p (i n) -> p i n", i=2)
        stT = [t1, v[0]]

        def stT_of(b):
            return stT[b // 2][:].rearrange("p m t -> p (m t)")[:, (b % 2) * C:(b % 2 + 1) * C]

        s_w = sem("B_weights")
        s_g = sem("B_gate_w")
        s_brep = sem("B_brep")
        s_gain = sem("B_gain")
        s_bo = sem("B_bo")
        s_aexp = sem("B_aexp")
        s_aneg = sem("B_aneg")
        s_bo_mm = sem("B_bo_mm")
        s_zero = sem("B_zero")
        s_xm = sem("B_xm")
        s_var = sem("B_var")
        s_ve = sem("B_ve")
        s_rstd = sem("B_rstd")
        s_tr = sem("B_tr")
        s_xmT = sem("B_xmT")
        s_xz_mm = sem("B_xz_mm")
        s_xz = sem("B_xz")
        s_conv = sem("B_conv")
        s_xc = sem("B_xc")
        s_pr_mm = sem("B_pr_mm")
        s_pr = sem("B_pr")
        s_dt_mm = sem("B_dt_mm")
        s_act = sem("B_act")
        s_ln = sem("B_ln")
        s_cb = sem("B_cb")
        s_cb_mm = sem("B_cb_mm")
        s_cr_mm = sem("B_cr_mm")
        s_cd = sem("B_cd")
        s_bd = sem("B_bd")
        s_S = sem("B_S")
        s_dec = sem("B_dec")
        s_v = sem("B_v")
        s_vend = sem("B_vend")
        s_prod = sem("B_prod")
        s_vT_mm = sem("B_vT_mm")
        s_vT = sem("B_vT")
        s_u_mm = sem("B_u_mm")
        s_u = sem("B_u")
        s_st = sem("B_st")
        s_sT_mm = sem("B_sT_mm")
        s_sT = sem("B_sT")
        s_y2 = sem("B_y2")
        s_y = sem("B_y")
        s_mean = sem("B_mean")
        s_yc = sem("B_yc")
        s_sq = sem("B_sq")
        s_vcol = sem("B_vcol")
        s_vc = sem("B_vc")
        s_out = sem("B_out")
        s_lg_mm = sem("B_lg_mm")
        s_lg = sem("B_lg")
        s_dve = sem("B_dve")

        def stand_alone(eng):
            eng.sem_inc(s_passed, 1)

        s_passed = sem("B_waits_passed")

        block = ctx.enter_context(nc.Block())

        @block.sync
        def _(sp):
            for k in range(KD):
                sp.dma_start(w_in[:, k, :], d["w_in"][k * P:(k + 1) * P, :]).then_inc(s_w, 16)
            sp.dma_start(w_x[:], d["w_x"].rearrange("(m p) n -> p m n", p=P)).then_inc(s_w, 16)
            sp.dma_start(w_dt[:], d["w_dt"]).then_inc(s_w, 16)
            sp.dma_start(chan[:], d["chan"]).then_inc(s_w, 16)
            sp.dma_start(w_out[:], d["w_out"].rearrange("(m p) n -> p m n", p=P)).then_inc(s_w, 16)
            sp.dma_start(gate_w[:], d["gate_w"].rearrange("(k p) n -> p k n", p=P)).then_inc(s_g, 16)
            zero_rows(sp)
            sp.sem_inc(s_xf_d, 1)
            with nc.sync.Fori(0, G) as g:
                sp.wait_ge(s_xm, 4 * g + 4)
                sp.dma_start(xf_d.rearrange("(g i p) n -> g p i n", i=2, p=P)[g], xm[:]).then_inc(s_xf_d, 16)
                sp.wait_ge(s_xmT, 4 * g + 4)
                sp.dma_start(xfT_d.rearrange("(k p) (g t) -> g p k t", p=P, g=G)[g], xmT[:]).then_inc(s_xf_d, 16)

        N_W = 16 * 8

        @block.gpsimd
        def _(pool):
            pool.memset(xe[:].rearrange("p m b t -> p (m b) t")[:, :, 0:3], 0.0).then_inc(s_zero, 1)
            pool.memset(cb, 0.0).then_inc(s_zero, 1)
            pool.memset(dtr[:], 1.0).then_inc(s_zero, 1)
            pool.wait_ge(s_zero, 3)
            with nc.gpsimd.Fori(0, G) as g:
                def rsqrt(n):
                    pool.wait_ge(s_var, 4 * g + n)
                    nc.gpsimd.tensor_tensor(ve[:], mv[:, :, 1], c["eps"][:], ALU.add).then_inc(s_ve, 1)

                def power(n):
                    pool.wait_ge(s_ve, 3 * g + n)
                    nc.gpsimd.tensor_tensor(rstd[:], ve[:], c["minus_half"][:, 0:2], ALU.pow).then_inc(s_rstd, 1)

                rsqrt(2)
                power(1)
                pool.wait_ge(s_pr, 4 * g + 4)
                for j in range(Q):
                    nc.gpsimd.tensor_tensor(cb[:, j, j:TG], cTt[:, j:TG], bT[:, 0:TG - j], ALU.mult).then_inc(s_cb, 1)
                for i in range(2):
                    nc.gpsimd.tensor_tensor(bd[:, i], c["own_chunk"][:],
                                            btok[:, i, :].unsqueeze(1).to_broadcast([P, 16, NS]),
                                            ALU.mult).then_inc(s_bd, 1)
                dch = dec[:].rearrange("p m (k t) -> p (m k) t", t=Q)
                pch = prod[:].rearrange("p m (k t) -> p (m k) t", t=Q)
                pool.wait_ge(s_cb_mm, g + 1)
                pool.wait_ge(s_dec, 8 * g + 8)
                nc.gpsimd.tensor_tensor(pch[:, :, 0:1], dch[:, :, 0:1],
                                        c["ones"][:, 0:1].unsqueeze(1).to_broadcast([P, MC * TG // Q, 1]),
                                        ALU.mult).then_inc(s_prod, 1)
                for t in range(1, Q):
                    pool.wait_ge(s_prod, 8 * g + t)
                    nc.gpsimd.tensor_tensor(pch[:, :, t:t + 1], pch[:, :, t - 1:t], dch[:, :, t:t + 1],
                                            ALU.mult).then_inc(s_prod, 1)
                pool.wait_ge(s_vc, g + 1)
                nc.gpsimd.tensor_tensor(ve[:], mv[:, :, 1], c["eps"][:], ALU.add).then_inc(s_ve, 1)
                power(2)
                rsqrt(4)
                power(3)

        @block.tensor
        def _(pe):
            pe.wait_ge(s_brep, MC)
            for m in range(MC):
                mm = nc.tensor.matmul(ps[:, 0, :], b_rep[:, m, :], w_out[:, m, :], start=(m == 0), stop=(m == MC - 1))
            mm.then_inc(s_bo_mm, 1)
            pe.wait_ge(s_gain, MC)
            pe.wait_ge(s_bo, 1)
            pe.wait_ge(s_zero, 3)
            pe.wait_ge(s_g, 16)

            with nc.tensor.Fori(0, G) as g:
                dmaj = ps[:, 0:2, :].rearrange("p b (k t) -> p (b k) t", k=2)

                def transposes():
                    for i in range(2):
                        for k in range(KD):
                            mm = nc.tensor.transpose(dmaj[:, k, i * P:(i + 1) * P], xm[:, i, k * P:(k + 1) * P],
                                                     c["ident"][:])
                    mm.then_inc(s_tr, 1)

                pe.wait_ge(s_xm, 4 * g + 2)
                transposes()
                pe.wait_ge(s_xmT, 4 * g + 2)
                for j in range(MC):
                    if j >= 6:
                        pe.wait_ge(s_xz, 8 * g + j - 5)
                    for a in range(2):
                        m = 2 * j + a
                        for k in range(KD):
                            mm = nc.tensor.matmul(ps[:, 2 + j % 6, a * TG:(a + 1) * TG], w_in[:, k, m * P:(m + 1) * P],
                                                  xmT[:, k, :], start=(k == 0), stop=(k == KD - 1))
                    mm.then_inc(s_xz_mm, 1)
                pe.wait_ge(s_xc, g + 1)
                for m in range(MC):
                    nc.tensor.matmul(ps[0:96, 0, 0:TG], w_x[:, m, :], xc[:, m, :], start=(m == 0), stop=(m == MC - 1))
                for i in range(2):
                    for m in range(MC):
                        mm = nc.tensor.matmul(ps[:, 1, i * NS:(i + 1) * NS], xc[:, m, i * P:(i + 1) * P],
                                              w_x[:, m, 32:32 + NS], start=(m == 0), stop=(m == MC - 1))
                mm.then_inc(s_pr_mm, 1)
                pe.wait_ge(s_pr, 4 * g + 4)
                pe.wait_ge(s_xz, 8 * g + 8)
                for m in range(MC):
                    mm = nc.tensor.matmul(ps[:, m // 2, (m % 2) * TG:(m % 2 + 1) * TG], w_dt[:, m * P:(m + 1) * P],
                                          dtr[:], start=True, stop=True)
                mm.then_inc(s_dt_mm, 1)
                nc.tensor.matmul(ps[:, 4, 0:TG], c["rep_state"][:].rearrange("n k m -> n (k m)"), cTt[:],
                                 start=True, stop=True).then_inc(s_cr_mm, 1)
                pe.wait_ge(s_cd, g + 1)
                for j in range(Q):
                    pe.wait_ge(s_cb, 8 * g + j + 1)
                    mm = nc.tensor.matmul(ps[:, 4 + j // 2, (j % 2) * TG:(j % 2 + 1) * TG], c["ones"][0:NS, :],
                                          cb[:, j, :], start=True, stop=True)
                mm.then_inc(s_cb_mm, 1)
                pe.wait_ge(s_vend, 8 * g + 8)
                for i in range(2):
                    for a in range(2):
                        for m in range(4):
                            mm = nc.tensor.transpose(ps[:, 2 * i + a, m * P:(m + 1) * P],
                                                     vend[:, 4 * a + m, i * P:(i + 1) * P], c["ident"][:])
                        mm.then_inc(s_vT_mm, 1)
                for i in range(2):
                    pe.wait_ge(s_bd, 2 * g + i + 1)
                    pe.wait_ge(s_vT, 4 * g + 4)
                    for a in range(4):
                        if i:
                            pe.wait_ge(s_u, 8 * g + a + 1)
                        for m in range(2 * a, 2 * a + 2):
                            mm = nc.tensor.matmul(ps[:, a, (m % 2) * TG:(m % 2 + 1) * TG], vT[:, i, m * P:(m + 1) * P],
                                                  bd[:, i].rearrange("p k n -> p (k n)"), start=True, stop=True)
                        mm.then_inc(s_u_mm, 1)
                pe.wait_ge(s_st, g + 1)
                for b in range(4):
                    for a in range(2):
                        j = 2 * b + a
                        if j >= 4:
                            pe.wait_ge(s_sT, 8 * g + j - 3)
                        for m in range(4):
                            mm = nc.tensor.transpose(ps[:, j % 4, m * P:(m + 1) * P],
                                                     st[:, 4 * a + m, b * P:(b + 1) * P], c["ident"][:])
                        mm.then_inc(s_sT_mm, 1)
                pe.wait_ge(s_sT, 8 * g + 8)
                for m in range(MC):
                    for b in range(4):
                        mm = nc.tensor.matmul(ps[:, 4 + m // 2, (m % 2) * TG + b * L:(m % 2) * TG + (b + 1) * L],
                                              stT_of(b)[:, m * P:(m + 1) * P], cd[:, b, :], start=True, stop=True)
                mm.then_inc(s_y2, 1)
                pe.wait_ge(s_y, g + 1)
                for m in range(MC):
                    mm = nc.tensor.matmul(ps[:, 0, 0:TG], c["ones_over_c"][:], y[:, m, :], start=(m == 0),
                                          stop=(m == MC - 1))
                mm.then_inc(s_mean, 1)
                pe.wait_ge(s_yc, g + 1)
                for i in range(2):
                    for m in range(MC):
                        mm = nc.tensor.matmul(ps[:, 2 + i, :], y[:, m, i * P:(i + 1) * P], w_out[:, m, :],
                                              start=(m == 0), stop=(m == MC - 1))
                    mm.then_inc(s_out, 1)
                pe.wait_ge(s_sq, g + 1)
                for i in range(2):
                    for m in range(MC):
                        mm = nc.tensor.matmul(ps[:, 1, i:i + 1], t1[:, m, i * P:(i + 1) * P],
                                              c["ones_over_c"][:, 0:1], start=(m == 0), stop=(m == MC - 1))
                mm.then_inc(s_vcol, 1)
                pe.wait_ge(s_xm, 4 * g + 4)
                transposes()
                pe.wait_ge(s_xmT, 4 * g + 4)
                for i in range(2):
                    for k in range(KD):
                        mm = nc.tensor.matmul(ps[:, 2, i * E:(i + 1) * E], xmT[:, k, i * P:(i + 1) * P], gate_w[:, k, :],
                                              start=(k == 0), stop=(k == KD - 1))
                mm.then_inc(s_lg_mm, 1)

        ACT_STEPS = 2

        @block.scalar
        def _(act):
            act.wait_ge(s_w, N_W)
            for m in range(MC):
                nc.scalar.activation(b_rep[:, m, :], c["ones"][:], ACT.Identity,
                                     scale=chan[:, m, 8:9]).then_inc(s_brep, 1)
            nc.scalar.activation(a_neg[:], chan[:, :, 5], ACT.Exp).then_inc(s_aexp, 1)
            act.wait_ge(s_bo_mm, 1)
            for m in range(MC):
                nc.scalar.activation(w_out[:, m, :], w_out[:, m, :], ACT.Identity,
                                     scale=chan[:, m, 7:8]).then_inc(s_gain, 1)
            act.wait_ge(s_aneg, 1)
            with nc.scalar.Fori(0, G) as g:
                steps = [0]

                def own(ins):
                    ins.then_inc(s_act, 1)
                    steps[0] += 1
                    act.wait_ge(s_act, ACT_STEPS * g + steps[0])

                def spread(n):
                    act.wait_ge(s_tr, 2 * g + n)
                    for b in range(2):
                        nc.scalar.copy(xmT[:, 2 * b:2 * b + 2, :].rearrange("p k t -> p (k t)"),
                                       ps[:, b, :]).then_inc(s_xmT, 1)

                act.wait_ge(s_xf_d, 32 * g + 1)
                spread(1)
                for j in range(MC):
                    act.wait_ge(s_xz_mm, 8 * g + j + 1)
                    src = ps[:, 2 + j % 6, :]
                    if j < 4:
                        nc.scalar.copy(xe[:, 2 * j:2 * j + 2].rearrange("p m b t -> p (m b) t")[:, :, 3:],
                                       src.rearrange("p (mb t) -> p mb t", t=L)).then_inc(s_xz, 1)
                    else:
                        nc.scalar.activation(zs[:, 2 * j - 8:2 * j - 6, :].rearrange("p m t -> p (m t)"), src,
                                             ACT.Silu).then_inc(s_xz, 1)
                act.wait_ge(s_conv, MC * g + MC)
                nc.scalar.activation(xc[:], xc[:], ACT.Silu).then_inc(s_xc, 1)
                act.wait_ge(s_pr_mm, g + 1)
                nc.scalar.copy(dtr[0:NS, :], ps[0:NS, 0, 0:TG]).then_inc(s_pr, 1)
                nc.scalar.copy(bT[:], ps[32:32 + NS, 0, 0:TG]).then_inc(s_pr, 1)
                nc.scalar.copy(cTt[:], ps[64:64 + NS, 0, 0:TG]).then_inc(s_pr, 1)
                nc.scalar.copy(btok[:].rearrange("p i n -> p (i n)"), ps[:, 1, 0:2 * NS]).then_inc(s_pr, 1)
                act.wait_ge(s_dt_mm, g + 1)
                own(nc.scalar.activation(t0[:].rearrange("p m t -> p (m t)"),
                                         ps[:, 0:4, :].rearrange("p b n -> p (b n)"), ACT.Abs))
                own(nc.scalar.activation(t0[:], t0[:], ACT.Exp, scale=-1.0))
                nc.scalar.activation(t1[:], t0[:], ACT.Ln, bias=1.0).then_inc(s_ln, 1)
                for m in range(MC):
                    act.wait_ge(s_S, MC * g + m + 1)
                    nc.scalar.activation(dec[:, m, :], t1[:, m, :], ACT.Exp, scale=a_neg[:, m:m + 1]).then_inc(s_dec, 1)
                for j in range(Q):
                    act.wait_ge(s_v, 8 * g + j + 1)
                    src = v[j % 2][:].rearrange("p m (k t) -> p (m k) t", t=Q)[:, :, Q - 1:Q]
                    dst = vend[:].rearrange("p m (k t) -> p (m k) t", t=Q)[:, :, Q - 1 - j:Q - j]
                    nc.scalar.copy(dst, src).then_inc(s_vend, 1)
                act.wait_ge(s_prod, 8 * g + 8)
                for b in range(4):
                    act.wait_ge(s_vT_mm, 4 * g + b + 1)
                    nc.scalar.copy(vT[:, b // 2, (b % 2) * 512:(b % 2 + 1) * 512], ps[:, b, :]).then_inc(s_vT, 1)
                for i in range(2):
                    for a in range(4):
                        act.wait_ge(s_u_mm, 8 * g + 4 * i + a + 1)
                        nc.scalar.copy(st[:, 2 * a:2 * a + 2, i * TG:(i + 1) * TG],
                                       ps[:, a, :].rearrange("p (m n) -> p m n", m=2)).then_inc(s_u, 1)
                for j in range(8):
                    act.wait_ge(s_sT_mm, 8 * g + j + 1)
                    nc.scalar.copy(stT_of(j // 2)[:, (j % 2) * 512:(j % 2 + 1) * 512], ps[:, j % 4, :]).then_inc(s_sT, 1)
                act.wait_ge(s_yc, g + 1)
                nc.scalar.activation(t1[:], y[:], ACT.Square).then_inc(s_sq, 1)
                spread(2)
                act.wait_ge(s_lg_mm, g + 1)
                nc.scalar.copy(logits[:, bass.ds(2 * g, 2), :],
                               ps[:, 2, 0:2 * E].rearrange("p (i e) -> p i e", i=2)).then_inc(s_lg, 1)
                assert steps[0] == ACT_STEPS, steps[0]

        DVE_STEPS = 72

        @block.vector
        def _(dve):
            dve.wait_ge(s_w, N_W)
            dve.wait_ge(s_aexp, 1)
            nc.vector.tensor_scalar(a_neg[:], a_neg[:], -1.0, None, ALU.mult).then_inc(s_aneg, 1)
            dve.wait_ge(s_bo_mm, 1)
            nc.vector.tensor_copy(b_out[:], ps[:, 0, :]).then_inc(s_bo, 1)
            dve.wait_ge(s_bo, 1)

            with nc.vector.Fori(0, G) as g:
                steps = [0]

                def own(*instructions):
                    for ins in instructions:
                        ins.then_inc(s_dve, 1)
                    steps[0] += len(instructions)
                    dve.wait_ge(s_dve, DVE_STEPS * g + steps[0])

                def chunks(t):
                    return t[:].rearrange("p m (k t) -> p (m k) t", t=Q)

                def norm(src, dst, n, s_out):
                    stand_alone(dve)
                    own(*[nc.vector.bn_stats(bst[:, i, :], src(i)) for i in range(2)])
                    stand_alone(dve)
                    for i in range(2):
                        nc.vector.bn_aggr(mv[:, i, :], bst[:, i, :]).then_inc(s_var, 1)
                    dve.wait_ge(s_rstd, 3 * g + (1 if n == 1 else 3))
                    dve.wait_ge(s_var, 4 * g + 2 * n)
                    for i in range(2):
                        nc.vector.tensor_scalar(dst(i), src(i), mv[:, i, 0:1], rstd[:, i:i + 1],
                                                ALU.subtract, ALU.mult).then_inc(s_out, 1)

                dve.wait_ge(s_xf_d, 32 * g + 1)
                norm(lambda i: xres[:, 2 * g + i, :], lambda i: xm[:, i, :], 1, s_xm)
                dve.wait_ge(s_xz, 8 * g + 4)
                own(*[nc.vector.tensor_scalar(xc[:, m, :].rearrange("p (b t) -> p b t", b=4), xe[:, m, :, 3:3 + L],
                                              chan[:, m, 3:4], chan[:, m, 4:5], ALU.mult, ALU.add)
                      for m in range(MC)])
                for j in range(3):
                    ins = [nc.vector.scalar_tensor_tensor(
                        xc[:, m, :].rearrange("p (b t) -> p b t", b=4), xe[:, m, :, j:j + L], chan[:, m, j:j + 1],
                        xc[:, m, :].rearrange("p (b t) -> p b t", b=4), ALU.mult, ALU.add) for m in range(MC)]
                    if j < 2:
                        own(*ins)
                for x in ins:
                    x.then_inc(s_conv, 1)
                dve.wait_ge(s_cr_mm, g + 1)
                nc.vector.tensor_tensor(cd[:].rearrange("p b t -> p (b t)").rearrange("p (b t) -> p b t", b=4),
                                        ps[:, 4, 0:TG].rearrange("p (b t) -> p b t", b=4),
                                        c["next_chunk"][:].rearrange("p k t -> p (k t)").unsqueeze(1).to_broadcast(
                                            [P, 4, L]), ALU.mult).then_inc(s_cd, 1)
                dve.wait_ge(s_ln, g + 1)
                own(nc.vector.tensor_scalar(y[:], t0[:], 1.0, 1.0, ALU.add, ALU.subtract))
                own(nc.vector.tensor_tensor(y[:], t1[:], y[:], ALU.subtract))
                own(nc.vector.tensor_tensor(y[:], y[:], t0[:], ALU.add))
                own(nc.vector.scalar_tensor_tensor(y[:].rearrange("p m t -> p (m t)"),
                                                   ps[:, 0:4, :].rearrange("p b n -> p (b n)"), 0.0,
                                                   y[:].rearrange("p m t -> p (m t)"), ALU.max, ALU.add))
                for m in range(MC):
                    nc.vector.tensor_tensor_scan(t1[:, m, :], c["in_sequence"][:], y[:, m, :], 0.0, ALU.mult,
                                                 ALU.add).then_inc(s_S, 1)
                nc.vector.tensor_tensor(v[0][:], y[:], xc[:], ALU.mult).then_inc(s_v, 1)
                dve.wait_ge(s_v, 8 * g + 1)
                dve.wait_ge(s_cb_mm, g + 1)

                def weight(j):
                    return ps[:, 4 + j // 2, (j % 2) * TG:(j % 2 + 1) * TG].rearrange(
                        "p (k t) -> p k t", t=Q).unsqueeze(1)[:, :, :, j:Q].to_broadcast([P, MC, TG // Q, Q - j])

                def four(t, j):
                    return t[:].rearrange("p m (k t) -> p m k t", t=Q)[:, :, :, j:Q]

                own(nc.vector.tensor_tensor(four(y, 0), four(v[0], 0), weight(0), ALU.mult))
                dve.wait_ge(s_dec, 8 * g + 8)
                for j in range(1, Q):
                    new, old = v[j % 2], v[(j - 1) % 2]
                    if j >= 2:
                        dve.wait_ge(s_vend, 8 * g + j - 1)
                    nc.vector.tensor_tensor(chunks(new)[:, :, j:Q], chunks(dec)[:, :, j:Q],
                                            chunks(old)[:, :, j - 1:Q - 1], ALU.mult).then_inc(s_v, 1)
                    dve.wait_ge(s_v, 8 * g + j + 1)
                    own(nc.vector.tensor_tensor(four(t0, j), four(new, j), weight(j), ALU.mult))
                    own(nc.vector.tensor_tensor(chunks(y)[:, :, j:Q], chunks(y)[:, :, j:Q], chunks(t0)[:, :, j:Q],
                                                ALU.add))
                own(*[nc.vector.scalar_tensor_tensor(y[:, m, :], xc[:, m, :], chan[:, m, 6:7], y[:, m, :],
                                                     ALU.mult, ALU.add) for m in range(MC)])
                dve.wait_ge(s_u, 8 * g + 8)
                dve.wait_ge(s_prod, 8 * g + 8)
                stk = st[:].rearrange("p m (b k n) -> p (m b) k n", b=4, k=Q)
                pck = prod[:].rearrange("p m (b k t) -> p (m b) k t", b=4, k=Q)
                for k in range(1, Q - 1):
                    own(nc.vector.tensor_tensor(stmp[:], stk[:, :, k - 1, :],
                                                pck[:, :, k, Q - 1:Q].to_broadcast([P, 4 * MC, NS]), ALU.mult))
                    add = nc.vector.tensor_tensor(stk[:, :, k, :], stk[:, :, k, :], stmp[:], ALU.add)
                    if k < Q - 2:
                        own(add)
                add.then_inc(s_st, 1)
                dve.wait_ge(s_y2, g + 1)
                own(nc.vector.tensor_tensor(v[1][:].rearrange("p m t -> p (m t)"),
                                            prod[:].rearrange("p m t -> p (m t)"),
                                            ps[:, 4:8, :].rearrange("p b n -> p (b n)"), ALU.mult))
                own(nc.vector.tensor_tensor(y[:], y[:], v[1][:], ALU.add))
                nc.vector.tensor_tensor(y[:], y[:], zs[:], ALU.mult).then_inc(s_y, 1)
                dve.wait_ge(s_mean, g + 1)
                dve.wait_ge(s_y, g + 1)
                nc.vector.tensor_tensor(y[:], y[:], ps[:, 0, 0:TG].unsqueeze(1).to_broadcast([P, MC, TG]),
                                        ALU.subtract).then_inc(s_yc, 1)
                own(*[nc.vector.tensor_tensor(xres[:, 2 * g + i, :], xres[:, 2 * g + i, :], b_out[:], ALU.add)
                      for i in range(2)])
                dve.wait_ge(s_vcol, g + 1)
                nc.vector.tensor_copy(mv[:, :, 1], ps[:, 1, 0:2]).then_inc(s_vc, 1)
                dve.wait_ge(s_rstd, 3 * g + 2)
                dve.wait_ge(s_out, 2 * g + 2)
                own(*[nc.vector.scalar_tensor_tensor(xres[:, 2 * g + i, :], ps[:, 2 + i, :], rstd[:, i:i + 1],
                                                     xres[:, 2 * g + i, :], ALU.mult, ALU.add) for i in range(2)])
                norm(lambda i: xres[:, 2 * g + i, :], lambda i: xm[:, i, :], 2, s_xm)
                assert steps[0] == DVE_STEPS, steps[0]


def ffn_block(nc, d, c, xres, xf_d, xfT_d, xs_d, ys_d, logits, s_xf_d, s_zero_d):
    with ExitStack() as ctx:
        def sb(name, shape, dt=F32):
            return ctx.enter_context(nc.sbuf_tensor("C_" + name, shape, dt))

        def sem(name):
            return ctx.enter_context(nc.semaphore(name))

        ps = ctx.enter_context(nc.psum_tensor("psC", [P, 8, 512], F32))
        TH = 512
        REST = CAP - P
        w1 = [sb(f"w1_{q}", [P, KD, H]) for q in range(2)]
        w3 = [sb(f"w3_{q}", [P, KD, H]) for q in range(2)]
        w2 = [sb(f"w2_{q}", [P, MH, D]) for q in range(2)]
        xfT = sb("xfT", [P, KD, N])
        xf = sb("xf", [P, NT, D])
        gate_b = sb("gate_b", [P, E])
        hT = sb("hTs", [P, MH, TH])
        sl = [sb(f"sl{a}", [P, TH]) for a in range(2)]
        sc = sb("sc", [P, NT, E])
        red = sb("red", [P, NT])
        best = sb("best", [P, NT, 8])
        best_i = sb("best_i", [P, NT, 8], U32)
        pick = sb("pick", [P, NT, 2])
        onehot = sb("onehot", [P, 2, NT, E])
        prod = sb("prodR", [P, NT, E])
        gate = sb("gate", [P, 2, NT])
        queue = sb("queue", [P, NT, E])
        queueT = sb("queueT", [E, N])
        onehotT = sb("onehotT", [E, 2, N])
        junk = sb("junk", [P, N])
        own_w = sb("own_w", [P, 2, NT])
        part = sb("part", [P, 2, NT, 4])
        rank = sb("rank", [P, 2, NT])
        slot = sb("slot", [P, 2, NT])
        keep = sb("keep", [P, 2, NT])
        slot_i = sb("slot_i", [P, 2, NT], U32)
        xs = [sb(f"xs{q}", [P, D]) for q in range(2)]
        xsr = [sb(f"xsr{q}", [REST, D]) for q in range(2)]
        flat = hT[:].rearrange("p m t -> p (m t)")
        xsT = [flat[:, q * KD * CAP:(q + 1) * KD * CAP].rearrange("p (k s) -> p k s", k=KD) for q in range(2)]
        eT = [flat[:, (2 * KD + q * MH) * CAP:(2 * KD + (q + 1) * MH) * CAP].rearrange("p (m s) -> p m s", m=MH)
              for q in range(2)]
        yT = sb("yT", [P, KD, CAP])
        gathered = xfT[:].rearrange("p k t -> p (k t)").rearrange("p (a k n) -> p a k n", a=4, k=2)
        yo = [gathered[:, 2, q, :] for q in range(2)]
        yor = [gathered[0:REST, 3, q, :] for q in range(2)]

        s_in = sem("C_in")
        s_wA = [sem(f"C_w13_{q}") for q in range(2)]
        s_wB = [sem(f"C_w2_{q}") for q in range(2)]
        s_r = sem("C_router")
        s_ex = sem("C_exp")
        s_qT_mm = sem("C_queueT_mm")
        s_qT = sem("C_queueT")
        s_row_mm = sem("C_row_mm")
        s_row = sem("C_row")
        s_slot = sem("C_slot")
        s_xs_d = sem("C_xs_d")
        s_h_mm = sem("C_h_mm")
        s_sl = sem("C_sl")
        s_h = sem("C_h")
        s_y_mm = sem("C_y_mm")
        s_y = sem("C_y")
        s_xs = [sem(f"C_xs{q}") for q in range(2)]
        s_xT_mm = sem("E_xT_mm")
        s_xT = sem("E_xT")
        s_e_mm = sem("E_h_mm")
        s_esl = sem("E_sl")
        s_e = sem("E_h")
        s_yT_mm = sem("E_yT_mm")
        s_yT = sem("E_yT")
        s_yo_mm = sem("E_yo_mm")
        s_yo = sem("E_yo")
        s_ys = [sem(f"E_ys{q}") for q in range(2)]
        s_g = [sem(f"F_g{a}") for a in range(2)]
        s_f = sem("F_sum")
        s_res = sem("F_out")

        units = [(hf, s) for s in range(2) for hf in range(2)]
        FIRST_ROW = 10

        block = ctx.enter_context(nc.Block())

        def load_w13(eng, q, a, b):
            eng.dma_start(w1[q][:], a.rearrange("(k p) n -> p k n", p=P)).then_inc(s_wA[q], 16)
            eng.dma_start(w3[q][:], b.rearrange("(k p) n -> p k n", p=P)).then_inc(s_wA[q], 16)

        def load_w2(eng, q, a):
            eng.dma_start(w2[q][:], a.rearrange("(m p) n -> p m n", p=P)).then_inc(s_wB[q], 16)

        def load_xs(eng, q, e):
            rows = xs_d.rearrange("(e s) n -> e s n", e=E)[e]
            eng.dma_start(xs[q][:], rows[0:P, :]).then_inc(s_xs[q], 16)
            eng.dma_start(xsr[q][:], rows[P:CAP, :]).then_inc(s_xs[q], 16)

        @block.sync
        def _(sp):
            sp.wait_ge(s_xf_d, 32 * G + 1)
            sp.dma_start(xfT[:], xfT_d.rearrange("(k p) t -> p k t", p=P)).then_inc(s_in, 16)
            load_w13(sp, 0, d["sw1"][0], d["sw3"][0])
            load_w2(sp, 0, d["sw2"][0])
            sp.dma_start(gate_b[:], d["gate_b"].partition_broadcast(P)).then_inc(s_in, 16)
            sp.dma_start(xf[:], xf_d.rearrange("(t p) n -> p t n", p=P)).then_inc(s_in, 16)
            load_w13(sp, 1, d["sw1"][1], d["sw3"][1])
            load_w2(sp, 1, d["sw2"][1])
            for q in range(2):
                sp.wait_ge(s_h_mm, 16 * q + 16)
                load_w13(sp, q, d["ew1"][q], d["ew3"][q])
                sp.wait_ge(s_y_mm, 8 * q + 8)
                load_w2(sp, q, d["ew2"][q])
            sp.wait_ge(s_xs_d, 16 * 2 * NT)
            for q in range(2):
                load_xs(sp, q, q)
            with nc.sync.Fori(0, E // 2 - 1) as ep:
                for q in range(2):
                    sp.wait_ge(s_e_mm, MH * (2 * ep + q + 1))
                    load_w13(sp, q, d["ew1"][2 * ep + q + 2], d["ew3"][2 * ep + q + 2])
                    load_xs(sp, q, 2 * ep + q + 2)
                    sp.wait_ge(s_yT_mm, 2 * (2 * ep + q + 1))
                    load_w2(sp, q, d["ew2"][2 * ep + q + 2])
            for t in range(NT):
                sp.wait_ge(s_f, 2 * t + 2)
                sp.dma_start(d["out"][t * P:(t + 1) * P, :], xres[:, t, :]).then_inc(s_res, 16)
            sp.wait_ge(s_res, 16 * NT)

        @block.gpsimd
        def _(pool):
            pool.wait_ge(s_slot, 1)
            pool.wait_ge(s_in, 48)
            pool.wait_ge(s_zero_d, 32)
            for t in range(NT):
                for k in range(2):
                    nc.gpsimd.indirect_dma_start(
                        xs_d, bass.IndirectOffsetOnAxis(ap=slot_i[:, k, t:t + 1], axis=0), xf[:, t, :], None,
                        bounds_check=E * CAP - 1, oob_is_err=False).then_inc(s_xs_d, 16)
            for q in range(2):
                pool.wait_ge(s_ys[q], 32 * E // 2 + 1)
            for t in range(NT):
                if t >= 2:
                    pool.wait_ge(s_f, 2 * t - 2)
                for k in range(2):
                    nc.gpsimd.indirect_dma_start(
                        gathered[:, t % 2, k, :], None, ys_d, bass.IndirectOffsetOnAxis(ap=slot_i[:, k, t:t + 1], axis=0),
                        bounds_check=E * CAP, oob_is_err=False).then_inc(s_g[t % 2], 16)

        @block.tensor
        def _(pe):
            pe.wait_ge(s_in, 48)

            def queues(n):
                if n == 0:
                    pe.wait_ge(s_r, R_QUEUE)
                else:
                    pe.wait_ge(s_qT, 2 * n)
                for t in range(NT):
                    src = queue[:, t, :] if n == 0 else onehot[:, n - 1, t, :]
                    mm = nc.tensor.transpose(ps[0:E, t // 4, (t % 4) * P:(t % 4 + 1) * P], src, c["ident"][:])
                mm.then_inc(s_qT_mm, 1)

            def row(r):
                t, k = r // 2, r % 2
                if r == 0:
                    pe.wait_ge(s_qT, 6)
                else:
                    pe.wait_ge(s_row, r)
                for b in range(2):
                    mm = nc.tensor.matmul(ps[:, b, :], onehotT[:, k, t * P:(t + 1) * P], queueT[:, b * 512:(b + 1) * 512],
                                          start=True, stop=True)
                mm.then_inc(s_row_mm, 1)

            step = 0
            for hf, s in units:
                if hf == 0:
                    pe.wait_ge(s_wA[s], 32)
                for m in range(MH):
                    if FIRST_ROW - 4 <= step < FIRST_ROW - 1:
                        queues(step - FIRST_ROW + 4)
                    if FIRST_ROW <= step < FIRST_ROW + 2 * NT:
                        row(step - FIRST_ROW)
                    if step >= 2:
                        pe.wait_ge(s_h, step - 1)
                    for a, w in enumerate((w1, w3)):
                        for k in range(KD):
                            mm = nc.tensor.matmul(ps[:, 2 + 2 * (step % 2) + a, :], w[s][:, k, m * P:(m + 1) * P],
                                                  xfT[:, k, hf * TH:(hf + 1) * TH], start=(k == 0), stop=(k == KD - 1))
                    mm.then_inc(s_h_mm, 1)
                    step += 1
                if hf == 0:
                    pe.wait_ge(s_wB[s], 16)
                pe.wait_ge(s_h, step)
                for t in range(4):
                    n = 4 * (2 * s + hf) + t
                    if n >= 2:
                        pe.wait_ge(s_y, n - 1)
                    for m in range(MH):
                        mm = nc.tensor.matmul(ps[:, 6 + n % 2, :], hT[:, m, t * P:(t + 1) * P], w2[s][:, m, :],
                                              start=(m == 0), stop=(m == MH - 1))
                    mm.then_inc(s_y_mm, 1)

            def rows_in(q, e):
                pe.wait_ge(s_xs[q], 16 * (e - q) + 32)
                for k in range(KD):
                    o = (k % 2) * CAP
                    nc.tensor.transpose(ps[:, k // 2, o:o + P], xs[q][:, k * P:(k + 1) * P], c["ident"][:])
                    mm = nc.tensor.transpose(ps[:, k // 2, o + P:o + CAP], xsr[q][:, k * P:(k + 1) * P],
                                             c["ident"][0:REST, 0:REST])
                mm.then_inc(s_xT_mm, 1)

            def expert(q, e, last):
                pe.wait_ge(s_wA[q], 16 * (e - q) + 64)
                pe.wait_ge(s_xT, 2 * e + 2)
                for m in range(MH):
                    if m >= 3:
                        pe.wait_ge(s_e, MH * e + m - 2)
                    if m == 2:
                        pe.wait_ge(s_yo, 2 * e + 1)
                    for a, w in enumerate((w1, w3)):
                        for k in range(KD):
                            mm = nc.tensor.matmul(ps[:, 2 + m % 3, a * CAP:(a + 1) * CAP], w[q][:, k, m * P:(m + 1) * P],
                                                  xsT[q][:, k, :], start=(k == 0), stop=(k == KD - 1))
                    mm.then_inc(s_e_mm, 1)
                if not last:
                    rows_in(1 - q, e + 1)
                pe.wait_ge(s_wB[q], 8 * (e - q) + 32)
                pe.wait_ge(s_e, MH * e + MH)
                for dm in range(KD):
                    for m in range(MH):
                        mm = nc.tensor.matmul(ps[:, 5 + dm // 2, (dm % 2) * CAP:(dm % 2 + 1) * CAP],
                                              w2[q][:, m, dm * P:(dm + 1) * P], eT[q][:, m, :],
                                              start=(m == 0), stop=(m == MH - 1))
                    if dm % 2:
                        mm.then_inc(s_yT_mm, 1)
                for half in range(2):
                    pe.wait_ge(s_yT, 2 * e + half + 1)
                    for dm in range(2 * half, 2 * half + 2):
                        mm = nc.tensor.transpose(ps[:, 7, dm * P:(dm + 1) * P], yT[:, dm, 0:P], c["ident"][:])
                mm.then_inc(s_yo_mm, 1)
                for dm in range(KD):
                    mm = nc.tensor.transpose(ps[0:REST, 4, dm * P:(dm + 1) * P], yT[:, dm, P:CAP], c["ident"][:])
                mm.then_inc(s_yo_mm, 1)

            pe.wait_ge(s_row, 2 * NT)
            rows_in(0, 0)
            with nc.tensor.Fori(0, E // 2 - 1) as ep:
                expert(0, 2 * ep, False)
                expert(1, 2 * ep + 1, False)
            expert(0, E - 2, False)
            expert(1, E - 1, True)

        @block.scalar
        def _(act):
            act.wait_ge(s_r, R_SHIFT)
            nc.scalar.activation(sc[:], sc[:], ACT.Exp).then_inc(s_ex, 1)
            step = 0
            for hf, s in units:
                for m in range(MH):
                    if FIRST_ROW - 4 <= step < FIRST_ROW - 1:
                        n = step - FIRST_ROW + 4
                        act.wait_ge(s_qT_mm, n + 1)
                        for b in range(2):
                            dst = queueT[:, b * 512:(b + 1) * 512] if n == 0 else onehotT[:, n - 1, b * 512:(b + 1) * 512]
                            nc.scalar.copy(dst, ps[0:E, b, :]).then_inc(s_qT, 1)
                    act.wait_ge(s_h_mm, step + 1)
                    if step >= 2:
                        act.wait_ge(s_h, step - 1)
                    nc.scalar.activation(sl[step % 2][:], ps[:, 2 + 2 * (step % 2), :], ACT.Silu).then_inc(s_sl, 1)
                    step += 1

            def rows_in(q, e):
                act.wait_ge(s_xT_mm, e + 1)
                for b in range(2):
                    nc.scalar.copy(xsT[q][:, 2 * b:2 * b + 2, :].rearrange("p k s -> p (k s)"),
                                   ps[:, b, 0:2 * CAP]).then_inc(s_xT, 1)

            def expert(q, e, last):
                for m in range(MH):
                    act.wait_ge(s_e_mm, MH * e + m + 1)
                    if m >= 2:
                        act.wait_ge(s_e, MH * e + m - 1)
                    nc.scalar.activation(sl[m % 2][:, 0:CAP], ps[:, 2 + m % 3, 0:CAP], ACT.Silu).then_inc(s_esl, 1)
                if not last:
                    rows_in(1 - q, e + 1)
                act.wait_ge(s_ys[q], 16 * (e - q) + 1)
                act.wait_ge(s_yo_mm, 2 * e + 1)
                nc.scalar.copy(yo[q], ps[:, 7, :]).then_inc(s_yo, 1)
                act.wait_ge(s_yo_mm, 2 * e + 2)
                nc.scalar.copy(yor[q], ps[0:REST, 4, :]).then_inc(s_yo, 1)
                rows = ys_d[0:E * CAP, :].rearrange("(e s) n -> e s n", e=E)[e]
                act.wait_ge(s_yo, 2 * e + 3)
                act.dma_start(rows[0:P, :], yo[q]).then_inc(s_ys[q], 16)
                act.dma_start(rows[P:CAP, :], yor[q]).then_inc(s_ys[q], 16)

            act.sem_inc(s_yo, 1)
            for q in range(2):
                act.sem_inc(s_ys[q], 1)
            rows_in(0, 0)
            with nc.scalar.Fori(0, E // 2 - 1) as ep:
                expert(0, 2 * ep, False)
                expert(1, 2 * ep + 1, False)
            expert(0, E - 2, False)
            expert(1, E - 1, True)

        @block.vector
        def _(dve):
            done = [0]

            def own(*instructions):
                for ins in instructions:
                    ins.then_inc(s_r, 1)
                done[0] += len(instructions)
                dve.wait_ge(s_r, done[0])

            wide = [P, NT, E]
            own(nc.vector.tensor_reduce(red[:], logits[:], AX.X, ALU.max))
            own(nc.vector.tensor_tensor(sc[:], logits[:], red[:].unsqueeze(2).to_broadcast(wide), ALU.subtract))
            assert done[0] == R_SHIFT
            dve.wait_ge(s_ex, 1)
            own(nc.vector.tensor_reduce(red[:], sc[:], AX.X, ALU.add))
            own(nc.vector.reciprocal(red[:], red[:]))
            own(nc.vector.tensor_tensor(sc[:], sc[:], red[:].unsqueeze(2).to_broadcast(wide), ALU.mult))
            dve.wait_ge(s_in, 48)
            own(nc.vector.tensor_tensor(sc[:], sc[:], gate_b[:].unsqueeze(1).to_broadcast(wide), ALU.add))
            own(*[nc.vector.max(best[:, t, :], sc[:, t, :]) for t in range(NT)])
            own(*[nc.vector.max_index(best_i[:, t, :], best[:, t, :], sc[:, t, :]) for t in range(NT)])
            own(nc.vector.tensor_copy(pick[:], best_i[:, :, 0:2]))
            for k in range(2):
                own(nc.vector.tensor_tensor(onehot[:, k], pick[:, :, k:k + 1].to_broadcast(wide),
                                            c["expert_index"][:].unsqueeze(1).to_broadcast(wide), ALU.is_equal))
                own(nc.vector.tensor_tensor(prod[:], onehot[:, k], logits[:], ALU.mult))
                own(nc.vector.tensor_reduce(gate[:, k, :], prod[:], AX.X, ALU.add))
            own(nc.vector.tensor_tensor(queue[:], onehot[:, 0], onehot[:, 1], ALU.add))
            own(nc.vector.tensor_tensor(prod[:], queue[:], logits[:], ALU.mult))
            own(nc.vector.tensor_scalar(queue[:], queue[:], -NOT_MINE, NOT_MINE, ALU.mult, ALU.add))
            own(nc.vector.tensor_tensor(queue[:], queue[:], prod[:], ALU.add))
            assert done[0] == R_QUEUE, done[0]
            own(nc.vector.memset(part[:], 0.0))

            def rank_row(r):
                t, k = r // 2, r % 2
                w = own_w[:, k, t:t + 1]
                a, b = t * P, (t + 1) * P
                row = ps[:, 0:2, :].rearrange("p b n -> p (b n)")
                dve.wait_ge(s_row_mm, r + 1)
                own(nc.vector.scalar_tensor_tensor(junk[:, a:b], row[:, a:b], 1.0, c["ident"][:], ALU.mult, ALU.mult,
                                                   accum_out=w))
                ins = []
                if t > 0:
                    ins.append(nc.vector.tensor_scalar(junk[:, 0:a], row[:, 0:a], w, None, ALU.is_ge, ALU.add,
                                                       accum_out=part[:, k, t, 0:1]))
                if t < NT - 1:
                    ins.append(nc.vector.tensor_scalar(junk[:, b:N], row[:, b:N], w, None, ALU.is_gt, ALU.add,
                                                       accum_out=part[:, k, t, 1:2]))
                ins.append(nc.vector.scalar_tensor_tensor(junk[:, a:b], row[:, a:b], w, c["lower"][:], ALU.is_ge,
                                                          ALU.mult, accum_out=part[:, k, t, 2:3]))
                own(*ins)
                own(nc.vector.scalar_tensor_tensor(junk[:, a:b], row[:, a:b], w, c["upper"][:], ALU.is_gt,
                                                   ALU.mult, accum_out=part[:, k, t, 3:4]))
                nc.vector.tensor_copy(own_w[:, k, t:t + 1], own_w[:, k, t:t + 1]).then_inc(s_row, 1)

            def slots():
                dve.wait_ge(s_row, 2 * NT)
                own(nc.vector.tensor_reduce(rank[:], part[:], AX.X, ALU.add))
                own(nc.vector.tensor_scalar(keep[:], rank[:], float(CAP), None, ALU.is_lt))
                own(nc.vector.scalar_tensor_tensor(slot[:], pick[:].rearrange("p t k -> p k t"), float(CAP), rank[:],
                                                   ALU.mult, ALU.add))
                own(nc.vector.scalar_tensor_tensor(slot[:], slot[:], float(-E * CAP), keep[:], ALU.add, ALU.mult))
                own(nc.vector.tensor_scalar(slot[:], slot[:], float(E * CAP), None, ALU.add))
                nc.vector.tensor_copy(slot_i[:], slot[:]).then_inc(s_slot, 1)

            step = 0
            for hf, s in units:
                for m in range(MH):
                    if FIRST_ROW <= step < FIRST_ROW + 2 * NT:
                        rank_row(step - FIRST_ROW)
                    if step == FIRST_ROW + 2 * NT:
                        slots()
                    dve.wait_ge(s_sl, step + 1)
                    nc.vector.tensor_tensor(hT[:, m, :], sl[step % 2][:], ps[:, 3 + 2 * (step % 2), :],
                                            ALU.mult).then_inc(s_h, 1)
                    step += 1
                for t in range(4):
                    n = 4 * (2 * s + hf) + t
                    dve.wait_ge(s_y_mm, n + 1)
                    if n >= 8:
                        dve.wait_ge(s_y, n - 7)
                    nc.vector.scalar_tensor_tensor(xres[:, 4 * hf + t, :], ps[:, 6 + n % 2, :], 0.5,
                                                   xres[:, 4 * hf + t, :], ALU.mult, ALU.add).then_inc(s_y, 1)

            def expert(q, e):
                for m in range(MH):
                    dve.wait_ge(s_esl, MH * e + m + 1)
                    nc.vector.tensor_tensor(eT[q][:, m, :], sl[m % 2][:, 0:CAP], ps[:, 2 + m % 3, CAP:2 * CAP],
                                            ALU.mult).then_inc(s_e, 1)
                for half in range(2):
                    dve.wait_ge(s_yT_mm, 2 * e + half + 1)
                    nc.vector.tensor_copy(yT[:, 2 * half:2 * half + 2, :].rearrange("p k s -> p (k s)"),
                                          ps[:, 5 + half, 0:2 * CAP]).then_inc(s_yT, 1)

            with nc.vector.Fori(0, E // 2) as ep:
                for q in range(2):
                    expert(q, 2 * ep + q)
            dve.wait_ge(s_y, 16)
            for t in range(NT):
                dve.wait_ge(s_g[t % 2], 32 * (t // 2 + 1))
                for k in range(2):
                    if k:
                        dve.wait_ge(s_f, 2 * t + 1)
                    nc.vector.scalar_tensor_tensor(xres[:, t, :], gathered[:, t % 2, k, :], gate[:, k, t:t + 1], xres[:, t, :],
                                                   ALU.mult, ALU.add).then_inc(s_f, 1)


R_SHIFT = 2
R_QUEUE = 33


def perceiver_kernel(nc, d):
    with ExitStack() as ctx:
        def sb(name, shape, dt=F32):
            return ctx.enter_context(nc.sbuf_tensor(name, shape, dt))

        def sem(name):
            return ctx.enter_context(nc.semaphore(name))

        xf_d = nc.dram_tensor("xf_scratch", (N, D), F32, kind="Internal").ap()
        xfT_d = nc.dram_tensor("xfT_scratch", (D, N), F32, kind="Internal").ap()
        xs_d = nc.dram_tensor("queue_rows", (E * CAP, D), F32, kind="Internal").ap()
        ys_d = nc.dram_tensor("expert_rows", (E * CAP + 1, D), F32, kind="Internal").ap()
        xres = sb("xres", [P, NT, D])
        logits = sb("logits", [P, NT, E])
        zeros = sb("zeros", [P, D])
        c = constants(nc, sb, sem, d)
        s_const = sem("constants")
        s_x = sem("x_in")
        s_z = sem("zeros")
        s_xf_d = sem("xf_to_dram")
        s_zero_d = sem("zero_rows")

        with nc.Block() as block:
            n_const = [0]

            @block.gpsimd
            def _(pool):
                n_const[0] = build_constants(nc, c, s_const)
                pool.memset(zeros[:], 0.0).then_inc(s_z, 1)

        def zero_rows(sp):
            sp.wait_ge(s_z, 1)
            sp.dma_start(xs_d.rearrange("(a p) n -> p a n", p=P),
                         zeros[:].unsqueeze(1).to_broadcast([P, E * CAP // P, D])).then_inc(s_zero_d, 16)
            sp.dma_start(ys_d[E * CAP:E * CAP + 1, :], zeros[0:1, :]).then_inc(s_zero_d, 16)

        attention_block(nc, d, c, s_const, n_const[0], xres, s_x)
        mamba_block(nc, d, c, s_const, n_const[0], xres, xf_d, xfT_d, logits, s_xf_d, zero_rows)
        ffn_block(nc, d, c, xres, xf_d, xfT_d, xs_d, ys_d, logits, s_xf_d, s_zero_d)


def kernel(**inputs):
    import numpy as np
    import concourse.bacc as bacc
    from concourse.bass_utils import run_bass_kernel_spmd

    a = {k: np.asarray(v) for k, v in inputs.items()}

    def by_channel(v):
        return v.reshape(MC, P).T

    pair = a["ctx_1024"].reshape(NB // 2, 2, KS, P, KD, P)
    w_x = np.zeros((C, 96), np.float32)
    for n in range(3):
        w_x[:, 32 * n:32 * n + NS] = a["L0_attn_W_xproj"][:, NS * n:NS * (n + 1)]
    chan = np.stack([by_channel(a["L0_attn_conv_w"][:, j]) for j in range(4)] + [
        by_channel(a["L0_attn_conv_b"]), by_channel(np.repeat(a["L0_attn_A_log"], C // 16)),
        by_channel(np.repeat(a["L0_attn_D_skip"], C // 16)), by_channel(a["L0_attn_ln_g"]),
        by_channel(a["L0_attn_ln_b"])], axis=2)
    host = {
        "x": a["x"].reshape(N, D),
        "ctx": pair.transpose(0, 1, 3, 2, 4, 5).reshape(NB // 2, 2, P, KS, D),
        "ctxT": pair.transpose(0, 1, 5, 4, 2, 3).reshape(NB // 2, 2, P, KD, SK),
        "wq1T": a["L0_xattn_Wq1"].T, "wk1T": a["L0_xattn_Wk1"].T, "wv1": a["L0_xattn_Wv1"],
        "wq2T": a["L0_xattn_Wq2"].T, "wk2T": a["L0_xattn_Wk2"].T, "wv2": a["L0_xattn_Wv2"],
        "fc1_w": a["L0_xattn_fc1_w"], "fc1_b": a["L0_xattn_fc1_b"].reshape(KD, P).T,
        "fc2_w": a["L0_xattn_fc2_w"], "fc2_b": a["L0_xattn_fc2_b"].reshape(1, D),
        "ln": np.stack([a[f"L0_xattn_ln{n}_{k}"] for n in (1, 2, 3) for k in "gb"]),
        "w_in": a["L0_attn_W_in"], "w_x": w_x,
        "w_dt": np.concatenate([a["L0_attn_W_dt"], a["L0_attn_b_dt"].reshape(1, C)], axis=0),
        "chan": chan, "w_out": a["L0_attn_W_out"],
        "gate_w": a["L0_ffn_gate_w"], "gate_b": a["L0_ffn_gate_b"],
        "ew1": a["L0_ffn_ew1"], "ew3": a["L0_ffn_ew3"], "ew2": a["L0_ffn_ew2"],
        "sw1": a["L0_ffn_sw1"], "sw3": a["L0_ffn_sw3"], "sw2": a["L0_ffn_sw2"],
    }
    nc = bacc.Bacc("TRN2", target_bir_lowering=False, num_devices=1)
    arrays, d = {}, {}
    for name, v in host.items():
        arrays["in_" + name] = np.ascontiguousarray(v)
        d[name] = nc.dram_tensor("in_" + name, v.shape, mybir.dt.from_np(v.dtype), kind="ExternalInput").ap()
    out = nc.dram_tensor("out_0", (N, D), F32, kind="ExternalOutput").ap()
    d["out"] = out
    perceiver_kernel(nc, d)
    r = run_bass_kernel_spmd(nc, [arrays], core_ids=[0])
    return r.results[0]["out_0"].reshape(NB, L, D)
```

```python
from contextlib import ExitStack

import concourse.bass as bass
from concourse import mybir

F32 = mybir.dt.float32
U32 = mybir.dt.uint32
ALU = mybir.AluOpType
ACT = mybir.ActivationFunctionType
AX = mybir.AxisListType

P = 128
D = 512
KD = D // P
NB = 16
L = 64
N = NB * L
NT = N // P
SK = 512
KA = 3
KS = SK // P
C = 1024
MC = C // P
NS = 16
Q = 8
E = 16
H = 1024
MH = H // P
CAP = 160
SCALE = float(1.0 / (32.0 ** 0.5))
EPS = 1e-5
BIG = -1.0e30
NOT_MINE = -3.0e38


def constants(nc, sb, sem, d):
    c = {}
    c["ident"] = sb("ident", [P, P])
    c["ones"] = sb("ones", [P, P])
    c["ones_over_c"] = sb("ones_over_c", [P, P])
    c["causal"] = sb("causal", [P, P])
    c["same_batch"] = sb("same_batch", [P, P])
    c["first_row"] = sb("first_row", [P, P])
    c["key_in_batch"] = sb("key_in_batch", [P, P])
    c["key_index"] = sb("key_index", [P, SK])
    c["expert_index"] = sb("expert_index", [P, E])
    c["own_chunk"] = sb("own_chunk", [P, 16, NS])
    c["next_chunk"] = sb("next_chunk", [P, Q, Q])
    c["rep_state"] = sb("rep_state", [NS, Q, NS])
    c["lower"] = sb("lower", [P, P])
    c["upper"] = sb("upper", [P, P])
    c["minus_half"] = sb("minus_half", [P, 2])
    c["eps"] = sb("eps", [P, 2])
    return c


def build_constants(nc, c, s_const):
    pool = nc.gpsimd
    n = [0]

    def put(ins, wait=False):
        ins.then_inc(s_const, 1)
        n[0] += 1
        if wait:
            pool.wait_ge(s_const, n[0])

    def select(t, out, pattern, base, mult, op, fill):
        put(pool.affine_select(out=out, in_=out, compare_op=op, fill=fill, base=base,
                               pattern=pattern, channel_multiplier=mult), wait=True)

    for name in ("ones", "same_batch", "causal", "first_row", "own_chunk", "next_chunk", "rep_state",
                 "lower", "upper"):
        put(pool.memset(c[name][:], 1.0))
    put(pool.memset(c["ident"][:], 0.0))
    put(pool.memset(c["ones_over_c"][:], 1.0 / C))
    put(pool.memset(c["minus_half"][:], -0.5))
    put(pool.memset(c["eps"][:], EPS))
    for name, pat in (("key_in_batch", [[0, 2], [1, L]]), ("key_index", [[1, SK]]), ("expert_index", [[1, E]])):
        put(pool.iota(c[name][:], pattern=pat, base=0, channel_multiplier=0,
                      allow_small_or_imprecise_dtypes=True))
    pool.wait_ge(s_const, n[0])
    select(c, c["ident"][:], [[-1, P]], 0, 1, ALU.not_equal, 1.0)
    sbm = c["same_batch"][:].rearrange("p (b j) -> p b j", b=2)
    select(c, sbm, [[-L, 2], [0, L]], 0, 1, ALU.is_ge, 0.0)
    select(c, sbm, [[L, 2], [0, L]], L - 1, -1, ALU.is_ge, 0.0)
    cm = c["causal"][:]
    select(c, cm, [[1, P]], 0, -1, ALU.is_gt, 0.0)
    put(pool.memset(c["causal"][L:P, 0:L], 1.0), wait=True)
    fr = c["first_row"][:].rearrange("p (b j) -> p b j", b=2)
    select(c, fr, [[-L, 2], [0, L]], 0, 1, ALU.is_equal, 0.0)
    oc = c["own_chunk"][:]
    select(c, oc, [[-Q, 16], [0, NS]], 0, 1, ALU.is_ge, 0.0)
    select(c, oc, [[Q, 16], [0, NS]], Q - 1, -1, ALU.is_ge, 0.0)
    nx = c["next_chunk"][:]
    select(c, nx, [[-NS, Q], [0, Q]], NS, 1, ALU.is_ge, 0.0)
    select(c, nx, [[NS, Q], [0, Q]], -1, -1, ALU.is_ge, 0.0)
    select(c, c["rep_state"][:], [[0, Q], [-1, NS]], 0, 1, ALU.is_equal, 0.0)
    select(c, c["lower"][:], [[-1, P]], 0, 1, ALU.is_gt, 0.0)
    select(c, c["upper"][:], [[1, P]], 0, -1, ALU.is_gt, 0.0)
    pool.wait_ge(s_const, n[0])
    put(pool.memset(c["lower"][0:1, 0:1], 0.0))
    return n[0]


def attention_block(nc, d, c, s_const, make_constants, xres, s_x, load_ahead):
    sems = []
    with ExitStack() as ctx:
        def sb(name, shape, dt=F32):
            return ctx.enter_context(nc.sbuf_tensor("A_" + name, shape, dt))

        def sem(name):
            sems.append(nc.alloc_semaphore(name))
            return sems[-1]

        ps = ctx.enter_context(nc.psum_tensor("psA", [P, 8, 512], F32))
        B_TR, B_V, B_E, B_LEN = 0, 1, 2, 3
        B_E2, B_C, B_Z, B_LEN2 = 4, 5, 6, 7
        wqk = [sb(f"wqk{a}", [P, KD, D]) for a in range(2)]
        wv1 = sb("wv1", [P, KD, D])
        wv2 = sb("wv2", [P, KD, D])
        fc1 = sb("fc1", [P, KD, D])
        fc2 = sb("fc2", [P, KD, D])
        fc1_b = sb("fc1_b", [P, KD])
        fc2_b = sb("fc2_b", [1, D])
        ln = sb("ln_gb", [P, 6, D])
        ctx_kd = [sb(f"ctx_kd{q}", [P, 2, KS, D]) for q in range(2)]
        ctx_dk = [sb(f"ctx_dk{q}", [P, 2, KD, SK]) for q in range(2)]
        wqT, wkT = [ctx_dk[1][:, 0], ctx_kd[1][:, 0]], [ctx_dk[1][:, 1], ctx_kd[1][:, 1]]
        xn = sb("xn", [P, D])
        tT = sb("tT", [P, KD, P])
        q1T = sb("q1T", [P, KD, P])
        v1 = sb("v1", [P, D])
        msk1 = sb("msk1", [P, P])
        pr1 = sb("pr1", [P, P])
        pr1T = sb("pr1T", [P, P])
        x1 = [sb(f"x1_{q}", [P, D]) for q in range(2)]
        q2T = [sb(f"q2T_{q}", [P, KD, P]) for q in range(2)]
        msk2 = sb("msk2", [P, SK])
        pr2 = sb("pr2", [P, SK])
        pr2T = sb("pr2T", [P, KS, P])
        cT = pr2T
        x2 = sb("x2", [P, D])
        uT = sb("uT", [P, KD, P])
        hT = uT
        x3 = msk2
        bst = [sb(f"bst{n}", [P, 6]) for n in range(4)]
        mv = [sb(f"mv{n}", [P, 2]) for n in range(4)]
        ve = [sb(f"ve{n}", [P, 1]) for n in range(4)]
        rstd = [sb(f"rstd{n}", [P, 1]) for n in range(4)]
        cnt = [sb(f"cnt{n}", [P, 1]) for n in range(2)]
        top = [sb(f"top{n}", [P, 1]) for n in range(2)]
        nmx = [sb(f"nmx{n}", [P, 1]) for n in range(2)]
        rsum = [sb(f"rsum{n}", [P, 1]) for n in range(2)]
        rinv = [sb(f"rinv{n}", [P, 1]) for n in range(2)]

        s_w = {k: sem("A_" + k) for k in ("w0", "w1", "v1", "rest", "ln")}
        s_dk = [sem(f"A_ctx_dk{q}") for q in range(2)]
        s_kd = [sem(f"A_ctx_kd{q}") for q in range(2)]
        s_wqk_mm = sem("A_wqk_mm")
        s_wqk = sem("A_wqk")
        s_var = [sem(f"A_var{n}") for n in range(4)]
        s_ve = [sem(f"A_ve{n}") for n in range(4)]
        s_rstd = [sem(f"A_rstd{n}") for n in range(4)]
        s_xn = sem("A_xn")
        s_tr = sem("A_tr")
        s_tT = sem("A_tT")
        s_q_mm = sem("A_q_mm")
        s_q = sem("A_q")
        s_v_mm = sem("A_v_mm")
        s_v = sem("A_v")
        s_e = [sem(f"A_e{n}") for n in range(2)]
        s_cnt = [sem(f"A_cnt{n}") for n in range(2)]
        s_len = [sem(f"A_len{n}") for n in range(2)]
        s_bias = [sem(f"A_bias{n}") for n in range(2)]
        s_exp = [sem(f"A_exp{n}") for n in range(2)]
        s_pT_mm = [sem(f"A_pT_mm{n}") for n in range(2)]
        s_pT = [sem(f"A_pT{n}") for n in range(2)]
        s_z1 = sem("A_z1")
        s_x1 = sem("A_x1")
        s_c_mm = sem("A_c_mm")
        s_c = sem("A_c")
        s_z2 = sem("A_z2")
        s_x2 = sem("A_x2")
        s_tr2 = sem("A_tr2")
        s_uT = sem("A_uT")
        s_f1_mm = sem("A_f1_mm")
        s_h = sem("A_h")
        s_z3 = sem("A_z3")
        s_done = sem("A_done")
        s_own0, s_own1, s_own2, s_own3 = (sem(f"A_own{n}") for n in range(4))
        s_gain1 = sem("A_gain1")
        s_gain2 = sem("A_gain2")
        s_y3 = sem("A_y3")
        s_ownf = sem("A_ownf")
        s_ownb = sem("A_ownb")
        s_passed = sem("A_waits_passed")
        block = ctx.enter_context(nc.Block())

        def stand_alone(eng):
            eng.sem_inc(s_passed, 1)

        def steps(engine, prologue, step):
            prologue()
            with engine.Fori(0, NT // 2 - 1) as g:
                step(2 * g, 0, True)
                step(2 * g + 1, 1, True)
            step(NT - 2, 0, True)
            step(NT - 1, 1, False)

        def w_view(w):
            return w.rearrange("(k p) n -> p k n", p=P)

        @block.sync
        def _(sp):
            for a in range(2):
                sp.dma_start(wqT[a], w_view(d[f"wq{a + 1}T"])).then_inc(s_w[f"w{a}"], 16)
                sp.dma_start(wkT[a], w_view(d[f"wk{a + 1}T"])).then_inc(s_w[f"w{a}"], 16)
                if a == 0:
                    sp.dma_start(xres[:], d["x"].rearrange("(t p) n -> p t n", p=P)).then_inc(s_x, 16)
            sp.dma_start(wv1[:], w_view(d["wv1"])).then_inc(s_w["v1"], 16)
            for n in range(6):
                sp.dma_start(ln[:, n, :], d["ln"][n].partition_broadcast(P)).then_inc(s_w["ln"], 16)

            def load_dk(t, q):
                for h in range(2):
                    sp.dma_start(ctx_dk[q][:, h], d["ctxT"][t, h]).then_inc(s_dk[q], 16)

            def load_kd(t, q):
                for h in range(2):
                    sp.dma_start(ctx_kd[q][:, h], d["ctx"][t, h]).then_inc(s_kd[q], 16)

            load_dk(0, 0)
            load_kd(0, 0)
            sp.dma_start(wv2[:], w_view(d["wv2"])).then_inc(s_w["rest"], 16)
            sp.dma_start(fc1[:], w_view(d["fc1_w"])).then_inc(s_w["rest"], 16)
            sp.dma_start(fc2[:], w_view(d["fc2_w"])).then_inc(s_w["rest"], 16)
            sp.dma_start(fc1_b[:], d["fc1_b"]).then_inc(s_w["rest"], 16)
            sp.dma_start(fc2_b[:], d["fc2_b"]).then_inc(s_w["rest"], 16)
            sp.wait_ge(s_wqk_mm, KD)
            load_dk(1, 1)
            sp.wait_ge(s_wqk_mm, 2 * KD)
            load_kd(1, 1)
            with nc.sync.Fori(0, NT // 2 - 1) as g:
                for q in range(2):
                    sp.wait_ge(s_e[1], 2 * g + q + 1)
                    load_dk(2 * g + q + 2, q)
                    sp.wait_ge(s_c_mm, 2 * g + q + 1)
                    load_kd(2 * g + q + 2, q)
            load_ahead(sp)

        n_const = [0]

        @block.gpsimd
        def _(pool):
            n_const[0] = make_constants(pool)

            def rsqrt(n, t):
                pool.wait_ge(s_var[n], t + 1)
                nc.gpsimd.tensor_tensor(ve[n][:], mv[n][:, 1:2], c["eps"][:, 0:1], ALU.add).then_inc(s_ve[n], 1)
                pool.wait_ge(s_ve[n], t + 1)
                nc.gpsimd.tensor_tensor(rstd[n][:], ve[n][:], c["minus_half"][:, 0:1], ALU.pow).then_inc(s_rstd[n], 1)

            def prologue():
                rsqrt(0, 0)
                rsqrt(1, 0)
                rsqrt(0, 1)

            def step(t, q, more):
                rsqrt(2, t)
                if more:
                    rsqrt(1, t + 1)
                    rsqrt(0, t + 2)
                rsqrt(3, t)

            def last(t, q, more):
                rsqrt(2, t)
                if more:
                    rsqrt(1, t + 1)
                rsqrt(3, t)

            prologue()
            with nc.gpsimd.Fori(0, NT // 2 - 1) as g:
                step(2 * g, 0, True)
                step(2 * g + 1, 1, True)
            last(NT - 2, 0, True)
            last(NT - 1, 1, False)

        @block.tensor
        def _(pe):
            def weight_product(a, m):
                for k in range(KD):
                    mm = nc.tensor.matmul(ps[:, 4 * a + m, :], wqT[a][:, k, m * P:(m + 1) * P], wkT[a][:, k, :],
                                          start=(k == 0), stop=(k == KD - 1))
                mm.then_inc(s_wqk_mm, 1)

            pe.wait_ge(s_w["w0"], 32)
            for m in range(KD):
                weight_product(0, m)
            pe.wait_ge(s_const, n_const[0])
            pe.wait_ge(s_wqk, KD)

            def transposes(bank, src, s):
                for k in range(KD):
                    mm = nc.tensor.transpose(ps[:, bank, k * P:(k + 1) * P], src[:, k * P:(k + 1) * P], c["ident"][:])
                mm.then_inc(s, 1)

            def widths_out(bank, w, src, s):
                for m in range(KD):
                    for k in range(KD):
                        mm = nc.tensor.matmul(ps[:, bank, m * P:(m + 1) * P], w[:, k, m * P:(m + 1) * P], src[:, k, :],
                                              start=(k == 0), stop=(k == KD - 1))
                mm.then_inc(s, 1)

            def xn_transposed(t):
                pe.wait_ge(s_xn, t + 1)
                transposes(B_TR, xn, s_tr)

            def queries(t):
                pe.wait_ge(s_tT, 2 * t + 1)
                widths_out(B_TR, wqk[0], tT, s_q_mm)

            def values(t):
                for k in range(KD):
                    mm = nc.tensor.matmul(ps[:, B_V, :], tT[:, k, :], wv1[:, k, :], start=(k == 0), stop=(k == KD - 1))
                mm.then_inc(s_v_mm, 1)

            def energies(t):
                pe.wait_ge(s_q, 2 * t + 1)
                for k in range(KD):
                    mm = nc.tensor.matmul(ps[:, B_E, 0:P], q1T[:, k, :], tT[:, k, :], start=(k == 0), stop=(k == KD - 1))
                mm.then_inc(s_e[0], 1)

            def keys_that_count(n, bank, t):
                pe.wait_ge(s_cnt[n], t + 1)
                nc.tensor.matmul(ps[:, bank, 0:1], c["first_row"][:], cnt[n][:], start=True, stop=True).then_inc(s_len[n], 1)

            def probabilities_transposed(t):
                pe.wait_ge(s_exp[0], t + 1)
                nc.tensor.transpose(ps[:, B_E, 0:P], pr1[:], c["ident"][:]).then_inc(s_pT_mm[0], 1)

            def attend(t):
                pe.wait_ge(s_pT[0], t + 1)
                pe.wait_ge(s_v, t + 1)
                nc.tensor.matmul(ps[:, B_V, :], pr1T[:], v1[:], start=True, stop=True).then_inc(s_z1, 1)

            def x1_transposed(t, q):
                pe.wait_ge(s_x1, t + 1)
                transposes(B_TR, x1[q], s_tr)

            def cross_queries(t):
                pe.wait_ge(s_tT, 2 * t + 2)
                widths_out(B_TR, wqk[1], tT, s_q_mm)

            def cross_energies(t, q):
                pe.wait_ge(s_q, 2 * t + 2)
                pe.wait_ge(s_dk[q], 16 * (t - q) + 32)
                for k in range(KD):
                    for h in range(2):
                        mm = nc.tensor.matmul(ps[h * L:(h + 1) * L, B_E2, :], q2T[q][:, k, h * L:(h + 1) * L],
                                              ctx_dk[q][:, h, k, :], start=(k == 0), stop=(k == KD - 1))
                mm.then_inc(s_e[1], 1)

            def cross_probabilities_transposed(t):
                pe.wait_ge(s_exp[1], t + 1)
                for b in range(KS):
                    mm = nc.tensor.transpose(ps[:, B_E2, b * P:(b + 1) * P], pr2[:, b * P:(b + 1) * P], c["ident"][:])
                mm.then_inc(s_pT_mm[1], 1)

            def contexts(t, q, h):
                if h == 0:
                    pe.wait_ge(s_pT[1], t + 1)
                    pe.wait_ge(s_kd[q], 16 * (t - q) + 32)
                for m in range(KD):
                    for b in range(KS):
                        o = m * P + h * L
                        mm = nc.tensor.matmul(ps[:, B_C, o:o + L], ctx_kd[q][:, h, b, m * P:(m + 1) * P],
                                              pr2T[:, b, h * L:(h + 1) * L], start=(b == 0), stop=(b == KS - 1))
                if h == 1:
                    mm.then_inc(s_c_mm, 1)

            def cross_values(t):
                pe.wait_ge(s_c, t + 1)
                for k in range(KD):
                    mm = nc.tensor.matmul(ps[:, B_Z, :], cT[:, k, :], wv2[:, k, :], start=(k == 0), stop=(k == KD - 1))
                mm.then_inc(s_z2, 1)

            def x2_transposed(t):
                pe.wait_ge(s_x2, t + 1)
                transposes(B_C, x2, s_tr2)

            def hidden(t):
                pe.wait_ge(s_uT, t + 1)
                widths_out(B_C, fc1, uT, s_f1_mm)

            def feed_forward(t):
                pe.wait_ge(s_h, 4 * t + 4)
                for k in range(KD):
                    nc.tensor.matmul(ps[:, B_Z, :], hT[:, k, :], fc2[:, k, :], start=(k == 0), stop=False)
                nc.tensor.matmul(ps[:, B_Z, :], c["ones"][0:1, :], fc2_b[0:1, :], start=False,
                                 stop=True).then_inc(s_z3, 1)

            def prologue():
                xn_transposed(0)
                pe.wait_ge(s_w["w1"], 32)
                weight_product(1, 0)
                pe.wait_ge(s_w["v1"], 16)
                queries(0)
                values(0)
                weight_product(1, 1)
                energies(0)
                weight_product(1, 2)
                keys_that_count(0, B_LEN, 0)
                weight_product(1, 3)
                probabilities_transposed(0)
                attend(0)
                x1_transposed(0, 0)
                pe.wait_ge(s_wqk, 2 * KD)
                cross_queries(0)
                pe.wait_ge(s_w["rest"], 16 * 5)

            def step(t, q, more):
                cross_energies(t, q)
                if more:
                    xn_transposed(t + 1)
                keys_that_count(1, B_LEN2, t)
                if more:
                    queries(t + 1)
                cross_probabilities_transposed(t)
                if more:
                    energies(t + 1)
                contexts(t, q, 0)
                if more:
                    keys_that_count(0, B_LEN, t + 1)
                contexts(t, q, 1)
                if more:
                    probabilities_transposed(t + 1)
                cross_values(t)
                if more:
                    values(t + 1)
                x2_transposed(t)
                if more:
                    attend(t + 1)
                hidden(t)
                if more:
                    x1_transposed(t + 1, 1 - q)
                    cross_queries(t + 1)
                feed_forward(t)

            steps(nc.tensor, prologue, step)

        @block.scalar
        def _(act):
            def weight_product(a, m):
                act.wait_ge(s_wqk_mm, KD * a + m + 1)
                nc.scalar.copy(wqk[a][:, m, :], ps[:, 4 * a + m, :]).then_inc(s_wqk, 1)

            for m in range(KD):
                weight_product(0, m)

            def flat(t):
                return t[:].rearrange("p k t -> p (k t)")

            def copy_of(s_ready, n, dst, bank, s_out):
                act.wait_ge(s_ready, n)
                nc.scalar.copy(flat(dst), ps[:, bank, :]).then_inc(s_out, 1)

            def softmax(n, t):
                act.wait_ge(s_bias[n], t + 1)
                nc.scalar.activation((pr1, pr2)[n][:], (msk1, msk2)[n][:], ACT.Exp, bias=nmx[n][:], scale=SCALE,
                                     accum_out=rsum[n][:]).then_inc(s_exp[n], 1)

            def probabilities(t):
                act.wait_ge(s_pT_mm[0], t + 1)
                nc.scalar.copy(pr1T[:], ps[:, B_E, 0:P]).then_inc(s_pT[0], 1)

            def relu(t):
                act.wait_ge(s_f1_mm, t + 1)
                for m in range(KD):
                    nc.scalar.activation(hT[:, m, :], ps[:, B_C, m * P:(m + 1) * P], ACT.Relu,
                                         bias=fc1_b[:, m:m + 1]).then_inc(s_h, 1)

            def prologue():
                copy_of(s_tr, 1, tT, B_TR, s_tT)
                weight_product(1, 0)
                copy_of(s_q_mm, 1, q1T, B_TR, s_q)
                weight_product(1, 1)
                weight_product(1, 2)
                softmax(0, 0)
                weight_product(1, 3)
                probabilities(0)
                copy_of(s_tr, 2, tT, B_TR, s_tT)
                copy_of(s_q_mm, 2, q2T[0], B_TR, s_q)
                act.wait_ge(s_w["rest"], 16 * 5)

            def step(t, q, more):
                if more:
                    copy_of(s_tr, 2 * t + 3, tT, B_TR, s_tT)
                softmax(1, t)
                if more:
                    copy_of(s_q_mm, 2 * t + 3, q1T, B_TR, s_q)
                copy_of(s_pT_mm[1], t + 1, pr2T, B_E2, s_pT[1])
                if more:
                    softmax(0, t + 1)
                copy_of(s_c_mm, t + 1, cT, B_C, s_c)
                if more:
                    probabilities(t + 1)
                copy_of(s_tr2, t + 1, uT, B_C, s_uT)
                relu(t)
                if more:
                    copy_of(s_tr, 2 * t + 4, tT, B_TR, s_tT)
                    copy_of(s_q_mm, 2 * t + 4, q2T[1 - q], B_TR, s_q)

            steps(nc.scalar, prologue, step)

        OWN_F, OWN_B = 5, 7

        @block.vector
        def _(dve):
            dve.wait_ge(s_x, 16)

            def statistics(n, src, s_own, count):
                stand_alone(dve)
                nc.vector.bn_stats(bst[n][:], src).then_inc(s_own, 1)
                dve.wait_ge(s_own, count)
                stand_alone(dve)

            def aggregate(n):
                nc.vector.bn_aggr(mv[n][:], bst[n][:]).then_inc(s_var[n], 1)

            def affine(n, src, dst, t, s_own, count, s_out):
                dve.wait_ge(s_var[n], t + 1)
                nc.vector.scalar_tensor_tensor(dst, src, mv[n][:, 0:1], ln[:, 2 * n - 2, :], ALU.subtract,
                                               ALU.mult).then_inc(s_own, 1)
                dve.wait_ge(s_rstd[n], t + 1)
                dve.wait_ge(s_own, count)
                nc.vector.scalar_tensor_tensor(dst, dst, rstd[n][:], ln[:, 2 * n - 1, :], ALU.mult,
                                               ALU.add).then_inc(s_out, 1)

            def input_statistics(t):
                statistics(0, xres[:, t, :], s_own0, t + 1)
                aggregate(0)

            def input_norm(t):
                dve.wait_ge(s_rstd[0], t + 1)
                dve.wait_ge(s_var[0], t + 1)
                nc.vector.tensor_scalar(xn[:], xres[:, t, :], mv[0][:, 0:1], rstd[0][:], ALU.subtract,
                                        ALU.mult).then_inc(s_xn, 1)

            def values(t):
                dve.wait_ge(s_v_mm, t + 1)
                nc.vector.tensor_copy(v1[:], ps[:, B_V, :]).then_inc(s_v, 1)

            def count_keys(t):
                dve.wait_ge(s_e[0], t + 1)
                nc.vector.scalar_tensor_tensor(msk1[:], ps[:, B_E, 0:P], 0.0, c["same_batch"][:], ALU.not_equal,
                                               ALU.mult, accum_out=cnt[0][:]).then_inc(s_cnt[0], 1)

            def mask(t):
                dve.wait_ge(s_cnt[0], t + 1)
                dve.wait_ge(s_len[0], t + 1)
                nc.vector.scalar_tensor_tensor(msk1[:], c["key_in_batch"][:], ps[:, B_LEN, 0:1], c["causal"][:],
                                               ALU.is_ge, ALU.max).then_inc(s_ownf, 1)
                dve.wait_ge(s_ownf, OWN_F * t + 1)
                nc.vector.scalar_tensor_tensor(msk1[:], msk1[:], BIG, ps[:, B_E, 0:P], ALU.mult,
                                               ALU.add).then_inc(s_ownf, 1)
                dve.wait_ge(s_ownf, OWN_F * t + 2)
                nc.vector.tensor_reduce(top[0][:], msk1[:], AX.X, ALU.max).then_inc(s_ownf, 1)
                dve.wait_ge(s_ownf, OWN_F * t + 3)
                nc.vector.tensor_scalar(nmx[0][:], top[0][:], -SCALE, None, ALU.mult).then_inc(s_bias[0], 1)

            def x1_sum(t, q):
                dve.wait_ge(s_exp[0], t + 1)
                nc.vector.reciprocal(rinv[0][:], rsum[0][:]).then_inc(s_ownf, 1)
                dve.wait_ge(s_ownf, OWN_F * t + 4)
                dve.wait_ge(s_z1, t + 1)
                nc.vector.scalar_tensor_tensor(x1[q][:], ps[:, B_V, :], rinv[0][:], xn[:], ALU.mult,
                                               ALU.add).then_inc(s_ownf, 1)
                dve.wait_ge(s_ownf, OWN_F * t + 5)
                statistics(1, x1[q][:], s_own1, t + 1)
                aggregate(1)

            def count_cross_keys(t):
                dve.wait_ge(s_e[1], t + 1)
                nc.vector.tensor_scalar(msk2[:], ps[:, B_E2, :], 0.0, None, ALU.not_equal, ALU.add,
                                        accum_out=cnt[1][:]).then_inc(s_cnt[1], 1)

            def cross_mask(t):
                dve.wait_ge(s_cnt[1], t + 1)
                dve.wait_ge(s_len[1], t + 1)
                nc.vector.tensor_scalar(msk2[:], c["key_index"][:], ps[:, B_LEN2, 0:1], BIG, ALU.is_ge,
                                        ALU.mult).then_inc(s_ownb, 1)
                dve.wait_ge(s_ownb, OWN_B * t + 1)
                nc.vector.tensor_tensor(msk2[:], msk2[:], ps[:, B_E2, :], ALU.add).then_inc(s_ownb, 1)
                dve.wait_ge(s_ownb, OWN_B * t + 2)
                nc.vector.tensor_reduce(top[1][:], msk2[:], AX.X, ALU.max).then_inc(s_ownb, 1)
                dve.wait_ge(s_ownb, OWN_B * t + 3)
                nc.vector.tensor_scalar(nmx[1][:], top[1][:], -SCALE, None, ALU.mult).then_inc(s_bias[1], 1)

            def x2_sum(t, q):
                dve.wait_ge(s_exp[1], t + 1)
                nc.vector.reciprocal(rinv[1][:], rsum[1][:]).then_inc(s_ownb, 1)
                dve.wait_ge(s_ownb, OWN_B * t + 4)
                dve.wait_ge(s_z2, t + 1)
                nc.vector.scalar_tensor_tensor(x2[:], ps[:, B_Z, :], rinv[1][:], x1[q][:], ALU.mult,
                                               ALU.add).then_inc(s_ownb, 1)
                dve.wait_ge(s_ownb, OWN_B * t + 5)
                statistics(2, x2[:], s_own2, t + 1)
                aggregate(2)

            def x3_sum(t):
                dve.wait_ge(s_x2, t + 1)
                dve.wait_ge(s_z3, t + 1)
                nc.vector.tensor_tensor(x3[:], ps[:, B_Z, :], x2[:], ALU.add).then_inc(s_ownb, 1)
                dve.wait_ge(s_ownb, OWN_B * t + 6)
                statistics(3, x3[:], s_own3, t + 1)
                aggregate(3)

            def result(t):
                affine(3, x3[:], x3[:], t, s_ownb, OWN_B * t + 7, s_y3)
                dve.wait_ge(s_y3, t + 1)
                nc.vector.tensor_tensor(xres[:, t, :], xres[:, t, :], x3[:], ALU.add).then_inc(s_done, 1)
                dve.wait_ge(s_done, t + 1)

            def prologue():
                input_statistics(0)
                input_norm(0)
                values(0)
                dve.wait_ge(s_const, n_const[0])
                count_keys(0)
                mask(0)
                x1_sum(0, 0)
                dve.wait_ge(s_w["ln"], 16 * 6)
                affine(1, x1[0][:], x1[0][:], 0, s_gain1, 1, s_x1)
                input_statistics(1)
                input_norm(1)

            def step(t, q, more, after=True):
                count_cross_keys(t)
                cross_mask(t)
                if more:
                    count_keys(t + 1)
                    mask(t + 1)
                x2_sum(t, q)
                affine(2, x2[:], x2[:], t, s_gain2, t + 1, s_x2)
                if more:
                    values(t + 1)
                    x1_sum(t + 1, 1 - q)
                    affine(1, x1[1 - q][:], x1[1 - q][:], t + 1, s_gain1, t + 2, s_x1)
                if after:
                    input_statistics(t + 2)
                    input_norm(t + 2)
                x3_sum(t)
                result(t)

            prologue()
            with nc.vector.Fori(0, NT // 2 - 1) as g:
                step(2 * g, 0, True)
                step(2 * g + 1, 1, True)
            step(NT - 2, 0, True, False)
            step(NT - 1, 1, False, False)
            dve.wait_ge(s_done, NT)

    nc.clear_and_free_semaphores(sems)
    nc.all_engine_barrier()


def mamba_block(nc, d, c, xres, w_in_a, s_w_in, xf_d, xfT_d, logits, s_xf_d, zero_rows, load_ahead):
    with ExitStack() as ctx:
        def sb(name, shape, dt=F32):
            return ctx.enter_context(nc.sbuf_tensor("B_" + name, shape, dt))

        def sem(name):
            return ctx.enter_context(nc.semaphore(name))

        ps = ctx.enter_context(nc.psum_tensor("psB", [P, 8, 512], F32))
        B_DT, B_CB, B_OUT, B_VAR, B_TR = 4, 6, 0, 1, 7
        B_XZ = (6, 7, 2, 3)
        B_PR, B_BT = 2, 0
        B_U = (0, 3, 1, 2)
        FIRST_PAIRS = 5
        NK = P // Q
        w_in_b = sb("w_in_b", [P, KD - KA, 2 * C])
        w_in = [w_in_a[:, k] for k in range(KA)] + [w_in_b[:, k] for k in range(KD - KA)]
        w_x = sb("w_x", [P, MC, 96])
        w_dt = sb("w_dt", [NS + 1, C])
        w_out = sb("w_out", [P, MC, D])
        gate_w = sb("gate_w", [P, KD, E])
        chan = sb("chan", [P, MC, 9])
        a_neg = sb("a_neg", [P, MC])
        b_out = sb("b_out", [P, D])
        xm = sb("xm", [P, D])
        xmT = sb("xmT", [P, KD, P])
        xe = sb("xe", [P, MC, 2, L + 3])
        zs = [sb(f"zs{q}", [P, MC, P]) for q in range(2)]
        xc = [sb(f"xc{q}", [P, MC, P]) for q in range(2)]
        dtr = sb("dtr", [NS + 1, P])
        bT = sb("bT", [NS, P])
        cTt = sb("cTt", [NS, P])
        btok = sb("btok", [P, NS])
        cb = sb("cb", [NS, Q, P])
        bd = sb("bd", [P, NK, NS])
        cd = sb("cd", [P, 2, L])
        t0 = sb("t0", [P, MC, P])
        t1 = sb("t1", [P, MC, P])
        dts = sb("dts", [P, MC, P])
        dec = sb("dec", [P, MC, P])
        v = [sb(f"v{a}", [P, MC, P]) for a in range(2)]
        tmp = sb("tmp", [P, MC, P])
        y = [sb(f"y{q}", [P, MC, P]) for q in range(2)]
        prod = [sb(f"prod{q}", [P, MC, P]) for q in range(2)]
        vend = sb("vend", [P, MC, P])
        b_rep = vend
        vT = sb("vT", [P, C])
        st = sb("st", [P, MC, NK * NS])
        stT = sb("stT", [P, 2, C])
        stmp = sb("stmp", [P, 2 * MC, NS])
        xf = sb("xf", [P, D])
        sq = vT[:].rearrange("p (m t) -> p m t", m=MC)
        xfT_tile = vT[:, 0:D].rearrange("p (k t) -> p k t", k=KD)
        in_sequence = sb("in_sequence", [P, C])
        bst = [sb(f"bst{n}", [P, 6]) for n in range(3)]
        mv = [sb(f"mv{n}", [P, 2]) for n in range(3)]
        ve = [sb(f"ve{n}", [P, 1]) for n in range(3)]
        rstd = [sb(f"rstd{n}", [P, 1]) for n in range(3)]

        s_w = sem("B_weights")
        s_chan = sem("B_chan")
        s_g = sem("B_gate_w")
        s_brep = sem("B_brep")
        s_gain = sem("B_gain")
        s_bo = sem("B_bo")
        s_aexp = sem("B_aexp")
        s_aneg = sem("B_aneg")
        s_bo_mm = sem("B_bo_mm")
        s_zero = sem("B_zero")
        s_bst = [sem(f"B_bst{n}") for n in range(3)]
        s_var = [sem(f"B_var{n}") for n in range(3)]
        s_ve = [sem(f"B_ve{n}") for n in range(3)]
        s_rstd = [sem(f"B_rstd{n}") for n in range(3)]
        s_xm = sem("B_xm")
        s_tr = sem("B_tr")
        s_xmT = sem("B_xmT")
        s_xz_mm = sem("B_xz_mm")
        s_xz = sem("B_xz")
        s_c0 = sem("B_conv_first")
        s_conv = sem("B_conv")
        s_xc = sem("B_xc")
        s_pr_mm = sem("B_pr_mm")
        s_pr = sem("B_pr")
        s_bt_mm = sem("B_bt_mm")
        s_bt = sem("B_bt")
        s_dt_mm = sem("B_dt_mm")
        s_act = sem("B_act")
        s_ln = sem("B_ln")
        s_cb = sem("B_cb")
        s_cb_mm = sem("B_cb_mm")
        s_cr_mm = sem("B_cr_mm")
        s_cd = sem("B_cd")
        s_bd = sem("B_bd")
        s_S = sem("B_S")
        s_dec = sem("B_dec")
        s_v = sem("B_v")
        s_vend = sem("B_vend")
        s_prod = sem("B_prod")
        s_vT_mm = sem("B_vT_mm")
        s_vT = sem("B_vT")
        s_u_mm = sem("B_u_mm")
        s_u = sem("B_u")
        s_st = sem("B_st")
        s_sT_mm = sem("B_sT_mm")
        s_sT = sem("B_sT")
        s_y2 = sem("B_y2")
        s_y = sem("B_y")
        s_mean = sem("B_mean")
        s_yc = sem("B_yc")
        s_sq = sem("B_sq")
        s_vcol = sem("B_vcol")
        s_out = sem("B_out")
        s_xf = sem("B_xf")
        s_trf = sem("B_trf")
        s_xfT = sem("B_xfT")
        s_lg_mm = sem("B_lg_mm")
        s_lg = sem("B_lg")
        s_front = sem("B_dve_front")
        s_chain = sem("B_dve_chain")
        s_back = sem("B_dve_back")
        s_passed = sem("B_waits_passed")

        def stand_alone(eng):
            eng.sem_inc(s_passed, 1)

        def steps(engine, prologue, step):
            prologue()
            with engine.Fori(0, NT // 2 - 1) as g:
                step(2 * g, 0, True, True)
                step(2 * g + 1, 1, True, True)
            step(NT - 2, 0, True, False)
            step(NT - 1, 1, False, False)

        def flat(t):
            return t[:].rearrange("p m t -> p (m t)")

        def banks(a, b):
            return ps[:, a:b, :].rearrange("p b n -> p (b n)")

        block = ctx.enter_context(nc.Block())

        @block.sync
        def _(sp):
            for k in range(KA, KD):
                sp.dma_start(w_in_b[:, k - KA, :], d["w_in"][k * P:(k + 1) * P, :]).then_inc(s_w_in, 16)
            sp.dma_start(chan[:], d["chan"]).then_inc(s_chan, 16)
            sp.dma_start(w_x[:], d["w_x"].rearrange("(m p) n -> p m n", p=P)).then_inc(s_w, 16)
            sp.dma_start(w_dt[:], d["w_dt"]).then_inc(s_w, 16)
            sp.dma_start(w_out[:], d["w_out"].rearrange("(m p) n -> p m n", p=P)).then_inc(s_w, 16)
            sp.dma_start(gate_w[:], d["gate_w"].rearrange("(k p) n -> p k n", p=P)).then_inc(s_g, 16)
            zero_rows(sp)
            load_ahead(sp)
            sp.sem_inc(s_xf_d, 1)
            with nc.sync.Fori(0, NT) as t:
                sp.wait_ge(s_xf, t + 1)
                sp.dma_start(xf_d.rearrange("(t p) n -> t p n", p=P)[t], xf[:]).then_inc(s_xf_d, 16)
                sp.wait_ge(s_xfT, t + 1)
                sp.dma_start(xfT_d.rearrange("(k p) (t n) -> t p k n", p=P, n=P)[t], xfT_tile).then_inc(s_xf_d, 16)
            sp.wait_ge(s_xf_d, 32 * NT + 1)

        N_W = 16 * 3

        @block.gpsimd
        def _(pool):
            pool.memset(xe[:].rearrange("p m b t -> p (m b) t")[:, :, 0:3], 0.0).then_inc(s_zero, 1)
            pool.memset(cb[:], 0.0).then_inc(s_zero, 1)
            pool.memset(dtr[:], 1.0).then_inc(s_zero, 1)
            pool.memset(in_sequence[:], 1.0).then_inc(s_zero, 1)
            pool.wait_ge(s_zero, 4)
            pool.memset(in_sequence[:].rearrange("p (a t) -> p a t", t=L)[:, :, 0:1], 0.0).then_inc(s_zero, 1)

            def rsqrt(n, t):
                pool.wait_ge(s_var[n], t + 1)
                nc.gpsimd.tensor_tensor(ve[n][:], mv[n][:, 1:2], c["eps"][:, 0:1], ALU.add).then_inc(s_ve[n], 1)
                pool.wait_ge(s_ve[n], t + 1)
                nc.gpsimd.tensor_tensor(rstd[n][:], ve[n][:], c["minus_half"][:, 0:1], ALU.pow).then_inc(s_rstd[n], 1)

            def pairs(t):
                pool.wait_ge(s_pr, 3 * t + 3)
                for j in range(Q):
                    nc.gpsimd.tensor_tensor(cb[:, j, j:P], cTt[:, j:P], bT[:, 0:P - j], ALU.mult).then_inc(s_cb, 1)

            def b_by_chunk(t):
                pool.wait_ge(s_bt, t + 1)
                nc.gpsimd.tensor_tensor(bd[:], c["own_chunk"][:], btok[:].unsqueeze(1).to_broadcast([P, NK, NS]),
                                        ALU.mult).then_inc(s_bd, 1)

            def chunk_products(t, q, distances):
                dch = dec[:].rearrange("p m (k t) -> p (m k) t", t=Q)
                pch = prod[q][:].rearrange("p m (k t) -> p (m k) t", t=Q)
                one = c["ones"][:, 0:1].unsqueeze(1).to_broadcast([P, MC * NK, 1])
                for j in distances:
                    if j == 0:
                        pool.wait_ge(s_dec, 8 * t + 8)
                        nc.gpsimd.tensor_tensor(pch[:, :, 0:1], dch[:, :, 0:1], one, ALU.mult).then_inc(s_prod, 1)
                    else:
                        pool.wait_ge(s_prod, 8 * t + j)
                        nc.gpsimd.tensor_tensor(pch[:, :, j:j + 1], pch[:, :, j - 1:j], dch[:, :, j:j + 1],
                                                ALU.mult).then_inc(s_prod, 1)
                    pool.wait_ge(s_v, 8 * t + j + 1)
                    nc.gpsimd.tensor_tensor(
                        vend[:].rearrange("p m (k t) -> p (m k) t", t=Q)[:, :, Q - 1 - j:Q - j],
                        v[j % 2][:].rearrange("p m (k t) -> p (m k) t", t=Q)[:, :, Q - 1:Q], one,
                        ALU.mult).then_inc(s_vend, 1)

            def prologue():
                rsqrt(0, 0)
                rsqrt(0, 1)
                pairs(0)
                b_by_chunk(0)
                chunk_products(0, 0, range(FIRST_PAIRS))

            def step(t, q, more, more2):
                chunk_products(t, q, range(FIRST_PAIRS, Q))
                if more2:
                    rsqrt(0, t + 2)
                if more:
                    pairs(t + 1)
                    pool.wait_ge(s_u_mm, 4 * t + 4)
                    b_by_chunk(t + 1)
                    chunk_products(t + 1, 1 - q, range(FIRST_PAIRS))
                rsqrt(1, t)
                rsqrt(2, t)

            steps(nc.gpsimd, prologue, step)

        @block.tensor
        def _(pe):
            pe.wait_ge(s_w_in, 16 * KD)

            def offset_out():
                pe.wait_ge(s_brep, MC)
                for m in range(MC):
                    mm = nc.tensor.matmul(ps[:, B_OUT, :], b_rep[:, m, :], w_out[:, m, :], start=(m == 0),
                                          stop=(m == MC - 1))
                mm.then_inc(s_bo_mm, 1)
                pe.wait_ge(s_gain, MC)
                pe.wait_ge(s_bo, 1)
                pe.wait_ge(s_zero, 5)
                pe.wait_ge(s_g, 16)

            def input_transposed(t):
                pe.wait_ge(s_xm, t + 1)
                for k in range(KD):
                    mm = nc.tensor.transpose(ps[:, B_TR, k * P:(k + 1) * P], xm[:, k * P:(k + 1) * P], c["ident"][:])
                mm.then_inc(s_tr, 1)
                pe.wait_ge(s_xmT, t + 1)

            def projections_in(parts):
                for j in parts:
                    for a in range(4):
                        m = 4 * j + a
                        for k in range(KD):
                            mm = nc.tensor.matmul(ps[:, B_XZ[j], a * P:(a + 1) * P], w_in[k][:, m * P:(m + 1) * P],
                                                  xmT[:, k, :], start=(k == 0), stop=(k == KD - 1))
                    mm.then_inc(s_xz_mm, 1)

            def projection_x(t, q, first):
                pe.wait_ge(s_xc, t + 1)
                if not first:
                    pe.wait_ge(s_bd, t)
                    pe.wait_ge(s_cd, t)
                for m in range(MC):
                    mm = nc.tensor.matmul(ps[0:96, B_PR, 0:P], w_x[:, m, :], xc[q][:, m, :], start=(m == 0),
                                          stop=(m == MC - 1))
                mm.then_inc(s_pr_mm, 1)
                pe.wait_ge(s_pr, 3 * t + 1)
                nc.tensor.matmul(ps[:, B_BT, 0:NS], bT[:], c["ident"][0:NS, 0:NS], start=True,
                                 stop=True).then_inc(s_bt_mm, 1)

            def time_steps(t):
                pe.wait_ge(s_pr, 3 * t + 2)
                for m in range(MC):
                    mm = nc.tensor.matmul(ps[:, B_DT + m // 4, (m % 4) * P:(m % 4 + 1) * P], w_dt[:, m * P:(m + 1) * P],
                                          dtr[:], start=True, stop=True)
                mm.then_inc(s_dt_mm, 1)

            def pairs(t, more):
                pe.wait_ge(s_pr, 3 * t + 3)
                nc.tensor.matmul(ps[:, 2, 0:P], c["rep_state"][:].rearrange("n k m -> n (k m)"), cTt[:],
                                 start=True, stop=True).then_inc(s_cr_mm, 1)
                if more:
                    pe.wait_ge(s_xz, 4 * t + 6)
                    pe.wait_ge(s_c0, MC * t + 2 * MC)
                for j in range(Q):
                    pe.wait_ge(s_cb, 8 * t + j + 1)
                    mm = nc.tensor.matmul(ps[:, B_CB + j // 4, (j % 4) * P:(j % 4 + 1) * P], c["ones"][0:NS, :],
                                          cb[:, j, :], start=True, stop=True)
                mm.then_inc(s_cb_mm, 1)

            def left_at_chunk_end(t, more):
                pe.wait_ge(s_vend, 8 * t + 8)
                if more:
                    pe.wait_ge(s_xz, 4 * t + 8)
                    pe.wait_ge(s_pr, 3 * t + 6)
                for a in range(2):
                    for m in range(4):
                        mm = nc.tensor.transpose(ps[:, 1 + a, m * P:(m + 1) * P], vend[:, 4 * a + m, :], c["ident"][:])
                    mm.then_inc(s_vT_mm, 1)
                pe.wait_ge(s_bd, t + 1)

            def chunk_updates(t):
                for a in range(4):
                    pe.wait_ge(s_vT, 2 * t + a // 2 + 1)
                    for m in range(2 * a, 2 * a + 2):
                        mm = nc.tensor.matmul(ps[:, B_U[a], (m % 2) * NK * NS:(m % 2 + 1) * NK * NS], vT[:, m * P:(m + 1) * P],
                                              bd[:].rearrange("p k n -> p (k n)"), start=True, stop=True)
                    mm.then_inc(s_u_mm, 1)

            def states_transposed(t):
                pe.wait_ge(s_st, t + 1)
                for b in range(2):
                    for a in range(2):
                        for m in range(4):
                            mm = nc.tensor.transpose(ps[:, 2 * b + a, m * P:(m + 1) * P],
                                                     st[:, 4 * a + m, b * P:(b + 1) * P], c["ident"][:])
                        mm.then_inc(s_sT_mm, 1)

            def from_states(t):
                pe.wait_ge(s_sT, 4 * t + 4)
                pe.wait_ge(s_cd, t + 1)
                for m in range(MC):
                    for b in range(2):
                        o = (m % 4) * P + b * L
                        mm = nc.tensor.matmul(ps[:, m // 4, o:o + L], stT[:, b, m * P:(m + 1) * P], cd[:, b, :],
                                              start=True, stop=True)
                mm.then_inc(s_y2, 1)

            def mean(t, q):
                pe.wait_ge(s_y, t + 1)
                for m in range(MC):
                    mm = nc.tensor.matmul(ps[:, 3, 0:P], c["ones_over_c"][:], y[q][:, m, :], start=(m == 0),
                                          stop=(m == MC - 1))
                mm.then_inc(s_mean, 1)

            def output(t, q, more2):
                pe.wait_ge(s_yc, t + 1)
                if more2:
                    pe.wait_ge(s_bt, t + 3)
                for m in range(MC):
                    mm = nc.tensor.matmul(ps[:, B_OUT, :], y[q][:, m, :], w_out[:, m, :], start=(m == 0), stop=(m == MC - 1))
                mm.then_inc(s_out, 1)
                pe.wait_ge(s_sq, t + 1)
                for m in range(MC):
                    mm = nc.tensor.matmul(ps[:, B_VAR, 0:1], sq[:, m, :], c["ones_over_c"][:, 0:1], start=(m == 0),
                                          stop=(m == MC - 1))
                mm.then_inc(s_vcol, 1)

            def ffn_input_transposed(t):
                pe.wait_ge(s_xf, t + 1)
                for k in range(KD):
                    mm = nc.tensor.transpose(ps[:, B_OUT, k * P:(k + 1) * P], xf[:, k * P:(k + 1) * P], c["ident"][:])
                mm.then_inc(s_trf, 1)

            def router(t):
                pe.wait_ge(s_xfT, t + 1)
                for k in range(KD):
                    mm = nc.tensor.matmul(ps[:, B_VAR, 0:E], xfT_tile[:, k, :], gate_w[:, k, :], start=(k == 0),
                                          stop=(k == KD - 1))
                mm.then_inc(s_lg_mm, 1)

            def prologue():
                input_transposed(0)
                projections_in(range(4))
                offset_out()
                projection_x(0, 0, True)
                time_steps(0)
                input_transposed(1)
                projections_in(range(2))
                pairs(0, True)
                projection_x(1, 1, False)
                time_steps(1)
                pe.wait_ge(s_pr, 6)
                projections_in(range(2, 4))

            def step(t, q, more, more2):
                left_at_chunk_end(t, more)
                chunk_updates(t)
                if more2:
                    input_transposed(t + 2)
                    projections_in([0, 1])
                states_transposed(t)
                from_states(t)
                if more:
                    pairs(t + 1, more2)
                mean(t, q)
                if more2:
                    projection_x(t + 2, q, False)
                    time_steps(t + 2)
                output(t, q, more2)
                if more2:
                    pe.wait_ge(s_pr, 3 * t + 9)
                    projections_in([2])
                ffn_input_transposed(t)
                if more2:
                    projections_in([3])
                router(t)
                pe.wait_ge(s_lg, t + 1)

            steps(nc.tensor, prologue, step)

        @block.scalar
        def _(act):
            act.wait_ge(s_chan, 16)
            act.wait_ge(s_zero, 5)

            def offset_out():
                act.wait_ge(s_w, N_W)
                for m in range(MC):
                    nc.scalar.activation(b_rep[:, m, :], c["ones"][:], ACT.Identity,
                                         scale=chan[:, m, 8:9]).then_inc(s_brep, 1)
                nc.scalar.activation(a_neg[:], chan[:, :, 5], ACT.Exp).then_inc(s_aexp, 1)
                act.wait_ge(s_bo_mm, 1)
                for m in range(MC):
                    nc.scalar.activation(w_out[:, m, :], w_out[:, m, :], ACT.Identity,
                                         scale=chan[:, m, 7:8]).then_inc(s_gain, 1)
                act.wait_ge(s_aneg, 1)

            def input_transposed(t):
                act.wait_ge(s_tr, t + 1)
                nc.scalar.copy(flat(xmT), ps[:, B_TR, :]).then_inc(s_xmT, 1)

            def projections_in(t, q, parts):
                for j in parts:
                    act.wait_ge(s_xz_mm, 4 * t + j + 1)
                    src = ps[:, B_XZ[j], :]
                    if j < 2:
                        nc.scalar.copy(xe[:, 4 * j:4 * j + 4].rearrange("p m b t -> p (m b) t")[:, :, 3:],
                                       src.rearrange("p (mb t) -> p mb t", t=L)).then_inc(s_xz, 1)
                        for a in range(4):
                            m = 4 * j + a
                            nc.scalar.activation(xc[q][:, m, :], src[:, a * P:(a + 1) * P], ACT.Identity,
                                                 bias=chan[:, m, 4:5], scale=chan[:, m, 3:4]).then_inc(s_c0, 1)
                    else:
                        nc.scalar.activation(zs[q][:, 4 * j - 8:4 * j - 4, :].rearrange("p m t -> p (m t)"), src,
                                             ACT.Silu).then_inc(s_xz, 1)

            def convolved(t, q):
                act.wait_ge(s_conv, MC * t + MC)
                nc.scalar.activation(xc[q][:], xc[q][:], ACT.Silu).then_inc(s_xc, 1)

            def projection_x(t):
                act.wait_ge(s_pr_mm, t + 1)
                nc.scalar.copy(bT[:], ps[32:32 + NS, B_PR, 0:P]).then_inc(s_pr, 1)
                nc.scalar.copy(dtr[0:NS, :], ps[0:NS, B_PR, 0:P]).then_inc(s_pr, 1)
                nc.scalar.copy(cTt[:], ps[64:64 + NS, B_PR, 0:P]).then_inc(s_pr, 1)
                act.wait_ge(s_bt_mm, t + 1)
                nc.scalar.copy(btok[:], ps[:, B_BT, 0:NS]).then_inc(s_bt, 1)

            def magnitudes(t):
                act.wait_ge(s_dt_mm, t + 1)
                nc.scalar.activation(flat(t0), banks(B_DT, B_DT + 2), ACT.Abs).then_inc(s_act, 1)

            def softplus(t):
                act.wait_ge(s_act, 2 * t + 1)
                nc.scalar.activation(t0[:], t0[:], ACT.Exp, scale=-1.0).then_inc(s_act, 1)
                act.wait_ge(s_act, 2 * t + 2)
                nc.scalar.activation(t1[:], t0[:], ACT.Ln, bias=1.0).then_inc(s_ln, 1)

            def decays(t):
                act.wait_ge(s_S, t + 1)
                for m in range(MC):
                    nc.scalar.activation(dec[:, m, :], t1[:, m, :], ACT.Exp, scale=a_neg[:, m:m + 1]).then_inc(s_dec, 1)

            def left_at_chunk_end(t):
                act.wait_ge(s_xf_d, 32 * t + 1)
                for a in range(2):
                    act.wait_ge(s_vT_mm, 2 * t + a + 1)
                    nc.scalar.copy(vT[:, a * 512:(a + 1) * 512], ps[:, 1 + a, :]).then_inc(s_vT, 1)

            def chunk_updates(t):
                for a in range(4):
                    act.wait_ge(s_u_mm, 4 * t + a + 1)
                    nc.scalar.copy(st[:, 2 * a:2 * a + 2, :], ps[:, B_U[a], :].rearrange("p (m n) -> p m n", m=2)).then_inc(s_u, 1)

            def states_transposed(t):
                for j in range(4):
                    act.wait_ge(s_sT_mm, 4 * t + j + 1)
                    nc.scalar.copy(stT[:, j // 2, (j % 2) * 512:(j % 2 + 1) * 512], ps[:, j, :]).then_inc(s_sT, 1)

            def squares(t, q):
                act.wait_ge(s_yc, t + 1)
                nc.scalar.activation(sq, y[q][:], ACT.Square).then_inc(s_sq, 1)

            def ffn_input_transposed(t):
                act.wait_ge(s_trf, t + 1)
                nc.scalar.copy(vT[:, 0:D], ps[:, B_OUT, :]).then_inc(s_xfT, 1)

            def router(t):
                act.wait_ge(s_lg_mm, t + 1)
                nc.scalar.copy(logits[:, t, :], ps[:, B_VAR, 0:E]).then_inc(s_lg, 1)

            def prologue():
                input_transposed(0)
                projections_in(0, 0, range(4))
                offset_out()
                convolved(0, 0)
                projection_x(0)
                magnitudes(0)
                softplus(0)
                input_transposed(1)
                projections_in(1, 1, range(2))
                decays(0)
                convolved(1, 1)
                projection_x(1)
                magnitudes(1)
                softplus(1)
                projections_in(1, 1, range(2, 4))

            def step(t, q, more, more2):
                left_at_chunk_end(t)
                chunk_updates(t)
                if more2:
                    input_transposed(t + 2)
                    projections_in(t + 2, q, [0, 1])
                states_transposed(t)
                if more:
                    decays(t + 1)
                if more2:
                    convolved(t + 2, q)
                    projection_x(t + 2)
                    magnitudes(t + 2)
                squares(t, q)
                if more2:
                    softplus(t + 2)
                    projections_in(t + 2, q, [2])
                ffn_input_transposed(t)
                if more2:
                    projections_in(t + 2, q, [3])
                router(t)

            steps(nc.scalar, prologue, step)

        OWN_F, OWN_C, OWN_B = 2 * MC + 4, 2 * Q - 1 + MC, 2 * (Q - 2) + 3

        @block.vector
        def _(dve):
            dve.wait_ge(s_chan, 16)

            def offset_out():
                dve.wait_ge(s_aexp, 1)
                nc.vector.tensor_scalar(a_neg[:], a_neg[:], -1.0, None, ALU.mult).then_inc(s_aneg, 1)
                dve.wait_ge(s_bo_mm, 1)
                nc.vector.tensor_copy(b_out[:], ps[:, B_OUT, :]).then_inc(s_bo, 1)
                dve.wait_ge(s_bo, 1)

            done = {"front": 0, "chain": 0, "back": 0}

            def front(t, *instructions):
                for ins in instructions:
                    ins.then_inc(s_front, 1)
                done["front"] += len(instructions)
                dve.wait_ge(s_front, OWN_F * t + done["front"])

            def chain(t, *instructions):
                for ins in instructions:
                    ins.then_inc(s_chain, 1)
                done["chain"] += len(instructions)
                dve.wait_ge(s_chain, OWN_C * t + done["chain"])

            def back(t, *instructions):
                for ins in instructions:
                    ins.then_inc(s_back, 1)
                done["back"] += len(instructions)
                dve.wait_ge(s_back, OWN_B * t + done["back"])

            def chunks(t):
                return t[:].rearrange("p m (k t) -> p (m k) t", t=Q)

            def statistics(n, t):
                stand_alone(dve)
                nc.vector.bn_stats(bst[n][:], xres[:, t, :]).then_inc(s_bst[n], 1)
                dve.wait_ge(s_bst[n], t + 1)
                stand_alone(dve)
                nc.vector.bn_aggr(mv[n][:], bst[n][:]).then_inc(s_var[n], 1)

            def normalise(n, dst, t, s_out):
                dve.wait_ge(s_var[n], t + 1)
                dve.wait_ge(s_rstd[n], t + 1)
                nc.vector.tensor_scalar(dst[:], xres[:, t, :], mv[n][:, 0:1], rstd[n][:], ALU.subtract,
                                        ALU.mult).then_inc(s_out, 1)

            def convolution(t, q):
                done["front"] = 0
                dve.wait_ge(s_xz, 4 * t + 2)
                dve.wait_ge(s_c0, MC * t + MC)

                def out(m):
                    return xc[q][:, m, :].rearrange("p (b t) -> p b t", b=2)

                for j in range(3):
                    ins = [nc.vector.scalar_tensor_tensor(out(m), xe[:, m, :, j:j + L], chan[:, m, j:j + 1], out(m),
                                                          ALU.mult, ALU.add) for m in range(MC)]
                    if j < 2:
                        front(t, *ins)
                for x in ins:
                    x.then_inc(s_conv, 1)

            def states_wanted(t):
                dve.wait_ge(s_cr_mm, t + 1)
                nc.vector.tensor_tensor(cd[:], ps[:, 2, 0:P].rearrange("p (b t) -> p b t", b=2),
                                        c["next_chunk"][:].rearrange("p k t -> p (k t)").unsqueeze(1).to_broadcast(
                                            [P, 2, L]), ALU.mult).then_inc(s_cd, 1)

            def softplus(t):
                dve.wait_ge(s_ln, t + 1)
                front(t, nc.vector.tensor_scalar(dts[:], t0[:], 1.0, 1.0, ALU.add, ALU.subtract))
                front(t, nc.vector.tensor_tensor(dts[:], t1[:], dts[:], ALU.subtract))
                front(t, nc.vector.tensor_tensor(dts[:], dts[:], t0[:], ALU.add))
                front(t, nc.vector.scalar_tensor_tensor(flat(dts), banks(B_DT, B_DT + 2), 0.0, flat(dts), ALU.max,
                                                        ALU.add))
                assert done["front"] == OWN_F, done

            def running_sums(t, q):
                nc.vector.tensor_tensor_scan(flat(t1), in_sequence[:], flat(dts), 0.0, ALU.mult,
                                             ALU.add).then_inc(s_S, 1)
                dve.wait_ge(s_xc, t + 1)
                nc.vector.tensor_tensor(v[0][:], dts[:], xc[q][:], ALU.mult).then_inc(s_v, 1)

            def inside_chunks(t, q, distances):
                def weight(j):
                    return ps[:, B_CB + j // 4, (j % 4) * P:(j % 4 + 1) * P].rearrange(
                        "p (k t) -> p k t", t=Q).unsqueeze(1)[:, :, :, j:Q].to_broadcast([P, MC, NK, Q - j])

                def four(t, j):
                    return t[:].rearrange("p m (k t) -> p m k t", t=Q)[:, :, :, j:Q]

                for j in distances:
                    if j == 0:
                        done["chain"] = 0
                        dve.wait_ge(s_v, 8 * t + 1)
                        dve.wait_ge(s_cb_mm, t + 1)
                        chain(t, nc.vector.tensor_tensor(four(y[q], 0), four(v[0], 0), weight(0), ALU.mult))
                        dve.wait_ge(s_dec, 8 * t + 8)
                        continue
                    new, old = v[j % 2], v[(j - 1) % 2]
                    if j >= 2:
                        dve.wait_ge(s_vend, 8 * t + j - 1)
                    nc.vector.tensor_tensor(chunks(new)[:, :, j:Q], chunks(dec)[:, :, j:Q],
                                            chunks(old)[:, :, j - 1:Q - 1], ALU.mult).then_inc(s_v, 1)
                    dve.wait_ge(s_v, 8 * t + j + 1)
                    chain(t, nc.vector.tensor_tensor(four(tmp, j), four(new, j), weight(j), ALU.mult))
                    chain(t, nc.vector.tensor_tensor(chunks(y[q])[:, :, j:Q], chunks(y[q])[:, :, j:Q],
                                                     chunks(tmp)[:, :, j:Q], ALU.add))

            def skip(t, q):
                chain(t, *[nc.vector.scalar_tensor_tensor(y[q][:, m, :], xc[q][:, m, :], chan[:, m, 6:7], y[q][:, m, :],
                                                          ALU.mult, ALU.add) for m in range(MC)])
                done["chain"] = 0

            def states(t, q):
                dve.wait_ge(s_u, 4 * t + 4)
                dve.wait_ge(s_prod, 8 * t + 8)
                stk = st[:].rearrange("p m (b k n) -> p (m b) k n", b=2, k=Q)
                pck = prod[q][:].rearrange("p m (b k t) -> p (m b) k t", b=2, k=Q)
                for k in range(1, Q - 1):
                    back(t, nc.vector.tensor_tensor(stmp[:], stk[:, :, k - 1, :],
                                                    pck[:, :, k, Q - 1:Q].to_broadcast([P, 2 * MC, NS]), ALU.mult))
                    add = nc.vector.tensor_tensor(stk[:, :, k, :], stk[:, :, k, :], stmp[:], ALU.add)
                    if k < Q - 2:
                        back(t, add)
                add.then_inc(s_st, 1)

            def offset_added(t):
                done["back"] = 0
                back(t, nc.vector.tensor_tensor(xres[:, t, :], xres[:, t, :], b_out[:], ALU.add))

            def gated(t, q):
                dve.wait_ge(s_y2, t + 1)
                back(t, nc.vector.tensor_tensor(flat(v[1]), flat(prod[q]), banks(0, 2), ALU.mult))
                back(t, nc.vector.tensor_tensor(y[q][:], y[q][:], v[1][:], ALU.add))
                nc.vector.tensor_tensor(y[q][:], y[q][:], zs[q][:], ALU.mult).then_inc(s_y, 1)

            def centred(t, q):
                dve.wait_ge(s_mean, t + 1)
                dve.wait_ge(s_y, t + 1)
                nc.vector.tensor_tensor(y[q][:], y[q][:], ps[:, 3, 0:P].unsqueeze(1).to_broadcast([P, MC, P]),
                                        ALU.subtract).then_inc(s_yc, 1)

            def output(t):
                dve.wait_ge(s_vcol, t + 1)
                nc.vector.tensor_copy(mv[1][:, 1:2], ps[:, B_VAR, 0:1]).then_inc(s_var[1], 1)
                dve.wait_ge(s_rstd[1], t + 1)
                dve.wait_ge(s_out, t + 1)
                back(t, nc.vector.scalar_tensor_tensor(xres[:, t, :], ps[:, B_OUT, :], rstd[1][:], xres[:, t, :],
                                                       ALU.mult, ALU.add))
                assert done["back"] == OWN_B, done
                statistics(2, t)
                dve.wait_ge(s_xf_d, 32 * t + 1)
                normalise(2, xf, t, s_xf)

            def prologue():
                statistics(0, 0)
                normalise(0, xm, 0, s_xm)
                convolution(0, 0)
                offset_out()
                statistics(0, 1)
                normalise(0, xm, 1, s_xm)
                softplus(0)
                running_sums(0, 0)
                convolution(1, 1)
                states_wanted(0)
                inside_chunks(0, 0, range(FIRST_PAIRS))

            def step(t, q, more, more2):
                done["chain"] = 2 * FIRST_PAIRS - 1
                inside_chunks(t, q, range(FIRST_PAIRS, Q))
                skip(t, q)
                if more2:
                    statistics(0, t + 2)
                offset_added(t)
                if more2:
                    normalise(0, xm, t + 2, s_xm)
                if more:
                    softplus(t + 1)
                states(t, q)
                if more:
                    running_sums(t + 1, 1 - q)
                if more2:
                    convolution(t + 2, q)
                gated(t, q)
                if more:
                    states_wanted(t + 1)
                    inside_chunks(t + 1, 1 - q, [0])
                centred(t, q)
                if more:
                    inside_chunks(t + 1, 1 - q, range(1, FIRST_PAIRS))
                output(t)

            steps(nc.vector, prologue, step)


def ffn_block(nc, d, c, xres, xf_d, xfT_d, w13_first, s_first, xs_d, ys_d, logits, s_xf_d, s_zero_d):
    with ExitStack() as ctx:
        def sb(name, shape, dt=F32):
            return ctx.enter_context(nc.sbuf_tensor("C_" + name, shape, dt))

        def sem(name):
            return ctx.enter_context(nc.semaphore(name))

        ps = ctx.enter_context(nc.psum_tensor("psC", [P, 8, 512], F32))
        TH = 512
        REST = CAP - P
        w13 = [[w13_first if q == half == 0 else sb(f"w13_{q}{half}", [P, 2, KD, H // 2]) for half in range(2)]
               for q in range(2)]
        w2 = [sb(f"w2_{q}", [P, MH, D]) for q in range(2)]
        xfT = sb("xfT", [P, KD, N])
        xf = sb("xf", [P, NT, D])
        gate_b = sb("gate_b", [P, E])
        hT = sb("hTs", [P, MH, TH])
        sl = [sb(f"sl{a}", [P, TH]) for a in range(2)]
        sc = sb("sc", [P, NT, E])
        red = sb("red", [P, NT])
        best = sb("best", [P, NT, 8])
        best_i = sb("best_i", [P, NT, 8], U32)
        pick = sb("pick", [P, NT, 2])
        onehot = sb("onehot", [P, 2, NT, E])
        prod = sb("prodR", [P, NT, E])
        gate = sb("gate", [P, 2, NT])
        queue = sb("queue", [P, NT, E])
        queueT = sb("queueT", [E, N])
        onehotT = sb("onehotT", [E, 2, N])
        junk = sb("junk", [P, N])
        own_w = sb("own_w", [P, 2, NT])
        part = sb("part", [P, 2, NT, 4])
        rank = sb("rank", [P, 2, NT])
        slot = sb("slot", [P, 2, NT])
        keep = sb("keep", [P, 2, NT])
        slot_i = sb("slot_i", [P, 2, NT], U32)
        xs = [sb(f"xs{q}", [P, D]) for q in range(2)]
        xsr = [sb(f"xsr{q}", [REST, D]) for q in range(2)]
        flat = hT[:].rearrange("p m t -> p (m t)")
        xsT = [flat[:, q * KD * CAP:(q + 1) * KD * CAP].rearrange("p (k s) -> p k s", k=KD) for q in range(2)]
        eT = [flat[:, (2 * KD + q * MH) * CAP:(2 * KD + (q + 1) * MH) * CAP].rearrange("p (m s) -> p m s", m=MH)
              for q in range(2)]
        yT = sb("yT", [P, KD, CAP])
        gathered = xfT[:].rearrange("p k t -> p (k t)").rearrange("p (a k n) -> p a k n", a=4, k=2)
        yo = [gathered[:, 2, q, :] for q in range(2)]
        yor = [gathered[0:REST, 3, q, :] for q in range(2)]

        s_in = sem("C_in")
        s_xfT = [sem(f"C_xfT{hf}") for hf in range(2)]
        s_wA = [sem(f"C_w13_{q}") for q in range(2)]
        s_wB = [sem(f"C_w2_{q}") for q in range(2)]
        s_r = sem("C_router")
        s_ex = sem("C_exp")
        s_qT_mm = sem("C_queueT_mm")
        s_qT = sem("C_queueT")
        s_row_mm = sem("C_row_mm")
        s_row = sem("C_row")
        s_slot = sem("C_slot")
        s_xs_d = sem("C_xs_d")
        s_h_mm = sem("C_h_mm")
        s_sl = sem("C_sl")
        s_h = sem("C_h")
        s_y_mm = sem("C_y_mm")
        s_y = sem("C_y")
        s_xs = [sem(f"C_xs{q}") for q in range(2)]
        s_xT_mm = sem("E_xT_mm")
        s_xT = sem("E_xT")
        s_e_mm = sem("E_h_mm")
        s_esl = sem("E_sl")
        s_e = sem("E_h")
        s_yT_mm = sem("E_yT_mm")
        s_yT = sem("E_yT")
        s_yo_mm = sem("E_yo_mm")
        s_yo = sem("E_yo")
        s_ys = [sem(f"E_ys{q}") for q in range(2)]
        s_g = [sem(f"F_g{a}") for a in range(4)]
        s_f = sem("F_sum")
        s_res = sem("F_out")

        units = [(hf, s) for s in range(2) for hf in range(2)]
        FIRST_ROW = 6

        block = ctx.enter_context(nc.Block())

        def load_halves(eng, q, half, a, b):
            cols = slice(half * H // 2, (half + 1) * H // 2)
            for i, w in enumerate((a, b)):
                eng.dma_start(w13[q][half][:, i], w.rearrange("(k p) n -> p k n", p=P)[:, :, cols]).then_inc(s_wA[q], 16)

        def load_w13(eng, q, a, b):
            load_halves(eng, q, 0, a, b)
            load_halves(eng, q, 1, a, b)

        def load_w2(eng, q, a):
            eng.dma_start(w2[q][:], a.rearrange("(m p) n -> p m n", p=P)).then_inc(s_wB[q], 16)

        def load_xs(eng, q, e):
            rows = xs_d.rearrange("(e s) n -> e s n", e=E)[e]
            eng.dma_start(xs[q][:], rows[0:P, :]).then_inc(s_xs[q], 16)
            eng.dma_start(xsr[q][:], rows[P:CAP, :]).then_inc(s_xs[q], 16)

        @block.sync
        def _(sp):
            sp.wait_ge(s_xf_d, 32 * NT + 1)
            for hf in range(2):
                sp.dma_start(xfT[:, :, hf * TH:(hf + 1) * TH],
                             xfT_d.rearrange("(k p) t -> p k t", p=P)[:, :, hf * TH:(hf + 1) * TH]).then_inc(s_xfT[hf], 16)
                if hf == 0:
                    load_halves(sp, 0, 1, d["sw1"][0], d["sw3"][0])
            load_w2(sp, 0, d["sw2"][0])
            sp.dma_start(gate_b[:], d["gate_b"].partition_broadcast(P)).then_inc(s_in, 16)
            sp.dma_start(xf[:], xf_d.rearrange("(t p) n -> p t n", p=P)).then_inc(s_in, 16)
            load_w13(sp, 1, d["sw1"][1], d["sw3"][1])
            load_w2(sp, 1, d["sw2"][1])
            for q in range(2):
                sp.wait_ge(s_h_mm, 16 * q + 16)
                load_w13(sp, q, d["ew1"][q], d["ew3"][q])
                if q == 1:
                    sp.wait_ge(s_xs_d, 16 * 2 * NT)
                    for n in range(2):
                        load_xs(sp, n, n)
                sp.wait_ge(s_y_mm, 8 * q + 8)
                load_w2(sp, q, d["ew2"][q])
            with nc.sync.Fori(0, E // 2 - 1) as ep:
                for q in range(2):
                    sp.wait_ge(s_e_mm, MH * (2 * ep + q + 1))
                    load_w13(sp, q, d["ew1"][2 * ep + q + 2], d["ew3"][2 * ep + q + 2])
                    load_xs(sp, q, 2 * ep + q + 2)
                    sp.wait_ge(s_yT_mm, 2 * (2 * ep + q + 1))
                    load_w2(sp, q, d["ew2"][2 * ep + q + 2])
            for t in range(NT):
                sp.wait_ge(s_f, 2 * t + 2)
                sp.dma_start(d["out"][t * P:(t + 1) * P, :], xres[:, t, :]).then_inc(s_res, 16)
            sp.wait_ge(s_res, 16 * NT)

        @block.gpsimd
        def _(pool):
            pool.wait_ge(s_slot, 1)
            pool.wait_ge(s_in, 32)
            pool.wait_ge(s_zero_d, 32)
            for t in range(NT):
                for k in range(2):
                    nc.gpsimd.indirect_dma_start(
                        xs_d, bass.IndirectOffsetOnAxis(ap=slot_i[:, k, t:t + 1], axis=0), xf[:, t, :], None,
                        bounds_check=E * CAP - 1, oob_is_err=False).then_inc(s_xs_d, 16)
            for q in range(2):
                pool.wait_ge(s_ys[q], 32 * E // 2 + 1)
            for t in range(NT):
                if t >= 4:
                    pool.wait_ge(s_f, 2 * t - 6)
                for k in range(2):
                    nc.gpsimd.indirect_dma_start(
                        gathered[:, t % 4, k, :], None, ys_d, bass.IndirectOffsetOnAxis(ap=slot_i[:, k, t:t + 1], axis=0),
                        bounds_check=E * CAP, oob_is_err=False).then_inc(s_g[t % 4], 16)

        @block.tensor
        def _(pe):
            pe.wait_ge(s_first, 32)

            def w_of(q, a, k, m):
                o = (m % (MH // 2)) * P
                return w13[q][m // (MH // 2)][:, a, k, o:o + P]

            def queues(n):
                if n == 0:
                    pe.wait_ge(s_r, R_QUEUE)
                else:
                    pe.wait_ge(s_qT, 2 * n)
                for t in range(NT):
                    src = queue[:, t, :] if n == 0 else onehot[:, n - 1, t, :]
                    mm = nc.tensor.transpose(ps[0:E, t // 4, (t % 4) * P:(t % 4 + 1) * P], src, c["ident"][:])
                mm.then_inc(s_qT_mm, 1)

            def row(r):
                t, k = r // 2, r % 2
                if r == 0:
                    pe.wait_ge(s_qT, 6)
                else:
                    pe.wait_ge(s_row, r)
                for b in range(2):
                    mm = nc.tensor.matmul(ps[:, b, :], onehotT[:, k, t * P:(t + 1) * P], queueT[:, b * 512:(b + 1) * 512],
                                          start=True, stop=True)
                mm.then_inc(s_row_mm, 1)

            step = 0
            for hf, s in units:
                if hf == 0 and s > 0:
                    pe.wait_ge(s_wA[s], 64)
                if s == 0:
                    pe.wait_ge(s_xfT[hf], 16)
                for m in range(MH):
                    if (hf, s, m) == (0, 0, MH // 2):
                        pe.wait_ge(s_wA[0], 32)
                    if FIRST_ROW - 4 <= step < FIRST_ROW - 1:
                        queues(step - FIRST_ROW + 4)
                    if FIRST_ROW <= step < FIRST_ROW + 2 * NT:
                        row(step - FIRST_ROW)
                    if step >= 2:
                        pe.wait_ge(s_h, step - 1)
                    for a in range(2):
                        for k in range(KD):
                            mm = nc.tensor.matmul(ps[:, 2 + 2 * (step % 2) + a, :], w_of(s, a, k, m),
                                                  xfT[:, k, hf * TH:(hf + 1) * TH], start=(k == 0), stop=(k == KD - 1))
                    mm.then_inc(s_h_mm, 1)
                    step += 1
                if hf == 0:
                    pe.wait_ge(s_wB[s], 16)
                pe.wait_ge(s_h, step)
                for t in range(4):
                    n = 4 * (2 * s + hf) + t
                    if n >= 2:
                        pe.wait_ge(s_y, n - 1)
                    for m in range(MH):
                        mm = nc.tensor.matmul(ps[:, 6 + n % 2, :], hT[:, m, t * P:(t + 1) * P], w2[s][:, m, :],
                                              start=(m == 0), stop=(m == MH - 1))
                    mm.then_inc(s_y_mm, 1)

            def rows_in(q, e):
                pe.wait_ge(s_xs[q], 16 * (e - q) + 32)
                for k in range(KD):
                    o = (k % 2) * CAP
                    nc.tensor.transpose(ps[:, k // 2, o:o + P], xs[q][:, k * P:(k + 1) * P], c["ident"][:])
                    mm = nc.tensor.transpose(ps[:, k // 2, o + P:o + CAP], xsr[q][:, k * P:(k + 1) * P],
                                             c["ident"][0:REST, 0:REST])
                mm.then_inc(s_xT_mm, 1)

            def expert(q, e, last):
                pe.wait_ge(s_wA[q], 32 * (e - q) + (96 if q == 0 else 128))
                pe.wait_ge(s_xT, 2 * e + 2)
                for m in range(MH):
                    if m >= 3:
                        pe.wait_ge(s_e, MH * e + m - 2)
                    if m == 2:
                        pe.wait_ge(s_yo, 2 * e + 1)
                    for a in range(2):
                        for k in range(KD):
                            mm = nc.tensor.matmul(ps[:, 2 + m % 3, a * CAP:(a + 1) * CAP], w_of(q, a, k, m),
                                                  xsT[q][:, k, :], start=(k == 0), stop=(k == KD - 1))
                    mm.then_inc(s_e_mm, 1)
                if not last:
                    rows_in(1 - q, e + 1)
                pe.wait_ge(s_wB[q], 8 * (e - q) + 32)
                pe.wait_ge(s_e, MH * e + MH)
                for dm in range(KD):
                    for m in range(MH):
                        mm = nc.tensor.matmul(ps[:, 5 + dm // 2, (dm % 2) * CAP:(dm % 2 + 1) * CAP],
                                              w2[q][:, m, dm * P:(dm + 1) * P], eT[q][:, m, :],
                                              start=(m == 0), stop=(m == MH - 1))
                    if dm % 2:
                        mm.then_inc(s_yT_mm, 1)
                for half in range(2):
                    pe.wait_ge(s_yT, 2 * e + half + 1)
                    for dm in range(2 * half, 2 * half + 2):
                        mm = nc.tensor.transpose(ps[:, 7, dm * P:(dm + 1) * P], yT[:, dm, 0:P], c["ident"][:])
                mm.then_inc(s_yo_mm, 1)
                for dm in range(KD):
                    mm = nc.tensor.transpose(ps[0:REST, 4, dm * P:(dm + 1) * P], yT[:, dm, P:CAP], c["ident"][:])
                mm.then_inc(s_yo_mm, 1)

            pe.wait_ge(s_row, 2 * NT)
            rows_in(0, 0)
            with nc.tensor.Fori(0, E // 2 - 1) as ep:
                expert(0, 2 * ep, False)
                expert(1, 2 * ep + 1, False)
            expert(0, E - 2, False)
            expert(1, E - 1, True)

        @block.scalar
        def _(act):
            act.wait_ge(s_r, R_SHIFT)
            nc.scalar.activation(sc[:], sc[:], ACT.Exp).then_inc(s_ex, 1)
            step = 0
            for hf, s in units:
                for m in range(MH):
                    if FIRST_ROW - 4 <= step < FIRST_ROW - 1:
                        n = step - FIRST_ROW + 4
                        act.wait_ge(s_qT_mm, n + 1)
                        for b in range(2):
                            dst = queueT[:, b * 512:(b + 1) * 512] if n == 0 else onehotT[:, n - 1, b * 512:(b + 1) * 512]
                            nc.scalar.copy(dst, ps[0:E, b, :]).then_inc(s_qT, 1)
                    act.wait_ge(s_h_mm, step + 1)
                    if step >= 2:
                        act.wait_ge(s_h, step - 1)
                    nc.scalar.activation(sl[step % 2][:], ps[:, 2 + 2 * (step % 2), :], ACT.Silu).then_inc(s_sl, 1)
                    step += 1

            def rows_in(q, e):
                act.wait_ge(s_xT_mm, e + 1)
                for b in range(2):
                    nc.scalar.copy(xsT[q][:, 2 * b:2 * b + 2, :].rearrange("p k s -> p (k s)"),
                                   ps[:, b, 0:2 * CAP]).then_inc(s_xT, 1)

            def expert(q, e, last):
                for m in range(MH):
                    act.wait_ge(s_e_mm, MH * e + m + 1)
                    if m >= 2:
                        act.wait_ge(s_e, MH * e + m - 1)
                    nc.scalar.activation(sl[m % 2][:, 0:CAP], ps[:, 2 + m % 3, 0:CAP], ACT.Silu).then_inc(s_esl, 1)
                if not last:
                    rows_in(1 - q, e + 1)
                act.wait_ge(s_ys[q], 16 * (e - q) + 1)
                act.wait_ge(s_yo_mm, 2 * e + 1)
                nc.scalar.copy(yo[q], ps[:, 7, :]).then_inc(s_yo, 1)
                act.wait_ge(s_yo_mm, 2 * e + 2)
                nc.scalar.copy(yor[q], ps[0:REST, 4, :]).then_inc(s_yo, 1)
                rows = ys_d[0:E * CAP, :].rearrange("(e s) n -> e s n", e=E)[e]
                act.wait_ge(s_yo, 2 * e + 3)
                act.dma_start(rows[0:P, :], yo[q]).then_inc(s_ys[q], 16)
                act.dma_start(rows[P:CAP, :], yor[q]).then_inc(s_ys[q], 16)

            act.sem_inc(s_yo, 1)
            for q in range(2):
                act.sem_inc(s_ys[q], 1)
            rows_in(0, 0)
            with nc.scalar.Fori(0, E // 2 - 1) as ep:
                expert(0, 2 * ep, False)
                expert(1, 2 * ep + 1, False)
            expert(0, E - 2, False)
            expert(1, E - 1, True)

        @block.vector
        def _(dve):
            done = [0]

            def own(*instructions):
                for ins in instructions:
                    ins.then_inc(s_r, 1)
                done[0] += len(instructions)
                dve.wait_ge(s_r, done[0])

            wide = [P, NT, E]
            own(nc.vector.tensor_reduce(red[:], logits[:], AX.X, ALU.max))
            own(nc.vector.tensor_tensor(sc[:], logits[:], red[:].unsqueeze(2).to_broadcast(wide), ALU.subtract))
            assert done[0] == R_SHIFT
            dve.wait_ge(s_ex, 1)
            own(nc.vector.tensor_reduce(red[:], sc[:], AX.X, ALU.add))
            own(nc.vector.reciprocal(red[:], red[:]))
            own(nc.vector.tensor_tensor(sc[:], sc[:], red[:].unsqueeze(2).to_broadcast(wide), ALU.mult))
            dve.wait_ge(s_in, 32)
            own(nc.vector.tensor_tensor(sc[:], sc[:], gate_b[:].unsqueeze(1).to_broadcast(wide), ALU.add))
            own(*[nc.vector.max(best[:, t, :], sc[:, t, :]) for t in range(NT)])
            own(*[nc.vector.max_index(best_i[:, t, :], best[:, t, :], sc[:, t, :]) for t in range(NT)])
            own(nc.vector.tensor_copy(pick[:], best_i[:, :, 0:2]))
            for k in range(2):
                own(nc.vector.tensor_tensor(onehot[:, k], pick[:, :, k:k + 1].to_broadcast(wide),
                                            c["expert_index"][:].unsqueeze(1).to_broadcast(wide), ALU.is_equal))
                own(nc.vector.tensor_tensor(prod[:], onehot[:, k], logits[:], ALU.mult))
                own(nc.vector.tensor_reduce(gate[:, k, :], prod[:], AX.X, ALU.add))
            own(nc.vector.tensor_tensor(queue[:], onehot[:, 0], onehot[:, 1], ALU.add))
            own(nc.vector.tensor_tensor(prod[:], queue[:], logits[:], ALU.mult))
            own(nc.vector.tensor_scalar(queue[:], queue[:], -NOT_MINE, NOT_MINE, ALU.mult, ALU.add))
            own(nc.vector.tensor_tensor(queue[:], queue[:], prod[:], ALU.add))
            assert done[0] == R_QUEUE, done[0]
            own(nc.vector.memset(part[:], 0.0))

            def rank_row(r):
                t, k = r // 2, r % 2
                w = own_w[:, k, t:t + 1]
                a, b = t * P, (t + 1) * P
                row = ps[:, 0:2, :].rearrange("p b n -> p (b n)")
                dve.wait_ge(s_row_mm, r + 1)
                own(nc.vector.scalar_tensor_tensor(junk[:, a:b], row[:, a:b], 1.0, c["ident"][:], ALU.mult, ALU.mult,
                                                   accum_out=w))
                ins = []
                if t > 0:
                    ins.append(nc.vector.tensor_scalar(junk[:, 0:a], row[:, 0:a], w, None, ALU.is_ge, ALU.add,
                                                       accum_out=part[:, k, t, 0:1]))
                if t < NT - 1:
                    ins.append(nc.vector.tensor_scalar(junk[:, b:N], row[:, b:N], w, None, ALU.is_gt, ALU.add,
                                                       accum_out=part[:, k, t, 1:2]))
                ins.append(nc.vector.scalar_tensor_tensor(junk[:, a:b], row[:, a:b], w, c["lower"][:], ALU.is_ge,
                                                          ALU.mult, accum_out=part[:, k, t, 2:3]))
                own(*ins)
                own(nc.vector.scalar_tensor_tensor(junk[:, a:b], row[:, a:b], w, c["upper"][:], ALU.is_gt,
                                                   ALU.mult, accum_out=part[:, k, t, 3:4]))
                nc.vector.tensor_copy(own_w[:, k, t:t + 1], own_w[:, k, t:t + 1]).then_inc(s_row, 1)

            def slots():
                dve.wait_ge(s_row, 2 * NT)
                own(nc.vector.tensor_reduce(rank[:], part[:], AX.X, ALU.add))
                own(nc.vector.tensor_scalar(keep[:], rank[:], float(CAP), None, ALU.is_lt))
                own(nc.vector.scalar_tensor_tensor(slot[:], pick[:].rearrange("p t k -> p k t"), float(CAP), rank[:],
                                                   ALU.mult, ALU.add))
                own(nc.vector.scalar_tensor_tensor(slot[:], slot[:], float(-E * CAP), keep[:], ALU.add, ALU.mult))
                own(nc.vector.tensor_scalar(slot[:], slot[:], float(E * CAP), None, ALU.add))
                nc.vector.tensor_copy(slot_i[:], slot[:]).then_inc(s_slot, 1)

            step = 0
            for hf, s in units:
                for m in range(MH):
                    if FIRST_ROW <= step < FIRST_ROW + 2 * NT:
                        rank_row(step - FIRST_ROW)
                    if step == FIRST_ROW + 2 * NT:
                        slots()
                    dve.wait_ge(s_sl, step + 1)
                    nc.vector.tensor_tensor(hT[:, m, :], sl[step % 2][:], ps[:, 3 + 2 * (step % 2), :],
                                            ALU.mult).then_inc(s_h, 1)
                    step += 1
                for t in range(4):
                    n = 4 * (2 * s + hf) + t
                    dve.wait_ge(s_y_mm, n + 1)
                    if n >= 8:
                        dve.wait_ge(s_y, n - 7)
                    nc.vector.scalar_tensor_tensor(xres[:, 4 * hf + t, :], ps[:, 6 + n % 2, :], 0.5,
                                                   xres[:, 4 * hf + t, :], ALU.mult, ALU.add).then_inc(s_y, 1)

            def expert(q, e):
                for m in range(MH):
                    dve.wait_ge(s_esl, MH * e + m + 1)
                    nc.vector.tensor_tensor(eT[q][:, m, :], sl[m % 2][:, 0:CAP], ps[:, 2 + m % 3, CAP:2 * CAP],
                                            ALU.mult).then_inc(s_e, 1)
                for half in range(2):
                    dve.wait_ge(s_yT_mm, 2 * e + half + 1)
                    nc.vector.tensor_copy(yT[:, 2 * half:2 * half + 2, :].rearrange("p k s -> p (k s)"),
                                          ps[:, 5 + half, 0:2 * CAP]).then_inc(s_yT, 1)

            with nc.vector.Fori(0, E // 2) as ep:
                for q in range(2):
                    expert(q, 2 * ep + q)
            dve.wait_ge(s_y, 16)
            for t in range(NT):
                dve.wait_ge(s_g[t % 4], 32 * (t // 4 + 1))
                for k in range(2):
                    if k:
                        dve.wait_ge(s_f, 2 * t + 1)
                    nc.vector.scalar_tensor_tensor(xres[:, t, :], gathered[:, t % 4, k, :], gate[:, k, t:t + 1], xres[:, t, :],
                                                   ALU.mult, ALU.add).then_inc(s_f, 1)


R_SHIFT = 2
R_QUEUE = 33


def perceiver_kernel(nc, d):
    with ExitStack() as ctx:
        def sb(name, shape, dt=F32):
            return ctx.enter_context(nc.sbuf_tensor(name, shape, dt))

        def sem(name):
            return ctx.enter_context(nc.semaphore(name))

        xf_d = nc.dram_tensor("xf_scratch", (N, D), F32, kind="Internal").ap()
        xfT_d = nc.dram_tensor("xfT_scratch", (D, N), F32, kind="Internal").ap()
        xs_d = nc.dram_tensor("queue_rows", (E * CAP, D), F32, kind="Internal").ap()
        ys_d = nc.dram_tensor("expert_rows", (E * CAP + 1, D), F32, kind="Internal").ap()
        xres = sb("xres", [P, NT, D])
        logits = sb("logits", [P, NT, E])
        zeros = sb("zeros", [P, D])
        c = constants(nc, sb, sem, d)
        s_const = sem("constants")
        s_x = sem("x_in")
        s_z = sem("zeros")
        s_xf_d = sem("xf_to_dram")
        s_zero_d = sem("zero_rows")
        s_w_in = sem("w_in")
        s_first = sem("w13_first")

        def constants_and_zeros(pool):
            n = build_constants(nc, c, s_const)
            pool.memset(zeros[:], 0.0).then_inc(s_z, 1)
            return n

        def zero_rows(sp):
            sp.wait_ge(s_z, 1)
            sp.dma_start(xs_d.rearrange("(a p) n -> p a n", p=P),
                         zeros[:].unsqueeze(1).to_broadcast([P, E * CAP // P, D])).then_inc(s_zero_d, 16)
            sp.dma_start(ys_d[E * CAP:E * CAP + 1, :], zeros[0:1, :]).then_inc(s_zero_d, 16)

        def load_w_in(sp):
            for k in range(KA):
                sp.dma_start(w_in_a[:, k, :], d["w_in"][k * P:(k + 1) * P, :]).then_inc(s_w_in, 16)

        def load_first(sp):
            for a, name in enumerate(("sw1", "sw3")):
                sp.dma_start(w13_first[:, a],
                             d[name][0].rearrange("(k p) n -> p k n", p=P)[:, :, 0:H // 2]).then_inc(s_first, 16)

        with nc.sbuf_tensor("w_in_a", [P, KA, 2 * C], F32, side="right") as w_in_a:
            attention_block(nc, d, c, s_const, constants_and_zeros, xres, s_x, load_w_in)
            w13_first = sb("w13_first", [P, 2, KD, H // 2])
            mamba_block(nc, d, c, xres, w_in_a, s_w_in, xf_d, xfT_d, logits, s_xf_d, zero_rows,
                        load_first)
        ffn_block(nc, d, c, xres, xf_d, xfT_d, w13_first, s_first, xs_d, ys_d, logits, s_xf_d, s_zero_d)


def kernel(**inputs):
    import numpy as np
    import concourse.bacc as bacc
    from concourse.bass_utils import run_bass_kernel_spmd

    a = {k: np.asarray(v) for k, v in inputs.items()}

    def by_channel(v):
        return v.reshape(MC, P).T

    pair = a["ctx_1024"].reshape(NB // 2, 2, KS, P, KD, P)
    w_x = np.zeros((C, 96), np.float32)
    for n in range(3):
        w_x[:, 32 * n:32 * n + NS] = a["L0_attn_W_xproj"][:, NS * n:NS * (n + 1)]
    chan = np.stack([by_channel(a["L0_attn_conv_w"][:, j]) for j in range(4)] + [
        by_channel(a["L0_attn_conv_b"]), by_channel(np.repeat(a["L0_attn_A_log"], C // 16)),
        by_channel(np.repeat(a["L0_attn_D_skip"], C // 16)), by_channel(a["L0_attn_ln_g"]),
        by_channel(a["L0_attn_ln_b"])], axis=2)
    host = {
        "x": a["x"].reshape(N, D),
        "ctx": pair.transpose(0, 1, 3, 2, 4, 5).reshape(NB // 2, 2, P, KS, D),
        "ctxT": pair.transpose(0, 1, 5, 4, 2, 3).reshape(NB // 2, 2, P, KD, SK),
        "wq1T": a["L0_xattn_Wq1"].T, "wk1T": a["L0_xattn_Wk1"].T, "wv1": a["L0_xattn_Wv1"],
        "wq2T": a["L0_xattn_Wq2"].T, "wk2T": a["L0_xattn_Wk2"].T, "wv2": a["L0_xattn_Wv2"],
        "fc1_w": a["L0_xattn_fc1_w"], "fc1_b": a["L0_xattn_fc1_b"].reshape(KD, P).T,
        "fc2_w": a["L0_xattn_fc2_w"], "fc2_b": a["L0_xattn_fc2_b"].reshape(1, D),
        "ln": np.stack([a[f"L0_xattn_ln{n}_{k}"] for n in (1, 2, 3) for k in "gb"]),
        "w_in": a["L0_attn_W_in"], "w_x": w_x,
        "w_dt": np.concatenate([a["L0_attn_W_dt"], a["L0_attn_b_dt"].reshape(1, C)], axis=0),
        "chan": chan, "w_out": a["L0_attn_W_out"],
        "gate_w": a["L0_ffn_gate_w"], "gate_b": a["L0_ffn_gate_b"],
        "ew1": a["L0_ffn_ew1"], "ew3": a["L0_ffn_ew3"], "ew2": a["L0_ffn_ew2"],
        "sw1": a["L0_ffn_sw1"], "sw3": a["L0_ffn_sw3"], "sw2": a["L0_ffn_sw2"],
    }
    nc = bacc.Bacc("TRN2", target_bir_lowering=False, num_devices=1)
    arrays, d = {}, {}
    for name, v in host.items():
        arrays["in_" + name] = np.ascontiguousarray(v)
        d[name] = nc.dram_tensor("in_" + name, v.shape, mybir.dt.from_np(v.dtype), kind="ExternalInput").ap()
    out = nc.dram_tensor("out_0", (N, D), F32, kind="ExternalOutput").ap()
    d["out"] = out
    perceiver_kernel(nc, d)
    r = run_bass_kernel_spmd(nc, [arrays], core_ids=[0])
    return r.results[0]["out_0"].reshape(NB, L, D)
```
